# Optimizing a Trainium2 kernel written in Bass

```python
import numpy as np
import jax
import jax.numpy as jnp

def _softmax(x, axis=-1):
    return jax.nn.softmax(x, axis=axis)

def _gelu(x):
    return jax.nn.gelu(x, approximate=True)

def _silu(x):
    return jax.nn.silu(x)

def _sigmoid(x):
    return jax.nn.sigmoid(x)

def _layernorm(x, axis=-1, eps=1e-05):
    m = jnp.mean(x, axis=axis, keepdims=True)
    v = jnp.var(x, axis=axis, keepdims=True)
    return (x - m) / jnp.sqrt(v + eps)

def _scatter_add(tgt, idx, src, axis=0):
    return tgt.at[idx].add(src)

def _segment_sum(src, seg, n):
    return jax.ops.segment_sum(src, seg, n)
kernel_name = 'mk_sandwich_d2_jaxref_r4_2e6fb7'

def setup_inputs(seed: int=0):
    np.random.seed(seed)
    _w = jnp.asarray

    def _L0_attn_setup():
        import jax, jax.numpy as jnp
        import numpy as np
        import math
        N_HEAD = 16
        ROPE_BASE = 10000.0

        def _rope_as_in_source(x):
            B, H, T, hd = x.shape
            theta = 1.0 / ROPE_BASE ** (jnp.arange(0, hd, 2, dtype=jnp.float32) / hd)
            ang = jnp.arange(H, dtype=jnp.float32)[:, None] * theta[None, :]
            cos = jnp.cos(ang)[None, :, None, :]
            sin = jnp.sin(ang)[None, :, None, :]
            xr = x.reshape(B, H, T, hd // 2, 2)
            out = jnp.stack([xr[..., 0] * cos - xr[..., 1] * sin, xr[..., 1] * cos + xr[..., 0] * sin], axis=-1)
            return out.reshape(B, H, T, hd)
        key = jax.random.key(seed)
        ks = jax.random.split(key, 5)
        B, T, C = (2, 512, 256)
        s = 0.02
        return {'x': jax.random.normal(ks[0], (B, T, C), dtype=jnp.float32), 'W_attn': jax.random.normal(ks[1], (C, 3 * C), dtype=jnp.float32) * s, 'b_attn': jnp.zeros((3 * C,), dtype=jnp.float32), 'W_proj': jax.random.normal(ks[2], (C, C), dtype=jnp.float32) * s, 'b_proj': jnp.zeros((C,), dtype=jnp.float32)}
    _L0_attn_in = _L0_attn_setup()

    def _L0_ffn_setup():
        import math
        import jax, jax.numpy as jnp
        import numpy as np
        B, T, D = (4, 1024, 256)
        H = 16
        HD = D // H
        CAP = int(1024 * 0.125)
        DFF = int(D * 4 * 2 / 3)
        EPS = 1e-06

        def rmsnorm(x, g):
            return x * jax.lax.rsqrt(jnp.mean(x * x, axis=-1, keepdims=True) + EPS) * g
        key = jax.random.key(seed)
        ks = jax.random.split(key, 9)
        s = lambda k, shape: jax.random.normal(k, shape, jnp.float32) * 0.02
        return {'x': jax.random.normal(ks[0], (B, T, D), jnp.float32), 'w_router': s(ks[1], (D,)), 'W_qkv': s(ks[2], (3 * D, D)), 'W_out': s(ks[3], (D, D)), 'g1': jnp.ones((D,), jnp.float32), 'g2': jnp.ones((D,), jnp.float32), 'W1': s(ks[4], (DFF, D)), 'W2': s(ks[5], (DFF, D)), 'W3': s(ks[6], (D, DFF))}
    _L0_ffn_in = _L0_ffn_setup()

    def _L1_attn_setup():
        import math
        import jax, jax.numpy as jnp
        import numpy as np
        B, L, D_MODEL, NHEAD, FACTOR = (8, 1024, 256, 16, 5)
        D_HEAD = D_MODEL // NHEAD
        SAMPLE_K = min(L, max(1, FACTOR * int(math.ceil(math.log(max(L, 2))))))
        TOP_U = min(L, max(1, FACTOR * int(math.ceil(math.log(max(L, 2))))))

        def _split_heads(t):
            b, l, _ = t.shape
            return t.reshape(b, l, NHEAD, D_HEAD).transpose(0, 2, 1, 3)
        key = jax.random.key(seed)
        ks = jax.random.split(key, 10)
        x = jax.random.normal(ks[0], (B, L, D_MODEL), dtype=jnp.float32)
        sample_idx = jax.random.randint(ks[1], (SAMPLE_K,), 0, L)
        s = 0.02
        Wq = jax.random.normal(ks[2], (D_MODEL, D_MODEL), dtype=jnp.float32) * s
        Wk = jax.random.normal(ks[3], (D_MODEL, D_MODEL), dtype=jnp.float32) * s
        Wv = jax.random.normal(ks[4], (D_MODEL, D_MODEL), dtype=jnp.float32) * s
        Wo = jax.random.normal(ks[5], (D_MODEL, D_MODEL), dtype=jnp.float32) * s
        bq = jnp.zeros((D_MODEL,), dtype=jnp.float32)
        bk = jnp.zeros((D_MODEL,), dtype=jnp.float32)
        bv = jnp.zeros((D_MODEL,), dtype=jnp.float32)
        bo = jnp.zeros((D_MODEL,), dtype=jnp.float32)
        return {'x': x, 'Wq': Wq, 'bq': bq, 'Wk': Wk, 'bk': bk, 'Wv': Wv, 'bv': bv, 'Wo': Wo, 'bo': bo, 'sample_idx': sample_idx}
    _L1_attn_in = _L1_attn_setup()

    def _L1_ffn_setup():
        import jax, jax.numpy as jnp
        import numpy as np
        B, S, H, F, G = (8, 512, 256, 1024, 128)
        EPS = 1e-05

        def _dequant(q, scales, g):
            K, N = q.shape
            w = (q.astype(jnp.float32) - 128.0).reshape(K // g, g, N) * scales[:, None, :]
            return w.reshape(K, N)
        key = jax.random.key(seed)
        ks = jax.random.split(key, 8)
        x = jax.random.normal(ks[0], (B, S, H), dtype=jnp.float32)
        ln_gamma = jnp.ones((H,), jnp.float32)
        ln_beta = jnp.zeros((H,), jnp.float32)
        fc1_q = jax.random.randint(ks[1], (H, F), 0, 64, dtype=jnp.int32)
        fc2_q = jax.random.randint(ks[2], (F, H), 0, 64, dtype=jnp.int32)
        fc1_scales = jax.random.uniform(ks[3], (H // G, F), jnp.float32) * 0.02 + 0.001
        fc2_scales = jax.random.uniform(ks[4], (F // G, H), jnp.float32) * 0.02 + 0.001
        fc1_bias = jax.random.normal(ks[5], (F,), jnp.float32) * 0.02
        fc2_bias = jax.random.normal(ks[6], (H,), jnp.float32) * 0.02
        return {'x': x, 'ln_gamma': ln_gamma, 'ln_beta': ln_beta, 'fc1_q': fc1_q, 'fc1_scales': fc1_scales, 'fc1_bias': fc1_bias, 'fc2_q': fc2_q, 'fc2_scales': fc2_scales, 'fc2_bias': fc2_bias}
    _L1_ffn_in = _L1_ffn_setup()
    _d = {'L0_attn_x': _L0_attn_in['x'], 'L0_attn_W_attn': _L0_attn_in['W_attn'], 'L0_attn_b_attn': _L0_attn_in['b_attn'], 'L0_attn_W_proj': _L0_attn_in['W_proj'], 'L0_attn_b_proj': _L0_attn_in['b_proj'], 'L0_ffn_w_router': _L0_ffn_in['w_router'], 'L0_ffn_W_qkv': _L0_ffn_in['W_qkv'], 'L0_ffn_W_out': _L0_ffn_in['W_out'], 'L0_ffn_g1': _L0_ffn_in['g1'], 'L0_ffn_g2': _L0_ffn_in['g2'], 'L0_ffn_W1': _L0_ffn_in['W1'], 'L0_ffn_W2': _L0_ffn_in['W2'], 'L0_ffn_W3': _L0_ffn_in['W3'], 'L1_attn_Wq': _L1_attn_in['Wq'], 'L1_attn_bq': _L1_attn_in['bq'], 'L1_attn_Wk': _L1_attn_in['Wk'], 'L1_attn_bk': _L1_attn_in['bk'], 'L1_attn_Wv': _L1_attn_in['Wv'], 'L1_attn_bv': _L1_attn_in['bv'], 'L1_attn_Wo': _L1_attn_in['Wo'], 'L1_attn_bo': _L1_attn_in['bo'], 'L1_attn_sample_idx': _L1_attn_in['sample_idx'], 'L1_ffn_ln_gamma': _L1_ffn_in['ln_gamma'], 'L1_ffn_ln_beta': _L1_ffn_in['ln_beta'], 'L1_ffn_fc1_q': _L1_ffn_in['fc1_q'], 'L1_ffn_fc1_scales': _L1_ffn_in['fc1_scales'], 'L1_ffn_fc1_bias': _L1_ffn_in['fc1_bias'], 'L1_ffn_fc2_q': _L1_ffn_in['fc2_q'], 'L1_ffn_fc2_scales': _L1_ffn_in['fc2_scales'], 'L1_ffn_fc2_bias': _L1_ffn_in['fc2_bias']}
    _x0 = _d['L0_attn_x']
    _d['L0_attn_x'] = jax.random.normal(jax.random.fold_in(jax.random.key(seed), 1), (8, 1024, 256), dtype=_x0.dtype)
    del _x0
    return _d

def reference(L0_attn_x, L0_attn_W_attn, L0_attn_b_attn, L0_attn_W_proj, L0_attn_b_proj, L0_ffn_w_router, L0_ffn_W_qkv, L0_ffn_W_out, L0_ffn_g1, L0_ffn_g2, L0_ffn_W1, L0_ffn_W2, L0_ffn_W3, L1_attn_Wq, L1_attn_bq, L1_attn_Wk, L1_attn_bk, L1_attn_Wv, L1_attn_bv, L1_attn_Wo, L1_attn_bo, L1_attn_sample_idx, L1_ffn_ln_gamma, L1_ffn_ln_beta, L1_ffn_fc1_q, L1_ffn_fc1_scales, L1_ffn_fc1_bias, L1_ffn_fc2_q, L1_ffn_fc2_scales, L1_ffn_fc2_bias):

    def _L0_attn_ref(x, W_attn, b_attn, W_proj, b_proj):
        import jax, jax.numpy as jnp
        import numpy as np
        import math
        N_HEAD = 16
        ROPE_BASE = 10000.0

        def _rope_as_in_source(x):
            B, H, T, hd = x.shape
            theta = 1.0 / ROPE_BASE ** (jnp.arange(0, hd, 2, dtype=jnp.float32) / hd)
            ang = jnp.arange(H, dtype=jnp.float32)[:, None] * theta[None, :]
            cos = jnp.cos(ang)[None, :, None, :]
            sin = jnp.sin(ang)[None, :, None, :]
            xr = x.reshape(B, H, T, hd // 2, 2)
            out = jnp.stack([xr[..., 0] * cos - xr[..., 1] * sin, xr[..., 1] * cos + xr[..., 0] * sin], axis=-1)
            return out.reshape(B, H, T, hd)
        B, T, C = x.shape
        H = N_HEAD
        hd = C // H
        qkv = x @ W_attn + b_attn
        q, k, v = jnp.split(qkv, 3, axis=2)
        q = q.reshape(B, T, H, hd).transpose(0, 2, 1, 3)
        k = k.reshape(B, T, H, hd).transpose(0, 2, 1, 3)
        v = v.reshape(B, T, H, hd).transpose(0, 2, 1, 3)
        q = _rope_as_in_source(q)
        k = _rope_as_in_source(k)
        att = jnp.einsum('bhqd,bhkd->bhqk', q, k) * (1.0 / math.sqrt(hd))
        causal = jnp.tril(jnp.ones((T, T), dtype=bool))
        att = jnp.where(causal[None, None, :, :], att, -jnp.inf)
        att = jax.nn.softmax(att, axis=-1)
        y = jnp.einsum('bhqk,bhkd->bhqd', att, v)
        y = y.transpose(0, 2, 1, 3).reshape(B, T, C)
        return y @ W_proj + b_proj

    def _L0_ffn_ref(x, w_router, W_qkv, W_out, g1, g2, W1, W2, W3):
        import math
        import jax, jax.numpy as jnp
        import numpy as np
        B, T, D = (4, 1024, 256)
        H = 16
        HD = D // H
        CAP = int(1024 * 0.125)
        DFF = int(D * 4 * 2 / 3)
        EPS = 1e-06

        def rmsnorm(x, g):
            return x * jax.lax.rsqrt(jnp.mean(x * x, axis=-1, keepdims=True) + EPS) * g
        Bq, Tq, Dq = x.shape
        scores = x @ w_router
        _, idx = jax.lax.top_k(scores, CAP)
        x_sel = jnp.take_along_axis(x, idx[:, :, None], axis=1)
        h = rmsnorm(x_sel, g1)
        qkv = (h @ W_qkv.T).reshape(Bq, CAP, 3, H, HD)
        q, k, v = jnp.moveaxis(qkv, 2, 0)
        att = jnp.einsum('bqhd,bkhd->bhqk', q, k) / math.sqrt(HD)
        mask = jnp.triu(jnp.ones((CAP, CAP), bool), 1)
        att = jnp.where(mask, -jnp.inf, att)
        att = jax.nn.softmax(att, axis=-1)
        o = jnp.einsum('bhqk,bkhd->bqhd', att, v).reshape(Bq, CAP, Dq)
        x_attn = o @ W_out.T
        h2 = rmsnorm(x_sel + x_attn, g2)
        x_ff = jax.nn.silu(h2 @ W1.T) * (h2 @ W2.T) @ W3.T
        x_proc = x_sel + x_attn + x_ff
        out = x.at[jnp.arange(Bq)[:, None], idx].set(x_proc)
        return out

    def _L1_attn_ref(x, Wq, bq, Wk, bk, Wv, bv, Wo, bo, sample_idx):
        import math
        import jax, jax.numpy as jnp
        import numpy as np
        B, L, D_MODEL, NHEAD, FACTOR = (8, 1024, 256, 16, 5)
        D_HEAD = D_MODEL // NHEAD
        SAMPLE_K = min(L, max(1, FACTOR * int(math.ceil(math.log(max(L, 2))))))
        TOP_U = min(L, max(1, FACTOR * int(math.ceil(math.log(max(L, 2))))))

        def _split_heads(t):
            b, l, _ = t.shape
            return t.reshape(b, l, NHEAD, D_HEAD).transpose(0, 2, 1, 3)
        b, l, d = x.shape
        q = _split_heads(x @ Wq.T + bq)
        k = _split_heads(x @ Wk.T + bk)
        v = _split_heads(x @ Wv.T + bv)
        scale = 1.0 / math.sqrt(D_HEAD)
        k_sample = k[:, :, sample_idx, :]
        scores_sample = jnp.einsum('bhqd,bhsd->bhqs', q, k_sample) * scale
        m = scores_sample.max(axis=-1) - scores_sample.mean(axis=-1)
        _, top_idx = jax.lax.top_k(m, TOP_U)
        context = jnp.broadcast_to(v.mean(axis=-2, keepdims=True), (b, NHEAD, l, D_HEAD))
        q_top = jnp.take_along_axis(q, top_idx[..., None], axis=2)
        scores_top = jnp.einsum('bhud,bhkd->bhuk', q_top, k) * scale
        attn = jax.nn.softmax(scores_top, axis=-1)
        out_top = jnp.einsum('bhuk,bhkd->bhud', attn, v)
        bi = jnp.arange(b)[:, None, None]
        hi = jnp.arange(NHEAD)[None, :, None]
        context = context.at[bi, hi, top_idx].set(out_top)
        out = context.transpose(0, 2, 1, 3).reshape(b, l, d)
        return out @ Wo.T + bo

    def _L1_ffn_ref(x, ln_gamma, ln_beta, fc1_q, fc1_scales, fc1_bias, fc2_q, fc2_scales, fc2_bias):
        import jax, jax.numpy as jnp
        import numpy as np
        B, S, H, F, G = (8, 512, 256, 1024, 128)
        EPS = 1e-05

        def _dequant(q, scales, g):
            K, N = q.shape
            w = (q.astype(jnp.float32) - 128.0).reshape(K // g, g, N) * scales[:, None, :]
            return w.reshape(K, N)
        residual = x
        mu = jnp.mean(x, axis=-1, keepdims=True)
        var = jnp.mean(jnp.square(x - mu), axis=-1, keepdims=True)
        h = (x - mu) * jax.lax.rsqrt(var + EPS) * ln_gamma + ln_beta
        hf = h.reshape(-1, H)
        w1 = _dequant(fc1_q, fc1_scales, G)
        y = hf @ w1 + fc1_bias
        y = jax.nn.silu(y)
        w2 = _dequant(fc2_q, fc2_scales, G)
        z = y @ w2 + fc2_bias
        return residual + 0.5 * z.reshape(residual.shape)
    x = L0_attn_x
    x = x + _layernorm(_L0_attn_ref(_layernorm(x, axis=-1), L0_attn_W_attn, L0_attn_b_attn, L0_attn_W_proj, L0_attn_b_proj), axis=-1)
    x = x + _layernorm(_L0_ffn_ref(_layernorm(x, axis=-1), L0_ffn_w_router, L0_ffn_W_qkv, L0_ffn_W_out, L0_ffn_g1, L0_ffn_g2, L0_ffn_W1, L0_ffn_W2, L0_ffn_W3), axis=-1)
    x = x + _layernorm(_L1_attn_ref(_layernorm(x, axis=-1), L1_attn_Wq, L1_attn_bq, L1_attn_Wk, L1_attn_bk, L1_attn_Wv, L1_attn_bv, L1_attn_Wo, L1_attn_bo, L1_attn_sample_idx), axis=-1)
    x = x + _layernorm(_L1_ffn_ref(_layernorm(x, axis=-1), L1_ffn_ln_gamma, L1_ffn_ln_beta, L1_ffn_fc1_q, L1_ffn_fc1_scales, L1_ffn_fc1_bias, L1_ffn_fc2_q, L1_ffn_fc2_scales, L1_ffn_fc2_bias), axis=-1)
    return x

_drawn_inputs = setup_inputs


def setup_inputs(seed=0):
    import zlib

    import numpy as np

    out = dict(_drawn_inputs(seed))
    spreads = {'L0_attn_b_attn': (0.0, 0.1),
     'L0_attn_b_proj': (0.0, 0.1),
     'L0_ffn_g1': (1.0, 0.6),
     'L0_ffn_g2': (1.0, 0.6),
     'L1_attn_bq': (0.0, 2.0),
     'L1_attn_bk': (0.0, 2.0),
     'L1_attn_bv': (0.0, 0.1),
     'L1_attn_bo': (0.0, 0.1),
     'L1_ffn_ln_gamma': (1.0, 0.2),
     'L1_ffn_ln_beta': (0.0, 0.1)}
    factors = {'L0_ffn_w_router': 5.838,
     'L0_ffn_W_qkv': 5.895,
     'L0_ffn_W_out': 5.685,
     'L0_ffn_W1': 8.0,
     'L0_ffn_W2': 8.0,
     'L0_ffn_W3': 8.0,
     'L1_attn_Wq': 8.0,
     'L1_attn_Wk': 8.0,
     'L1_ffn_fc1_bias': 64.0,
     'L1_ffn_fc2_bias': 64.0}
    for name, (base, spread) in spreads.items():
        noise = np.random.default_rng([zlib.crc32(name.encode()), seed]).standard_normal(out[name].shape)
        drawn = base * np.exp(spread * noise) if base else spread * noise
        out[name] = jnp.asarray(drawn.astype(out[name].dtype))
    for name, factor in factors.items():
        out[name] = (out[name] * factor).astype(out[name].dtype)
    return out
```

```python
import math
from contextlib import ExitStack

import numpy as np

import concourse.bass as bass
from concourse import mybir

F32 = mybir.dt.float32
BF16 = mybir.dt.bfloat16
I32 = mybir.dt.int32
U32 = mybir.dt.uint32
ALU = mybir.AluOpType
ACT = mybir.ActivationFunctionType
AX = mybir.AxisListType

P = 128
B, T, C = 8, 1024, 256
NT = T // P
KC = C // P
H = 16
D = C // H
HC = H // KC
BANK = 512
NHALF = T // BANK
SCALE = 1.0 / math.sqrt(D)
CAP = 128
DFF = 682
FT = -(-DFF // P)
S = 35
S1 = S + 1
HU = H * S
MT = 5
MR = HU // MT
F2 = 1024
F2T = F2 // P
EPS_LN = 1e-5
EPS_RMS = 1e-6
NEG = -1e30
ROUNDS_C = CAP // 8
ROUNDS_E = -(-S // 8)


class Memory:

    def __init__(self, nc):
        self.nc = nc
        self.stack = ExitStack()
        self.sems = []

    def __enter__(self):
        self.stack.__enter__()
        return self

    def __exit__(self, *e):
        return self.stack.__exit__(*e)

    def sb(self, name, shape, dt=F32):
        return self.stack.enter_context(self.nc.sbuf_tensor(name, shape, dt))

    def sem(self, name):
        s = self.stack.enter_context(self.nc.semaphore(name))
        self.sems.append(s)
        return s

    def clear(self):
        for s in self.sems:
            self.nc.sync.sem_clear(s)
        self.nc.all_engine_barrier()


def spread(ap, axis, n):
    ap = ap.unsqueeze(axis)
    shape = list(ap.shape)
    shape[axis] = n
    return ap.to_broadcast(shape)


def over_partitions(row, n=P):
    return row.partition_broadcast(n)



def setup_attention(nc, io, w, ps):
    with Memory(nc) as m:
        loaded = m.sem("loaded")
        made = m.sem("made")
        zeroed = m.sem("zeroed")
        turned = m.sem("turned")
        cols = m.sem("cols")
        rows = m.sem("rows")

        wqkv_raw = m.sb("wqkv_raw", [P, KC, 3 * C])
        ropec = m.sb("ropec", [P, H * D // 2])
        ropes = m.sb("ropes", [P, H * D // 2])
        brow = m.sb("brow", [1, 2 * C])
        brot = m.sb("brot", [1, 2 * C])
        one = m.sb("one", [1, 1])
        t0 = m.sb("t0", [P, H * D // 2])
        t1 = m.sb("t1", [P, H * D // 2])
        bv = m.sb("bv0", [P, KC])
        bvrep = m.sb("bvrep", [P, KC, P])
        bproj = m.sb("bproj", [P, C])
        iota_i = m.sb("iota_i", [P, T], I32)
        iota_c = m.sb("iota_c", [P, NT], I32)
        ones = m.sb("ones", [P, P])

        loads = [(wqkv_raw[:, :, :], io["L0_attn_W_attn"].rearrange("(k p) n -> p k n", p=P)),
                 (ropec[:, :], over_partitions(io["rope_cos"])),
                 (ropes[:, :], over_partitions(io["rope_sin"])),
                 (brow[:, :], io["L0_attn_b_attn"][0:2 * C].rearrange("(a n) -> a n", a=1)),
                 (bv[:, :], io["L0_attn_b_attn"][2 * C:3 * C].rearrange("(k p) -> p k", p=P)),
                 (bproj[:, :], over_partitions(io["L0_attn_b_proj"])),
                 (w["wproj"][:, :, :], io["L0_attn_W_proj"].rearrange("(k p) n -> p k n", p=P)),
                 (w["router"][:, :], over_partitions(io["L0_ffn_w_router"]))]

        with nc.Block() as block:
            @block.sync
            def _(sp):
                with nc.allow_non_contiguous_dma(reason="a few columns of a bias"):
                    for dst, src in loads:
                        sp.dma_start(dst, src).then_inc(loaded, 16)

            @block.gpsimd
            def _(g):
                nc.gpsimd.memset(ones[:, :], 1.0).then_inc(made, 1)
                nc.gpsimd.memset(w["ident"][:, :], 0.0).then_inc(made, 1)
                nc.gpsimd.memset(w["bdmask"][:, :, :], 1.0).then_inc(made, 1)
                nc.gpsimd.memset(w["mhalf"][:, :], -0.5)
                nc.gpsimd.iota(iota_i[:, :], pattern=[[1, T]], base=0, channel_multiplier=0)
                nc.gpsimd.iota(iota_c[:, :], pattern=[[P, NT]], base=0, channel_multiplier=1)
                g.wait_ge(made, 3)
                nc.gpsimd.affine_select(out=w["ident"][:, :], in_=w["ident"][:, :], compare_op=ALU.not_equal,
                                        fill=1.0, base=0, pattern=[[-1, P]], channel_multiplier=1)
                nc.gpsimd.affine_select(out=w["bdmask"][:, :, :], in_=w["bdmask"][:, :, :], compare_op=ALU.is_ge,
                                        fill=0.0, base=0, pattern=[[-D, HC], [0, S1]],
                                        channel_multiplier=1).then_inc(made, 1)
                g.wait_ge(made, 4)
                nc.gpsimd.affine_select(out=w["bdmask"][:, :, :], in_=w["bdmask"][:, :, :], compare_op=ALU.is_ge,
                                        fill=0.0, base=D - 1, pattern=[[D, HC], [0, S1]],
                                        channel_multiplier=-1).then_inc(made, 1)
                g.wait_ge(zeroed, 1)
                nc.gpsimd.affine_select(out=w["mask_qk"][:, :], in_=w["zeros16"][:, :], compare_op=ALU.is_ge,
                                        fill=NEG, base=0, pattern=[[-1, P]], channel_multiplier=1)
                nc.gpsimd.affine_select(out=w["mask_kq"][:, :], in_=w["zeros16"][:, :], compare_op=ALU.is_ge,
                                        fill=NEG, base=0, pattern=[[1, P]], channel_multiplier=-1)
                nc.gpsimd.affine_select(out=w["mask_f32"][:, :], in_=w["zeros32"][:, :], compare_op=ALU.is_ge,
                                        fill=NEG, base=0, pattern=[[-1, P]], channel_multiplier=1)

            @block.vector
            def _(v):
                nc.vector.memset(w["zeros32"][:, :], 0.0)
                nc.vector.memset(w["zeros16"][:, :], 0.0).then_inc(zeroed, 1)
                v.wait_ge(loaded, 16 * len(loads))
                for src, dst, n in [(wqkv_raw[:, k, :], w["wqkv"][:, k, :], P) for k in range(KC)] \
                        + [(brow[:, :], brot[:, :], 1)]:
                    for qk in range(2):
                        a = src[:, qk * C:(qk + 1) * C].rearrange("p (n two) -> p n two", two=2)
                        o = dst[:, qk * C:(qk + 1) * C].rearrange("p (n two) -> p n two", two=2)
                        for into, x, y, op in ((0, 0, 1, ALU.subtract), (1, 1, 0, ALU.add)):
                            nc.vector.tensor_tensor(t0[0:n, :], a[:, :, x], ropec[0:n, :], ALU.mult)
                            nc.vector.tensor_tensor(t1[0:n, :], a[:, :, y], ropes[0:n, :], ALU.mult)
                            nc.vector.drain()
                            nc.vector.tensor_tensor(o[:, :, into], t0[0:n, :], t1[0:n, :], op)
                            nc.vector.drain()
                nc.vector.memset(one[:, :], 1.0)
                v.wait_ge(made, 5)
                for k in range(KC):
                    nc.vector.tensor_copy(w["wqkv"][:, k, 2 * C:3 * C], wqkv_raw[:, k, 2 * C:3 * C])
                    nc.vector.tensor_scalar(bvrep[:, k, :], ones[:, :], bv[:, k:k + 1], None, ALU.mult)
                nc.vector.tensor_copy(w["ident16"][:, :], w["ident"][:, :]).then_inc(turned, 1)
                nc.vector.tensor_copy(w["iota_row"][:, :], iota_i[:, :])
                nc.vector.tensor_copy(w["iota_col"][:, :], iota_c[:, :])
                v.wait_ge(cols, 1)
                nc.vector.tensor_copy(w["bqk"][:, :], ps[:, 6, 0:2 * KC])
                v.wait_ge(rows, 1)
                nc.vector.tensor_tensor(w["bias_proj"][:, :], ps[:, 7, 0:C], bproj[:, :], ALU.add)

            @block.tensor
            def _(pe):
                pe.wait_ge(turned, 1)
                for n in range(2 * KC):
                    last = nc.tensor.matmul(ps[:, 6, n:n + 1], brot[0:1, n * P:(n + 1) * P], one[:, :],
                                            start=True, stop=True)
                last.then_inc(cols, 1)
                for k in range(KC):
                    last = nc.tensor.matmul(ps[:, 7, 0:C], bvrep[:, k, :], w["wproj"][:, k, :],
                                            start=(k == 0), stop=(k == KC - 1))
                last.then_inc(rows, 1)
        m.clear()


def setup_rest_and_top_tokens(nc, io, w, ps):
    with Memory(nc) as m:
        loaded = m.sem("loaded2")
        q_loaded = m.sem("q_loaded")
        padded = m.sem("padded")
        flipped = m.sem("flipped")
        flipped_out = m.sem("flipped_out")
        unpacked = m.sem("unpacked")
        scaled = m.sem("scaled")
        sc_full = m.sem("sc_full")
        sc_ready = m.sem("sc_ready")
        sc_out = m.sem("sc_out")
        sc_in = m.sem("sc_in")
        idx_ready = m.sem("idx_ready")
        idx_out = m.sem("idx_out")

        sidx = m.sb("sidx", [P, S], I32)
        sidxf = m.sb("sidxf", [P, S])
        bigq = m.sb("bigq", [P, 2, F2], I32)
        scl = m.sb("scl", [P, 2, F2])
        b2row = m.sb("b2row", [P, C])
        sct = m.sb("sct", [B * NT, P])
        s8 = m.sb("s8", [B, T])
        top = m.sb("top8", [B, CAP])
        idx = m.sb("idx", [B, CAP], U32)
        idxf = m.sb("idxf", [B, CAP])

        turn = [(io["L0_ffn_W_qkv"], 3 * C, w["mod_wqkv"]), (io["L0_ffn_W_out"], C, w["mod_wout"]),
                (io["L0_ffn_W1"], DFF, w["mod_w1"]), (io["L0_ffn_W2"], DFF, w["mod_w2"]),
                (io["L1_attn_Wq"], C, w["ps_wq"]), (io["L1_attn_Wk"], C, w["ps_wk"]),
                (io["L1_attn_Wv"], C, w["ps_wv"]), (io["L1_attn_Wo"], C, w["ps_wo"])]
        stage = [m.sb(f"stage{n}", [P, -(-nrows // P), C]) for n, (_, nrows, _) in enumerate(turn)]
        w3 = m.sb("w3stage", [P, KC, DFF])
        loads = [(w["g1"][:, :], over_partitions(io["L0_ffn_g1"])),
                 (w["g2"][:, :], over_partitions(io["L0_ffn_g2"])),
                 (sidx[:, :], over_partitions(io["L1_attn_sample_idx"])),
                 (w["ps_bq"][:, :], over_partitions(io["L1_attn_bq"])),
                 (w["ps_bv"][:, :], over_partitions(io["L1_attn_bv"])),
                 (w["ps_bo"][:, :], over_partitions(io["L1_attn_bo"])),
                 (b2row[:, :], over_partitions(io["L1_ffn_fc2_bias"])),
                 (w["ps_bk"][:, :], io["L1_attn_bk"].rearrange("(k p) -> p k", p=P)),
                 (w["gamma"][:, :], io["L1_ffn_ln_gamma"].rearrange("(k p) -> p k", p=P)),
                 (w["beta"][:, :], io["L1_ffn_ln_beta"].rearrange("(k p) -> p k", p=P)),
                 (w["fc1_b"][:, :], io["L1_ffn_fc1_bias"].rearrange("(k p) -> p k", p=P)),
                 (w3[:, :, :], io["L0_ffn_W3"].rearrange("(a p) n -> p a n", p=P))]
        pieces = []
        for n, (src, nrows, dst) in enumerate(turn):
            full = nrows // P
            loads.append((stage[n][:, 0:full, :], src[0:full * P, :].rearrange("(a p) c -> p a c", p=P)))
            if nrows % P:
                loads.append((stage[n][0:nrows % P, full, :], src[full * P:nrows, :]))
            for a in range(-(-nrows // P)):
                r = min(P, nrows - a * P)
                for c in range(KC):
                    pieces.append((stage[n][0:r, a, c * P:(c + 1) * P], dst[:, c, a * P:a * P + r], P, r))
        for a in range(FT):
            k = min(P, DFF - a * P)
            for c in range(KC):
                pieces.append((w3[:, c, a * P:a * P + k], w["mod_w3"][0:k, a, c * P:(c + 1) * P], k, P))
        quant = [(io["L1_ffn_fc1_q"][k * P:(k + 1) * P, :], io["L1_ffn_fc1_scales"][k, :], w["fc1"][:, k, :], 1)
                 for k in range(KC)]
        quant += [(io["L1_ffn_fc2_q"][n * 4 * P:(n + 1) * 4 * P, :],
                   io["L1_ffn_fc2_scales"][n * 4:(n + 1) * 4, :].rearrange("k n -> (k n)"),
                   w["fc2"][:, n * 4:(n + 1) * 4, :].rearrange("p k n -> p (k n)"), 4) for n in range(2)]

        with nc.Block() as block:
            @block.sync
            def _(sp):
                with nc.allow_non_contiguous_dma(reason="a few columns of a bias"):
                    for dst, src in loads:
                        sp.dma_start(dst, src).then_inc(loaded, 16)
                sp.wait_ge(sc_ready, 1)
                sp.dma_start(io["scores"], sct[:, :]).then_inc(sc_out, 16)
                sp.wait_ge(sc_out, 16)
                sp.dma_start(s8[:, :], io["scores"].rearrange("(b j) p -> b (j p)", b=B)).then_inc(sc_in, 16)
                for n, (codes, scales, _, k) in enumerate(quant):
                    if n >= 2:
                        sp.wait_ge(scaled, n - 1)
                    sp.dma_start(bigq[:, n % 2, :].rearrange("p (k n) -> p k n", k=k),
                                 codes.rearrange("(k p) n -> p k n", p=P)).then_inc(q_loaded, 16)
                    sp.dma_start(scl[:, n % 2, :], over_partitions(scales)).then_inc(q_loaded, 16)
                    sp.wait_ge(q_loaded, 32 * (n + 1))
                sp.wait_ge(idx_ready, 1)
                sp.dma_start(io["top_tokens"], idxf[:, :]).then_inc(idx_out, 16)
                sp.wait_ge(idx_out, 16)

            @block.gpsimd
            def _(g):
                for n, (_, _, dst, _) in enumerate(quant):
                    g.wait_ge(q_loaded, 32 * (n + 1))
                    nc.gpsimd.tensor_copy(dst, bigq[:, n % 2, :]).then_inc(unpacked, 1)

            @block.vector
            def _(v):
                nc.vector.memset(w["mod_w1"][:, :, DFF:FT * P], 0.0)
                nc.vector.memset(w["mod_w2"][:, :, DFF:FT * P], 0.0)
                nc.vector.memset(w["mod_w3"][:, FT - 1, :], 0.0).then_inc(padded, 1)
                v.wait_ge(sc_full, 1)
                nc.vector.tensor_copy(sct[:, :], ps[0:B * NT, 7, 0:P]).then_inc(sc_ready, 1)
                v.wait_ge(sc_in, 16)
                for n in range(ROUNDS_C):
                    t8 = slice(8 * n, 8 * n + 8)
                    nc.vector.max(top[:, t8], s8[:, :])
                    nc.vector.drain()
                    nc.vector.max_index(idx[:, t8], top[:, t8], s8[:, :])
                    nc.vector.drain()
                    if n < ROUNDS_C - 1:
                        nc.vector.match_replace(s8[:, :], top[:, t8], s8[:, :], -3e38)
                        nc.vector.drain()
                nc.vector.tensor_copy(idxf[:, :], idx[:, :]).then_inc(idx_ready, 1)
                for n, (_, _, dst, _) in enumerate(quant):
                    v.wait_ge(unpacked, n + 1)
                    nc.vector.scalar_tensor_tensor(dst, dst, -128.0, scl[:, n % 2, :],
                                                   ALU.add, ALU.mult).then_inc(scaled, 1)
                nc.vector.drain()
                nc.vector.tensor_scalar(w["fc2"][:, :, :], w["fc2"][:, :, :], 0.5, None, ALU.mult)
                v.wait_ge(loaded, 16 * len(loads))
                nc.vector.tensor_scalar(w["fc2_b"][:, :], b2row[:, :], 0.5, None, ALU.mult)
                nc.vector.tensor_copy(sidxf[:, :], sidx[:, :])
                nc.vector.drain()
                for j in range(NT):
                    nc.vector.tensor_scalar(w["onehot_s"][:, j, :], sidxf[:, :], w["iota_col"][:, j:j + 1], None,
                                            ALU.is_equal)

            @block.tensor
            def _(pe):
                nc.tensor.transpose(ps[0:B * NT, 7, 0:P], w["scores"][:, :, :].rearrange("p b j -> p (b j)"),
                                    w["ident"][:, :]).then_inc(sc_full, 1)
                pe.wait_ge(loaded, 16 * len(loads))
                for n, (src, _, k, r) in enumerate(pieces):
                    if n >= 4:
                        pe.wait_ge(flipped_out, n - 3)
                    nc.tensor.transpose(ps[0:k, n % 4, 0:r], src,
                                        w["ident"][0:src.shape[0], 0:src.shape[0]]).then_inc(flipped, 1)

            @block.scalar
            def _(a):
                a.wait_ge(padded, 1)
                for n, (_, dst, k, r) in enumerate(pieces):
                    a.wait_ge(flipped, n + 1)
                    nc.scalar.copy(dst, ps[0:k, n % 4, 0:r]).then_inc(flipped_out, 1)
        m.clear()


TABLES = {
    "ident": ([P, P], F32), "ident16": ([P, P], BF16), "mask_qk": ([P, P], BF16), "mask_kq": ([P, P], BF16),
    "zeros16": ([P, P], BF16), "zeros32": ([P, P], F32), "mask_f32": ([P, P], F32),
    "bdmask": ([P, HC, S1], F32), "mhalf": ([P, NT], F32),
    "iota_row": ([P, T], F32), "iota_col": ([P, NT], F32),
    "scores": ([P, B, NT], F32),
}
ATTENTION_WEIGHTS = {
    "wqkv": ([P, KC, 3 * C], F32), "bqk": ([P, 2 * KC], F32), "wproj": ([P, KC, C], F32),
    "bias_proj": ([P, C], F32), "router": ([P, C], F32),
}
MOD_WEIGHTS = {
    "g1": ([P, C], F32), "g2": ([P, C], F32), "onehot_s": ([P, NT, S], F32),
    "mod_wqkv": ([P, KC, 3 * C], F32), "mod_wout": ([P, KC, C], F32),
    "mod_w1": ([P, KC, FT * P], F32), "mod_w2": ([P, KC, FT * P], F32), "mod_w3": ([P, FT, C], F32),
    "measure": ([P, NT, B * H], F32),
}
OTHER_WEIGHTS = {
    "ps_wq": ([P, KC, C], F32), "ps_wk": ([P, KC, C], F32), "ps_wv": ([P, KC, C], F32), "ps_wo": ([P, KC, C], F32),
    "ps_bq": ([P, C], F32), "ps_bv": ([P, C], F32), "ps_bo": ([P, C], F32), "ps_bk": ([P, KC], F32),
    "gamma": ([P, KC], F32), "beta": ([P, KC], F32),
    "fc1": ([P, KC, F2], F32), "fc1_b": ([P, F2T], F32), "fc2": ([P, F2T, C], F32), "fc2_b": ([P, C], F32),
}



SETS = 4
HS = H // SETS
PARTS = 3
Q_PARTS = (0, 0, 0, 1, 1, 2)
K_PARTS = (0, 1, 2, 0, 1, 0)
ROWS = len(Q_PARTS) * D
ROWS_M = ROWS + PARTS


def max_units():
    return [(i, n, n * BANK, min(BANK, (i + 1) * P - n * BANK))
            for i in range(NT) for n in range(NHALF) if (i + 1) * P > n * BANK]


def exp_units():
    return [(n, j, max(n * BANK, j * P), (n + 1) * BANK - max(n * BANK, j * P))
            for n in range(NHALF) for j in range((n + 1) * BANK // P)]


MU = max_units()
EU = exp_units()


def layer_stats(nc, stats, mv, tile, j):
    nc.vector.bn_stats(stats[:, j, :], tile)
    nc.vector.drain()
    return nc.vector.bn_aggr(mv[:, j, :], stats[:, j, :])


def rstd_of(nc, var, out, w, n, eps, ready, tmp, count):
    nc.gpsimd.tensor_scalar(tmp, var, eps, None, ALU.add).then_inc(ready, 1)
    nc.gpsimd.wait_ge(ready, count)
    return nc.gpsimd.tensor_tensor(out, tmp, w["mhalf"][:, 0:n], ALU.pow)


def attention_loop(nc, io, w, ps):
    with Memory(nc) as m:
        x = m.sb("x", [P, NT, C])
        xn = m.sb("xn", [P, NT, C])
        stats = m.sb("stats", [P, NT, 6])
        mv = m.sb("mv", [P, NT, 2])
        vtmp = m.sb("vtmp", [P, NT])
        rstd = m.sb("rstd", [P, NT])
        xnt = m.sb("xnt", [P, KC, T])
        qk = m.sb("qk", [P, 2 * KC, T])
        rest = m.sb("rest", [P, T])
        part = m.sb("part", [P, 2 * KC, PARTS, T], BF16)
        sq = m.sb("sq", [P, H, T], BF16)
        sk = m.sb("sk", [P, H, T], BF16)
        val = m.sb("val", [P, NT, H, 32])
        mx = m.sb("mx", [P, H, NT, NHALF])
        nm = m.sb("nm", [P, H, NT])
        nmr = m.sb("nmr", [P, P])
        nmp = m.sb("nmp", [P, PARTS, P], BF16)
        pt = m.sb("pt", [P, 3, HS, BANK])
        yt = qk
        rs = m.sb("rs", [P, 2, H])
        yn = m.sb("yn", [P, 2, H, D])
        ynt = m.sb("ynt", [P, 2, KC, P])
        att = xnt[:, :, :].rearrange("p k (j c) -> p (k j) c", c=C)
        sc = m.sb("sc", [P, NT])
        junk = m.sb("junk", [P, C])

        x_in = m.sem("x_in")
        x_stat = m.sem("x_stat")
        pool_step = m.sem("pool_step")
        x_rstd = m.sem("x_rstd")
        xn_ready = m.sem("xn_ready")
        xnt_full = m.sem("xnt_full")
        xnt_ready = m.sem("xnt_ready")
        qk_full = m.sem("qk_full")
        qk_ready = m.sem("qk_ready")
        v_full = m.sem("v_full")
        v_ready = m.sem("v_ready")
        parts_ready = m.sem("parts_ready")
        parts_out = [m.sem(f"parts_out{n}") for n in range(2 * KC)]
        stack_in = [m.sem(f"stack_in{n}") for n in range(KC)]
        m_full = m.sem("m_full")
        m_free = m.sem("m_free")
        nm_ready = m.sem("nm_ready")
        nmp_ready = m.sem("nmp_ready")
        nm_out = m.sem("nm_out")
        nm_in = [m.sem(f"nm_in{s}") for s in range(SETS)]
        s_full = m.sem("s_full")
        exp_done = m.sem("exp_done")
        av_done = m.sem("av_done")
        yt_ready = m.sem("yt_ready")
        yq_full = m.sem("yq_full")
        yn_ready = m.sem("yn_ready")
        ynt_full = m.sem("ynt_full")
        ynt_ready = m.sem("ynt_ready")
        proj_full = m.sem("proj_full")
        att_ready = m.sem("att_ready")
        a_stat = m.sem("a_stat")
        a_rstd = m.sem("a_rstd")
        a_norm = m.sem("a_norm")
        x1_ready = m.sem("x1_ready")
        x1_stat = m.sem("x1_stat")
        x1_rstd = m.sem("x1_rstd")
        xn1_ready = m.sem("xn1_ready")
        out_done = m.sem("out_done")
        preset = m.sem("preset")

        with nc.Block() as block:
            @block.vector
            def _(v):
                nc.vector.memset(val[:, :, :, D:32], 0.0)
                nc.vector.memset(sk[ROWS:P, :, :], 1.0)
                nc.vector.memset(mx[:, :, :, :], -3e38)
                nc.vector.drain()
                nc.vector.memset(val[:, :, :, D:D + 1], 1.0)
        m.clear()

        n_eu = len(EU)

        with nc.Fori(0, B) as b:
            with nc.Block() as block:
                @block.sync
                def _(sp):
                    for j in range(NT):
                        sp.dma_start(x[:, j, :], io["x"][b, j * P:(j + 1) * P, :]).then_inc(x_in, 16)
                    for n, cc in enumerate((0, 2, 1, 3)):
                        sp.wait_ge(parts_ready, n + 1)
                        sp.dma_start(io["parts"][cc].rearrange("a r t -> r a t"),
                                     part[:, cc, :, :]).then_inc(parts_out[n], 16)
                    for n, cc in enumerate((0, 2, 1, 3)):
                        sp.wait_ge(parts_out[n], 16)
                        dst, use = (sq, Q_PARTS) if cc < KC else (sk, K_PARTS)
                        h0 = (cc % KC) * HC
                        for a, p_ in enumerate(use):
                            sp.dma_start(dst[a * D:(a + 1) * D, h0:h0 + HC, :],
                                         io["parts"][cc, p_].rearrange("(h d) t -> d h t", d=D))\
                                .then_inc(stack_in[cc % KC], 16)
                    for s in range(SETS):
                        sp.wait_ge(nmp_ready, s + 1)
                        sp.dma_start(io["nm_parts"][:, s].rearrange("a r q -> r a q"),
                                     nmp[0:HS * NT, :, :]).then_inc(nm_out, 16)
                        sp.wait_ge(nm_out, 16 * (s + 1))
                        sp.dma_start(sq[ROWS:ROWS_M, s * HS:(s + 1) * HS, :],
                                     io["nm_parts"][:, s].rearrange("a (h i) q -> a h (i q)", h=HS))\
                            .then_inc(nm_in[s], 16)
                    for j in range(NT):
                        sp.wait_ge(x1_ready, j + 1)
                        sp.dma_start(io["x1"][b, j * P:(j + 1) * P, :], x[:, j, :]).then_inc(out_done, 16)
                    for j in range(NT):
                        sp.wait_ge(xn1_ready, j + 1)
                        sp.dma_start(io["xn1"][b, j * P:(j + 1) * P, :], xn[:, j, :]).then_inc(out_done, 16)
                    sp.wait_ge(out_done, 16 * 2 * NT)

                @block.gpsimd
                def _(g):
                    g.wait_ge(x_stat, 1)
                    rstd_of(nc, mv[:, :, 1], rstd[:, :], w, NT, EPS_LN, pool_step, vtmp[:, :], 1).then_inc(x_rstd, 1)
                    g.wait_ge(a_stat, 1)
                    rstd_of(nc, mv[:, :, 1], rstd[:, :], w, NT, EPS_LN, pool_step, vtmp[:, :], 2).then_inc(a_rstd, 1)
                    for j in range(NT):
                        g.wait_ge(a_norm, j + 1)
                        nc.gpsimd.tensor_tensor(x[:, j, :], x[:, j, :], att[:, j, :], ALU.add).then_inc(x1_ready, 1)
                    g.wait_ge(x1_stat, 1)
                    rstd_of(nc, mv[:, :, 1], rstd[:, :], w, NT, EPS_LN, pool_step, vtmp[:, :], 3).then_inc(x1_rstd, 1)

                @block.vector
                def _(v):
                    for j in range(NT):
                        v.wait_ge(x_in, 16 * NT)
                        last = layer_stats(nc, stats, mv, x[:, j, :], j)
                    last.then_inc(x_stat, 1)
                    v.wait_ge(x_rstd, 1)
                    for j in range(NT):
                        nc.vector.tensor_scalar(xn[:, j, :], x[:, j, :], mv[:, j, 0:1], rstd[:, j:j + 1],
                                                ALU.subtract, ALU.mult).then_inc(xn_ready, 1)
                    for n, cc in enumerate((0, 2, 1, 3)):
                        v.wait_ge(qk_ready, NHALF * (n + 1))
                        nc.vector.tensor_copy(part[:, cc, 0, :], qk[:, cc, :])
                        nc.vector.drain()
                        nc.vector.tensor_tensor(rest[:, :], qk[:, cc, :], part[:, cc, 0, :], ALU.subtract)
                        nc.vector.drain()
                        nc.vector.tensor_copy(part[:, cc, 1, :], rest[:, :])
                        nc.vector.drain()
                        nc.vector.tensor_tensor(part[:, cc, 2, :], rest[:, :], part[:, cc, 1, :],
                                                ALU.subtract).then_inc(parts_ready, 1)
                        nc.vector.drain()
                    for s in range(SETS):
                        n_unit = 0
                        for hh, i, half, n in set_units(s):
                            v.wait_ge(m_full, slot_of(s, n_unit) + 1)
                            nc.vector.reduce_max(mx[:, s * HS + hh, i, half:half + 1],
                                                 ps[:, slot_of(s, n_unit) % 2, 0:n], AX.X).then_inc(m_free, 1)
                            n_unit += 1
                        nc.vector.drain()
                        nc.vector.tensor_reduce(nm[:, s * HS:(s + 1) * HS, :], mx[:, s * HS:(s + 1) * HS, :, :],
                                                AX.X, ALU.max, negate=True).then_inc(nm_ready, 1)
                        k = slot_of(s, n_unit)
                        R = HS * NT
                        v.wait_ge(m_full, k + 1)
                        if s:
                            v.wait_ge(nm_out, 16 * s)
                        nc.vector.tensor_copy(nmr[0:R, :], ps[0:R, k % 2, 0:P]).then_inc(m_free, 1)
                        nc.vector.drain()
                        nc.vector.tensor_copy(nmp[0:R, 0, :], nmr[0:R, :])
                        nc.vector.drain()
                        nc.vector.tensor_tensor(nmr[0:R, :], nmr[0:R, :], nmp[0:R, 0, :], ALU.subtract)
                        nc.vector.drain()
                        nc.vector.tensor_copy(nmp[0:R, 1, :], nmr[0:R, :])
                        nc.vector.drain()
                        nc.vector.tensor_tensor(nmp[0:R, 2, :], nmr[0:R, :], nmp[0:R, 1, :],
                                                ALU.subtract).then_inc(nmp_ready, 1)
                    for i in range(NT + 1):
                        if i < NT:
                            v.wait_ge(yq_full, i + 1)
                            if i >= 2:
                                v.wait_ge(ynt_full, i - 1)
                            yq = ps[:, i % 2, :].rearrange("p (h d) -> p h d", d=32)
                            nc.vector.reciprocal(rs[:, i % 2, :], yq[:, :, D])
                            nc.vector.drain()
                            nc.vector.tensor_tensor(yn[:, i % 2, :, :], yq[:, :, 0:D],
                                                    spread(rs[:, i % 2, :], 2, D), ALU.mult).then_inc(yn_ready, 1)
                        if i >= 1:
                            v.wait_ge(proj_full, i)
                            nc.vector.tensor_tensor(att[:, i - 1, :], ps[:, 4 + (i - 1) % 2, 0:C], w["bias_proj"][:, :],
                                                    ALU.add).then_inc(att_ready, 1)
                            nc.vector.drain()
                            last = layer_stats(nc, stats, mv, att[:, i - 1, :], i - 1)
                    last.then_inc(a_stat, 1)
                    v.wait_ge(a_rstd, 1)
                    for j in range(NT):
                        nc.vector.tensor_scalar(att[:, j, :], att[:, j, :], mv[:, j, 0:1], rstd[:, j:j + 1],
                                                ALU.subtract, ALU.mult).then_inc(a_norm, 1)
                    nc.vector.drain()
                    for j in range(NT):
                        v.wait_ge(x1_ready, j + 1)
                        last = layer_stats(nc, stats, mv, x[:, j, :], j)
                    last.then_inc(x1_stat, 1)
                    v.wait_ge(x1_rstd, 1)
                    for j in range(NT):
                        nc.vector.tensor_scalar(xn[:, j, :], x[:, j, :], mv[:, j, 0:1], rstd[:, j:j + 1],
                                                ALU.subtract, ALU.mult).then_inc(xn1_ready, 1)
                        nc.vector.drain()
                        nc.vector.scalar_tensor_tensor(junk[:, :], xn[:, j, :], 1.0, w["router"][:, :],
                                                       ALU.mult, ALU.mult, accum_out=sc[:, j:j + 1])
                    nc.vector.drain()
                    nc.vector.tensor_copy(w["scores"][:, bass.ds(b, 1), :], spread(sc[:, :], 1, 1))

                @block.tensor
                def _(pe):
                    for n in range(NHALF):
                        pe.wait_ge(xn_ready, 4 * (n + 1))
                        for k in range(KC):
                            for t in range(4):
                                last = nc.tensor.transpose(ps[:, 2 * n + k, t * P:(t + 1) * P],
                                                           xn[:, 4 * n + t, k * P:(k + 1) * P], w["ident"][:, :])
                            last.then_inc(xnt_full, 1)
                    pe.wait_ge(xnt_ready, NHALF * KC)
                    u = 0
                    for cc in (0, 2, 1, 3):
                        for n in range(NHALF):
                            if u >= 4:
                                pe.wait_ge(qk_ready, u - 3)
                            for k in range(KC):
                                last = nc.tensor.matmul(ps[:, 4 + u % 4, :], w["wqkv"][:, k, cc * P:(cc + 1) * P],
                                                        xnt[:, k, n * BANK:(n + 1) * BANK],
                                                        start=(k == 0), stop=(k == KC - 1))
                            last.then_inc(qk_full, 1)
                            u += 1
                    for j in range(NT):
                        if j >= 4:
                            pe.wait_ge(v_ready, j - 3)
                        for k in range(KC):
                            last = nc.tensor.matmul(ps[:, j % 4, 0:C], xnt[:, k, j * P:(j + 1) * P],
                                                    w["wqkv"][:, k, 2 * C:3 * C], start=(k == 0), stop=(k == KC - 1))
                        last.then_inc(v_full, 1)
                    pe.wait_ge(v_ready, NT)
                    pe.wait_ge(qk_ready, 2 * KC * NHALF)

                    def max_unit(s, n_unit):
                        hh, i, half, n = set_units(s)[n_unit]
                        h, k = s * HS + hh, slot_of(s, n_unit)
                        if n_unit == 0:
                            pe.wait_ge(stack_in[s * HS // HC], 16 * 2 * len(Q_PARTS))
                        if k >= 2:
                            pe.wait_ge(m_free, k - 1)
                        diag = (i * P) // BANK == half
                        last = nc.tensor.matmul(ps[:, k % 2, 0:n], sq[0:ROWS, h, i * P:(i + 1) * P],
                                                sk[0:ROWS, h, half * BANK:half * BANK + n],
                                                start=True, stop=not diag)
                        if diag:
                            last = nc.tensor.matmul(ps[:, k % 2, n - P:n], w["ident16"][:, :], w["mask_qk"][:, :],
                                                    start=False, stop=True)
                        last.then_inc(m_full, 1)

                    def max_rows(s):
                        k = slot_of(s, len(set_units(s)))
                        pe.wait_ge(m_free, k - 1)
                        pe.wait_ge(nm_ready, s + 1)
                        nc.tensor.transpose(ps[0:HS * NT, k % 2, 0:P],
                                            nm[:, s * HS:(s + 1) * HS, :].rearrange("p h i -> p (h i)"),
                                            w["ident"][:, :]).then_inc(m_full, 1)

                    def exp_unit(s, g):
                        half, j, q0, n = EU[g]
                        if g == 0:
                            pe.wait_ge(nm_in[s], 16)
                        for pair in range(2):
                            t = 2 * (s * n_eu + g) + pair
                            if t >= 2:
                                pe.wait_ge(exp_done, t - 1)
                            for e in range(2):
                                h = s * HS + 2 * pair + e
                                bank = 2 + 2 * (t % 2) + e
                                diag = q0 == j * P
                                last = nc.tensor.matmul(ps[:, bank, 0:n], sk[0:ROWS_M, h, j * P:(j + 1) * P],
                                                        sq[0:ROWS_M, h, q0:q0 + n], start=True, stop=not diag)
                                if diag:
                                    last = nc.tensor.matmul(ps[:, bank, 0:P], w["ident16"][:, :], w["mask_kq"][:, :],
                                                            start=False, stop=True)
                            last.then_inc(s_full, 1)

                    def av_unit(s, g):
                        half, j, q0, n = EU[g]
                        t = s * n_eu + g
                        y = NHALF * s + half
                        if j == 0 and y >= 2:
                            pe.wait_ge(yt_ready, y - 1)
                        pe.wait_ge(exp_done, 2 * t + 2)
                        c0 = q0 - half * BANK
                        for hh in range(HS):
                            last = nc.tensor.matmul(ps[32 * hh:32 * hh + 32, 6 + half, c0:c0 + n],
                                                    val[:, j, s * HS + hh, :], pt[:, t % 3, hh, 0:n],
                                                    start=(j == 0), stop=(q0 + n == (j + 1) * P),
                                                    skip_group_check=True)
                        last.then_inc(av_done, 1)

                    for n_unit in range(len(set_units(0))):
                        max_unit(0, n_unit)
                    max_rows(0)
                    for s in range(SETS):
                        n_next = 0
                        for g in range(n_eu):
                            if s + 1 < SETS:
                                upto = min(len(set_units(s + 1)), (g + 1) * 5)
                                while n_next < upto:
                                    max_unit(s + 1, n_next)
                                    n_next += 1
                                if g == n_eu - 2:
                                    max_rows(s + 1)
                            exp_unit(s, g)
                            if g:
                                av_unit(s, g - 1)
                        av_unit(s, n_eu - 1)
                    for i in range(NT + 2):
                        if i < NT:
                            if i == 0:
                                pe.wait_ge(m_free, slots_total())
                                pe.wait_ge(yt_ready, NHALF * SETS)
                            if i >= 2:
                                pe.wait_ge(yn_ready, i - 1)
                            for s in range(SETS):
                                last = nc.tensor.transpose(ps[:, i % 2, s * P:(s + 1) * P],
                                                           yt[:, s, i * P:(i + 1) * P], w["ident"][:, :])
                            last.then_inc(yq_full, 1)
                        if 1 <= i <= NT:
                            t = i - 1
                            pe.wait_ge(yn_ready, t + 1)
                            if t >= 2:
                                pe.wait_ge(ynt_ready, t - 1)
                            for k in range(KC):
                                last = nc.tensor.transpose(
                                    ps[:, 2 + t % 2, k * P:(k + 1) * P],
                                    yn[:, t % 2, k * HC:(k + 1) * HC, :].rearrange("p h d -> p (h d)"), w["ident"][:, :])
                            last.then_inc(ynt_full, 1)
                        if i >= 2:
                            t = i - 2
                            pe.wait_ge(ynt_ready, t + 1)
                            if t >= 2:
                                pe.wait_ge(att_ready, t - 1)
                            for k in range(KC):
                                last = nc.tensor.matmul(ps[:, 4 + t % 2, 0:C], ynt[:, t % 2, k, :], w["wproj"][:, k, :],
                                                        start=(k == 0), stop=(k == KC - 1))
                            last.then_inc(proj_full, 1)

                @block.scalar
                def _(a):
                    for n in range(NHALF):
                        for k in range(KC):
                            a.wait_ge(xnt_full, KC * n + k + 1)
                            nc.scalar.copy(xnt[:, k, n * BANK:(n + 1) * BANK], ps[:, 2 * n + k, :]).then_inc(xnt_ready, 1)
                    u = 0
                    for cc in (0, 2, 1, 3):
                        for n in range(NHALF):
                            a.wait_ge(qk_full, u + 1)
                            nc.scalar.activation(qk[:, cc, n * BANK:(n + 1) * BANK], ps[:, 4 + u % 4, :], ACT.Identity,
                                                 bias=w["bqk"][:, cc:cc + 1]).then_inc(qk_ready, 1)
                            u += 1
                    for j in range(NT):
                        a.wait_ge(v_full, j + 1)
                        nc.scalar.copy(val[:, j, :, 0:D],
                                       ps[:, j % 4, 0:C].rearrange("p (h d) -> p h d", d=D)).then_inc(v_ready, 1)
                    for s in range(SETS):
                        for g in range(n_eu):
                            half, j, q0, n = EU[g]
                            if j == 0 and (s or half):
                                evacuate_y(nc, a, ps, yt, av_done, yt_ready, s, half)
                            for pair in range(2):
                                u = s * n_eu + g
                                t = 2 * u + pair
                                a.wait_ge(s_full, t + 1)
                                if u >= 3:
                                    a.wait_ge(av_done, u - 2)
                                bank = 2 + 2 * (t % 2)
                                nc.scalar.activation(pt[:, u % 3, 2 * pair:2 * pair + 2, 0:n], ps[:, bank:bank + 2, 0:n],
                                                     ACT.Exp, scale=SCALE).then_inc(exp_done, 1)
                    evacuate_y(nc, a, ps, yt, av_done, yt_ready, SETS, 0)
                    for i in range(NT):
                        a.wait_ge(ynt_full, i + 1)
                        nc.scalar.copy(ynt[:, i % 2, :, :],
                                       ps[:, 2 + i % 2, 0:C].rearrange("p (k t) -> p k t", k=KC)).then_inc(ynt_ready, 1)
            m.clear()


def set_units(s):
    return [(hh, i, half, n) for hh in range(HS) for i, half, _, n in MU]


def slot_of(s, n_unit):
    return s * (HS * len(MU) + 1) + n_unit


def slots_total():
    return SETS * (HS * len(MU) + 1)


def evacuate_y(nc, a, ps, yt, av_done, yt_ready, s, half):
    y = NHALF * s + half - 1
    s_, half_ = divmod(y, NHALF)
    done = s_ * len(EU) + sum(1 for u in EU if u[0] <= half_)
    a.wait_ge(av_done, done)
    nc.scalar.copy(yt[:, s_, half_ * BANK:(half_ + 1) * BANK], ps[:, 6 + half_, :]).then_inc(yt_ready, 1)



def mod_loop(nc, io, w, ps):
    with Memory(nc) as m:
        x = m.sb("cx", [P, NT, C])
        xn = m.sb("cxn", [P, NT, C])
        idxc = m.sb("idxc", [P, 1])
        idxb = m.sb("idxb", [P, CAP])
        oh = m.sb("oh", [P, NT, CAP])
        oht = m.sb("oht", [CAP, T])
        xs = m.sb("xs", [P, C])
        ss = m.sb("ss", [P, 2])
        stmp = m.sb("stmp", [P, 2])
        srs = m.sb("srs", [P, 2])
        junk = m.sb("cjunk", [P, C])
        hn = m.sb("hn", [P, C])
        hnt = m.sb("hnt", [P, KC, P])
        qt = m.sb("cqt", [P, KC, P])
        kbd = m.sb("kbd", [P, KC, HC, P])
        vv = m.sb("vv", [P, C])
        sm = m.sb("sm", [P, H, P])
        smx = m.sb("smx", [P, H])
        ssum = m.sb("ssum", [P, H])
        pt = m.sb("cpt", [P, H, P])
        o = m.sb("co", [P, H, D])
        ot = m.sb("cot", [P, KC, P])
        xa = m.sb("xa", [P, C])
        gate = m.sb("gate", [P, FT, P])
        delta = m.sb("delta", [P, C])
        stats = m.sb("cstats", [P, NT, 6])
        mv = m.sb("cmv", [P, NT, 2])
        vtmp = m.sb("cvtmp", [P, NT])
        rstd = m.sb("crstd", [P, NT])
        xnt = m.sb("cxnt", [P, KC, T])
        xst = m.sb("xst", [P, KC, S])
        ks = m.sb("ks", [P, KC, S1])
        ksbd = m.sb("ksbd", [P, KC, HC, S1])
        q = m.sb("cq", [P, NT, C])
        qtt = m.sb("qtt", [P, KC, T])
        mm = m.sb("mm", [P, NT, KC, HC])

        names = """x_in xn_in idx_in oh_ready oht_ready xs_full xs_ss rms_step rms_ready hn_ready hnt_full hnt_ready
            qk_full v_full qt_ready kbd_ready vv_ready s_full s_masked s_less exp_ready pt_full pt_ready pt_ready_v
            o_full o_ready ot_full ot_ready xa_full gate_full up_full silu_ready gate_ready ff_full delta_ready
            put_full put_ready a_stat a_rstd a_norm x2_ready x2_stat x2_rstd xn2_ready xnt_full xnt_ready xst_full
            xst_ready ks_full ksbd_ready q_full q_ready qtt_full qtt_ready ms_full ms_ready stored
            pool_step""".split()
        e = {n: m.sem("c_" + n) for n in names}

        with nc.Fori(0, B) as b:
            with nc.Block() as block:
                @block.sync
                def _(sp):
                    sp.dma_start(idxb[:, :], over_partitions(io["top_tokens"][b, :])).then_inc(e["idx_in"], 16)
                    sp.dma_start(idxc[:, :], io["top_tokens"][b, :].rearrange("(p a) -> p a", a=1))\
                        .then_inc(e["idx_in"], 16)
                    sp.dma_start(xn[:, :, :], io["xn1"][b].rearrange("(j p) c -> p j c", p=P)).then_inc(e["xn_in"], 16)
                    sp.dma_start(x[:, :, :], io["x1"][b].rearrange("(j p) c -> p j c", p=P)).then_inc(e["x_in"], 16)
                    sp.wait_ge(e["x2_ready"], NT)
                    sp.dma_start(io["x2"][b].rearrange("(j p) c -> p j c", p=P), x[:, :, :]).then_inc(e["stored"], 16)
                    sp.wait_ge(e["xn2_ready"], NT)
                    sp.dma_start(io["xn2"][b].rearrange("(j p) c -> p j c", p=P), xn[:, :, :]).then_inc(e["stored"], 16)
                    sp.wait_ge(e["q_ready"], NT)
                    sp.dma_start(io["q"][b].rearrange("(j p) c -> p j c", p=P), q[:, :, :]).then_inc(e["stored"], 16)
                    sp.wait_ge(e["stored"], 48)

                @block.gpsimd
                def _(g):
                    for n in range(2):
                        g.wait_ge(e["xs_ss"], n + 1)
                        nc.gpsimd.tensor_scalar(stmp[:, n:n + 1], ss[:, n:n + 1], 1.0 / C, EPS_RMS,
                                                ALU.mult, ALU.add).then_inc(e["rms_step"], 1)
                        g.wait_ge(e["rms_step"], n + 1)
                        nc.gpsimd.tensor_tensor(srs[:, n:n + 1], stmp[:, n:n + 1], w["mhalf"][:, 0:1],
                                                ALU.pow).then_inc(e["rms_ready"], 1)
                    g.wait_ge(e["a_stat"], 1)
                    rstd_of(nc, mv[:, :, 1], rstd[:, :], w, NT, EPS_LN, e["pool_step"], vtmp[:, :], 1)\
                        .then_inc(e["a_rstd"], 1)
                    g.wait_ge(e["x_in"], 16)
                    for j in range(NT):
                        g.wait_ge(e["a_norm"], j + 1)
                        nc.gpsimd.tensor_tensor(x[:, j, :], x[:, j, :], xn[:, j, :], ALU.add)\
                            .then_inc(e["x2_ready"], 1)
                    g.wait_ge(e["x2_stat"], 1)
                    rstd_of(nc, mv[:, :, 1], rstd[:, :], w, NT, EPS_LN, e["pool_step"], vtmp[:, :], 2)\
                        .then_inc(e["x2_rstd"], 1)

                @block.vector
                def _(v):
                    v.wait_ge(e["idx_in"], 32)
                    for j in range(NT):
                        nc.vector.tensor_scalar(oh[:, j, :], idxb[:, :], w["iota_col"][:, j:j + 1], None,
                                                ALU.is_equal).then_inc(e["oh_ready"], 1)
                    nc.vector.tensor_scalar(oht[:, :], w["iota_row"][:, :], idxc[:, :], None,
                                            ALU.is_equal).then_inc(e["oht_ready"], 1)
                    v.wait_ge(e["xs_full"], 1)
                    nc.vector.tensor_copy(xs[:, :], ps[:, 0, 0:C])
                    nc.vector.drain()
                    nc.vector.scalar_tensor_tensor(junk[:, :], xs[:, :], 1.0, xs[:, :], ALU.mult, ALU.mult,
                                                   accum_out=ss[:, 0:1]).then_inc(e["xs_ss"], 1)
                    v.wait_ge(e["rms_ready"], 1)
                    nc.vector.scalar_tensor_tensor(hn[:, :], xs[:, :], srs[:, 0:1], w["g1"][:, :],
                                                   ALU.mult, ALU.mult).then_inc(e["hn_ready"], 1)
                    v.wait_ge(e["qk_full"], 1)
                    for k in range(KC):
                        nc.vector.tensor_tensor(kbd[:, k, :, :], spread(ps[:, 0, k * P:(k + 1) * P], 1, HC),
                                                w["bdmask"][:, :, 0:1].to_broadcast([P, HC, P]),
                                                ALU.mult).then_inc(e["kbd_ready"], 1)
                    for n in range(4):
                        v.wait_ge(e["s_full"], n + 1)
                        nc.vector.scalar_tensor_tensor(sm[:, 4 * n:4 * n + 4, :],
                                                       ps[:, 4 + n, :].rearrange("p (h k) -> p h k", k=P), SCALE,
                                                       spread(w["mask_f32"][:, :], 1, 4), ALU.mult, ALU.add)
                    nc.vector.drain()
                    nc.vector.reduce_max(smx[:, :], sm[:, :, :], AX.X)
                    nc.vector.drain()
                    nc.vector.tensor_tensor(sm[:, :, :], sm[:, :, :], spread(smx[:, :], 2, P),
                                            ALU.subtract).then_inc(e["s_less"], 1)
                    v.wait_ge(e["exp_ready"], 1)
                    nc.vector.reduce_sum(ssum[:, :], sm[:, :, :], AX.X)
                    nc.vector.drain()
                    nc.vector.reciprocal(ssum[:, :], ssum[:, :])
                    for n in (1, 3):
                        v.wait_ge(e["pt_full"], n + 1)
                        nc.vector.tensor_copy(pt[:, 4 * n:4 * n + 4, :],
                                              ps[:, n, :].rearrange("p (h k) -> p h k", k=P)).then_inc(e["pt_ready_v"], 1)
                    v.wait_ge(e["o_full"], 1)
                    nc.vector.tensor_tensor(o[:, :, :], ps[:, 4, 0:C].rearrange("p (h d) -> p h d", d=D),
                                            spread(ssum[:, :], 2, D), ALU.mult).then_inc(e["o_ready"], 1)
                    v.wait_ge(e["xa_full"], 1)
                    nc.vector.tensor_tensor(xa[:, :], ps[:, 6, 0:C], xs[:, :], ALU.add)
                    nc.vector.drain()
                    nc.vector.scalar_tensor_tensor(junk[:, :], xa[:, :], 1.0, xa[:, :], ALU.mult, ALU.mult,
                                                   accum_out=ss[:, 1:2]).then_inc(e["xs_ss"], 1)
                    v.wait_ge(e["rms_ready"], 2)
                    nc.vector.scalar_tensor_tensor(hn[:, :], xa[:, :], srs[:, 1:2], w["g2"][:, :],
                                                   ALU.mult, ALU.mult).then_inc(e["hn_ready"], 1)
                    v.wait_ge(e["silu_ready"], 2)
                    v.wait_ge(e["up_full"], 1)
                    nc.vector.tensor_tensor(gate[:, 0:4, :], gate[:, 0:4, :],
                                            ps[:, 2, :].rearrange("p (f t) -> p f t", t=P), ALU.mult)
                    nc.vector.tensor_tensor(gate[:, 4:FT, :], gate[:, 4:FT, :],
                                            ps[:, 3, 0:(FT - 4) * P].rearrange("p (f t) -> p f t", t=P),
                                            ALU.mult).then_inc(e["gate_ready"], 1)
                    v.wait_ge(e["ff_full"], 1)
                    nc.vector.tensor_tensor(delta[:, :], ps[:, 4, 0:C], xa[:, :], ALU.add)
                    nc.vector.drain()
                    nc.vector.tensor_tensor(delta[:, :], delta[:, :], xs[:, :], ALU.subtract).then_inc(e["delta_ready"], 1)
                    for j in range(NT):
                        v.wait_ge(e["put_full"], j + 1)
                        nc.vector.tensor_tensor(xn[:, j, :], xn[:, j, :], ps[:, 5 + j % 2, 0:C],
                                                ALU.add).then_inc(e["put_ready"], 1)
                        nc.vector.drain()
                        last = layer_stats(nc, stats, mv, xn[:, j, :], j)
                    last.then_inc(e["a_stat"], 1)
                    v.wait_ge(e["a_rstd"], 1)
                    for j in range(NT):
                        nc.vector.tensor_scalar(xn[:, j, :], xn[:, j, :], mv[:, j, 0:1], rstd[:, j:j + 1],
                                                ALU.subtract, ALU.mult).then_inc(e["a_norm"], 1)
                    nc.vector.drain()
                    for j in range(NT):
                        v.wait_ge(e["x2_ready"], j + 1)
                        last = layer_stats(nc, stats, mv, x[:, j, :], j)
                    last.then_inc(e["x2_stat"], 1)
                    v.wait_ge(e["x2_rstd"], 1)
                    for j in range(NT):
                        nc.vector.tensor_scalar(xn[:, j, :], x[:, j, :], mv[:, j, 0:1], rstd[:, j:j + 1],
                                                ALU.subtract, ALU.mult).then_inc(e["xn2_ready"], 1)
                    v.wait_ge(e["xst_full"], 1)
                    nc.vector.tensor_copy(xst[:, :, :], ps[:, 4, 0:KC * S].rearrange("p (k s) -> p k s", s=S))\
                        .then_inc(e["xst_ready"], 1)
                    v.wait_ge(e["ks_full"], 1)
                    for k in range(KC):
                        nc.vector.tensor_scalar(ks[:, k, 0:S], ps[:, 5, k * S:(k + 1) * S], w["ps_bk"][:, k:k + 1], None,
                                                ALU.add)
                    nc.vector.drain()
                    nc.vector.reduce_sum(ks[:, :, S:S1], ks[:, :, 0:S], AX.X)
                    nc.vector.drain()
                    nc.vector.tensor_scalar(ks[:, :, S:S1], ks[:, :, S:S1], 1.0 / S, None, ALU.mult)
                    nc.vector.drain()
                    for k in range(KC):
                        nc.vector.tensor_tensor(ksbd[:, k, :, :], spread(ks[:, k, :], 1, HC), w["bdmask"][:, :, :],
                                                ALU.mult).then_inc(e["ksbd_ready"], 1)
                    for j in range(NT):
                        v.wait_ge(e["q_full"], j + 1)
                        nc.vector.tensor_tensor(q[:, j, :], ps[:, 6 + j % 2, 0:C], w["ps_bq"][:, :],
                                                ALU.add).then_inc(e["q_ready"], 1)
                    for j in range(NT):
                        v.wait_ge(e["ms_full"], j + 1)
                        two = ps[:, 2 * (j % 2):2 * (j % 2) + 2, 0:HC * S1].rearrange("p k (h s) -> p k h s", s=S1)
                        nc.vector.reduce_max(mm[:, j, :, :], two[:, :, :, 0:S], AX.X)
                        nc.vector.drain()
                        nc.vector.tensor_tensor(mm[:, j, :, :], mm[:, j, :, :], two[:, :, :, S],
                                                ALU.subtract).then_inc(e["ms_ready"], 1)
                    nc.vector.drain()
                    nc.vector.tensor_copy(w["measure"][:, :, bass.ds(b * H, H)],
                                          mm[:, :, :, :].rearrange("p j k h -> p j (k h)"))

                @block.tensor
                def _(pe):
                    pe.wait_ge(e["xn_in"], 16)
                    for j in range(NT):
                        pe.wait_ge(e["oh_ready"], j + 1)
                        last = nc.tensor.matmul(ps[:, 0, 0:C], oh[:, j, :], xn[:, j, :],
                                                start=(j == 0), stop=(j == NT - 1))
                    last.then_inc(e["xs_full"], 1)

                    def turn(src, bank, full):
                        for k in range(KC):
                            last = nc.tensor.transpose(ps[:, bank, k * P:(k + 1) * P], src[:, k * P:(k + 1) * P],
                                                       w["ident"][:, :])
                        last.then_inc(full, 1)

                    pe.wait_ge(e["hn_ready"], 1)
                    turn(hn, 1, e["hnt_full"])
                    pe.wait_ge(e["hnt_ready"], 1)
                    for cc in range(2 * KC):
                        for k in range(KC):
                            last = nc.tensor.matmul(ps[:, 2 - cc // KC * 2, cc % KC * P:(cc % KC + 1) * P],
                                                    w["mod_wqkv"][:, k, cc * P:(cc + 1) * P], hnt[:, k, :],
                                                    start=(k == 0), stop=(k == KC - 1))
                    last.then_inc(e["qk_full"], 1)
                    for k in range(KC):
                        last = nc.tensor.matmul(ps[:, 3, 0:C], hnt[:, k, :], w["mod_wqkv"][:, k, 2 * C:3 * C],
                                                start=(k == 0), stop=(k == KC - 1))
                    last.then_inc(e["v_full"], 1)
                    pe.wait_ge(e["qt_ready"], 1)
                    for n in range(4):
                        k, half = divmod(n, 2)
                        pe.wait_ge(e["kbd_ready"], k + 1)
                        nc.tensor.matmul(ps[:, 4 + n, :], qt[:, k, :],
                                         kbd[:, k, 4 * half:4 * half + 4, :].rearrange("p h t -> p (h t)"),
                                         start=True, stop=True).then_inc(e["s_full"], 1)
                    pe.wait_ge(e["exp_ready"], 1)
                    pe.wait_ge(e["vv_ready"], 1)
                    for n in range(4):
                        for t in range(4):
                            last = nc.tensor.transpose(ps[:, n, t * P:(t + 1) * P], sm[:, 4 * n + t, :], w["ident"][:, :])
                        last.then_inc(e["pt_full"], 1)
                    pe.wait_ge(e["pt_ready"], 2)
                    pe.wait_ge(e["pt_ready_v"], 2)
                    for h in range(H):
                        last = nc.tensor.matmul(ps[:, 4, h * D:(h + 1) * D], pt[:, h, :], vv[:, h * D:(h + 1) * D],
                                                start=True, stop=True)
                    last.then_inc(e["o_full"], 1)
                    pe.wait_ge(e["o_ready"], 1)
                    turn(o[:, :, :].rearrange("p h d -> p (h d)"), 5, e["ot_full"])
                    pe.wait_ge(e["ot_ready"], 1)
                    for k in range(KC):
                        last = nc.tensor.matmul(ps[:, 6, 0:C], ot[:, k, :], w["mod_wout"][:, k, :],
                                                start=(k == 0), stop=(k == KC - 1))
                    last.then_inc(e["xa_full"], 1)
                    pe.wait_ge(e["hn_ready"], 2)
                    turn(hn, 7, e["hnt_full"])
                    pe.wait_ge(e["hnt_ready"], 2)
                    for wt, bank0, full in ((w["mod_w1"], 0, e["gate_full"]), (w["mod_w2"], 2, e["up_full"])):
                        for f in range(FT):
                            for k in range(KC):
                                last = nc.tensor.matmul(ps[:, bank0 + f // 4, (f % 4) * P:(f % 4 + 1) * P],
                                                        wt[:, k, f * P:(f + 1) * P], hnt[:, k, :],
                                                        start=(k == 0), stop=(k == KC - 1))
                        last.then_inc(full, 1)
                    pe.wait_ge(e["gate_ready"], 1)
                    for f in range(FT):
                        last = nc.tensor.matmul(ps[:, 4, 0:C], gate[:, f, :], w["mod_w3"][:, f, :],
                                                start=(f == 0), stop=(f == FT - 1))
                    last.then_inc(e["ff_full"], 1)
                    pe.wait_ge(e["delta_ready"], 1)
                    pe.wait_ge(e["oht_ready"], 1)
                    for j in range(NT):
                        if j >= 2:
                            pe.wait_ge(e["put_ready"], j - 1)
                        nc.tensor.matmul(ps[:, 5 + j % 2, 0:C], oht[:, j * P:(j + 1) * P], delta[:, :],
                                         start=True, stop=True).then_inc(e["put_full"], 1)
                    for n in range(NHALF):
                        pe.wait_ge(e["xn2_ready"], 4 * (n + 1))
                        for k in range(KC):
                            for t in range(4):
                                last = nc.tensor.transpose(ps[:, 2 * n + k, t * P:(t + 1) * P],
                                                           xn[:, 4 * n + t, k * P:(k + 1) * P], w["ident"][:, :])
                            last.then_inc(e["xnt_full"], 1)
                    for k in range(KC):
                        for j in range(NT):
                            last = nc.tensor.matmul(ps[:, 4, k * S:(k + 1) * S], xn[:, j, k * P:(k + 1) * P],
                                                    w["onehot_s"][:, j, :], start=(j == 0), stop=(j == NT - 1))
                    last.then_inc(e["xst_full"], 1)
                    pe.wait_ge(e["xst_ready"], 1)
                    for cc in range(KC):
                        for k in range(KC):
                            last = nc.tensor.matmul(ps[:, 5, cc * S:(cc + 1) * S], w["ps_wk"][:, k, cc * P:(cc + 1) * P],
                                                    xst[:, k, :], start=(k == 0), stop=(k == KC - 1))
                    last.then_inc(e["ks_full"], 1)
                    pe.wait_ge(e["xnt_ready"], NHALF * KC)
                    for j in range(NT):
                        if j >= 2:
                            pe.wait_ge(e["q_ready"], j - 1)
                        for k in range(KC):
                            last = nc.tensor.matmul(ps[:, 6 + j % 2, 0:C], xnt[:, k, j * P:(j + 1) * P],
                                                    w["ps_wq"][:, k, :], start=(k == 0), stop=(k == KC - 1))
                        last.then_inc(e["q_full"], 1)
                    for n in range(NHALF):
                        pe.wait_ge(e["q_ready"], 4 * (n + 1))
                        for k in range(KC):
                            for t in range(4):
                                last = nc.tensor.transpose(ps[:, 4 + 2 * n + k, t * P:(t + 1) * P],
                                                           q[:, 4 * n + t, k * P:(k + 1) * P], w["ident"][:, :])
                            last.then_inc(e["qtt_full"], 1)
                    pe.wait_ge(e["ksbd_ready"], KC)
                    for j in range(NT):
                        if j % 4 == 0:
                            pe.wait_ge(e["qtt_ready"], KC * (j // 4 + 1))
                        if j >= 2:
                            pe.wait_ge(e["ms_ready"], j - 1)
                        for k in range(KC):
                            last = nc.tensor.matmul(ps[:, 2 * (j % 2) + k, 0:HC * S1], qtt[:, k, j * P:(j + 1) * P],
                                                    ksbd[:, k, :, :].rearrange("p h s -> p (h s)"), start=True, stop=True)
                        last.then_inc(e["ms_full"], 1)

                @block.scalar
                def _(a):
                    def out_of(bank, dst, full, count, ready):
                        a.wait_ge(full, count)
                        nc.scalar.copy(dst, ps[:, bank, 0:C].rearrange("p (k t) -> p k t", k=KC)).then_inc(ready, 1)

                    out_of(1, hnt[:, :, :], e["hnt_full"], 1, e["hnt_ready"])
                    out_of(2, qt[:, :, :], e["qk_full"], 1, e["qt_ready"])
                    a.wait_ge(e["v_full"], 1)
                    nc.scalar.copy(vv[:, :], ps[:, 3, 0:C]).then_inc(e["vv_ready"], 1)
                    a.wait_ge(e["s_less"], 1)
                    nc.scalar.activation(sm[:, :, :], sm[:, :, :], ACT.Exp).then_inc(e["exp_ready"], 1)
                    for n in (0, 2):
                        a.wait_ge(e["pt_full"], n + 1)
                        nc.scalar.copy(pt[:, 4 * n:4 * n + 4, :],
                                       ps[:, n, :].rearrange("p (h k) -> p h k", k=P)).then_inc(e["pt_ready"], 1)
                    out_of(5, ot[:, :, :], e["ot_full"], 1, e["ot_ready"])
                    out_of(7, hnt[:, :, :], e["hnt_full"], 2, e["hnt_ready"])
                    a.wait_ge(e["gate_full"], 1)
                    nc.scalar.activation(gate[:, 0:4, :], ps[:, 0, :].rearrange("p (f t) -> p f t", t=P),
                                         ACT.Silu).then_inc(e["silu_ready"], 1)
                    nc.scalar.activation(gate[:, 4:FT, :], ps[:, 1, 0:(FT - 4) * P].rearrange("p (f t) -> p f t", t=P),
                                         ACT.Silu).then_inc(e["silu_ready"], 1)
                    for n in range(NHALF):
                        for k in range(KC):
                            a.wait_ge(e["xnt_full"], KC * n + k + 1)
                            nc.scalar.copy(xnt[:, k, n * BANK:(n + 1) * BANK],
                                           ps[:, 2 * n + k, :]).then_inc(e["xnt_ready"], 1)
                    for n in range(NHALF):
                        for k in range(KC):
                            a.wait_ge(e["qtt_full"], KC * n + k + 1)
                            nc.scalar.copy(qtt[:, k, n * BANK:(n + 1) * BANK],
                                           ps[:, 4 + 2 * n + k, :]).then_inc(e["qtt_ready"], 1)
            m.clear()


def top_queries(nc, io, w, ps):
    with Memory(nc) as m:
        full = m.sem("d_full")
        ready = m.sem("d_ready")
        stored = m.sem("d_stored")
        ms = m.sb("ms", [P, T])
        top = m.sb("dtop", [P, 8 * ROUNDS_E])
        idx = m.sb("didx", [P, 8 * ROUNDS_E], U32)
        idxf = m.sb("didxf", [P, 8 * ROUNDS_E])
        with nc.Block() as block:
            @block.tensor
            def _(pe):
                for j in range(NT):
                    nc.tensor.transpose(ps[:, j // 4, (j % 4) * P:(j % 4 + 1) * P], w["measure"][:, j, :],
                                        w["ident"][:, :]).then_inc(full, 1)

            @block.vector
            def _(v):
                for n in range(NHALF):
                    v.wait_ge(full, 4 * (n + 1))
                    nc.vector.tensor_copy(ms[:, n * BANK:(n + 1) * BANK], ps[:, n, :])
                nc.vector.drain()
                for n in range(ROUNDS_E):
                    t8 = slice(8 * n, 8 * n + 8)
                    nc.vector.max(top[:, t8], ms[:, :])
                    nc.vector.drain()
                    nc.vector.max_index(idx[:, t8], top[:, t8], ms[:, :])
                    nc.vector.drain()
                    if n < ROUNDS_E - 1:
                        nc.vector.match_replace(ms[:, :], top[:, t8], ms[:, :], -3e38)
                        nc.vector.drain()
                nc.vector.tensor_copy(idxf[:, :], idx[:, :]).then_inc(ready, 1)

            @block.sync
            def _(sp):
                sp.wait_ge(ready, 1)
                sp.dma_start(io["top_queries"].rearrange("b (h u) -> (b h) u", u=S), idxf[:, 0:S]).then_inc(stored, 16)
                sp.wait_ge(stored, 16)
        m.clear()



def chunks_of(mt):
    half = HU // KC
    return [k for k in range(KC) if mt * MR < (k + 1) * half and (mt + 1) * MR > k * half]


def prob_loop(nc, io, w, ps):
    HALF = HU // KC
    with Memory(nc) as m:
        x = m.sb("ex", [P, NT, C])
        xn = m.sb("exn", [P, NT, C])
        q = m.sb("eq", [P, NT, C])
        idxb = m.sb("eidxb", [P, HU])
        idxc = m.sb("eidxc", [MR, MT])
        oh = m.sb("eoh", [P, NT, HU])
        oht = m.sb("eoht", [MR, MT, T])
        xnt = m.sb("exnt", [P, KC, T])
        kt = m.sb("ekt", [P, KC, T])
        vv = m.sb("evv", [P, NT, C])
        qbd = m.sb("qbd", [P, KC, HU])
        obd = m.sb("obd", [P, KC, HU])
        nmx = m.sb("nmx", [MR, MT])
        nb = m.sb("nb", [MR, MT])
        sums = m.sb("sums", [MR, MT])
        dg = m.sb("dg", [MR, MT, MR])
        pr = m.sb("pr", [MR, MT, T])
        pt = m.sb("ept", [P, NT, HU])
        vm = m.sb("vm", [P, KC])
        vmr = m.sb("vmr", [P, KC, P])
        mean1 = m.sb("mean1", [P, 1])
        gg = m.sb("gg", [MR, MT, C])
        base = m.sb("base", [P, C])
        stats = m.sb("estats", [P, NT, 6])
        mv = m.sb("emv", [P, NT, 2])
        vtmp = m.sb("evtmp", [P, NT])
        rstd = m.sb("erstd", [P, NT])
        att = q
        hh = kt[:, :, :].rearrange("p k (j c) -> p (k j) c", c=C)
        hn = vv
        ht = xnt
        yb = oh[:, 0:NT, 0:BANK]

        names = """x_in xn_in q_in idx_in oh_ready oht_ready xnt_full xnt_ready qb_full qbd_ready kt_full kt_ready
            v_full v_ready s_full nb_ready exp_ready dg_ready pt_full pt_ready_a pt_ready_v vm_full vmr_ready ot_full
            obd_ready g_full g_ready base_full base_ready ctx_full ctx_ready a_stat a_rstd a_norm x3_ready x3_stat
            x3_rstd hh_ready hh_stat hh_rstd hn_ready hb_ready ht_full ht_ready f1_full y_ready f2_full r_ready r_stat
            r_rstd r_norm out_ready stored pool_step""".split()
        e = {n: m.sem("e_" + n) for n in names}

        with nc.Block() as block:
            @block.vector
            def _(v):
                nc.vector.memset(qbd[:, :, :], 0.0)
                nc.vector.memset(obd[:, :, :], 0.0)
                nc.vector.memset(mean1[:, :], 1.0 / T)
        m.clear()

        with nc.Fori(0, B) as b:
            with nc.Block() as block:
                @block.sync
                def _(sp):
                    def rows(name):
                        return io[name][b].rearrange("(j p) c -> p j c", p=P)

                    sp.dma_start(xn[:, :, :], rows("xn2")).then_inc(e["xn_in"], 16)
                    sp.dma_start(idxb[:, :], over_partitions(io["top_queries"][b, :])).then_inc(e["idx_in"], 16)
                    with nc.allow_non_contiguous_dma(reason="560 indices as columns"):
                        sp.dma_start(idxc[:, :], io["top_queries"][b, :].rearrange("(m r) -> r m", r=MR))\
                            .then_inc(e["idx_in"], 16)
                    sp.dma_start(q[:, :, :], rows("q")).then_inc(e["q_in"], 16)
                    sp.dma_start(x[:, :, :], rows("x2")).then_inc(e["x_in"], 16)
                    for n in range(2):
                        sp.wait_ge(e["out_ready"], 4 * (n + 1))
                        sp.dma_start(io["out"][b, n * BANK:(n + 1) * BANK, :].rearrange("(j p) c -> p j c", p=P),
                                     x[:, 4 * n:4 * n + 4, :]).then_inc(e["stored"], 16)
                    sp.wait_ge(e["stored"], 32)

                @block.gpsimd
                def _(g):
                    def rstd_step(stat, n, done):
                        g.wait_ge(e[stat], 1)
                        rstd_of(nc, mv[:, :, 1], rstd[:, :], w, NT, EPS_LN, e["pool_step"], vtmp[:, :], n)\
                            .then_inc(e[done], 1)

                    rstd_step("a_stat", 1, "a_rstd")
                    g.wait_ge(e["x_in"], 16)
                    for j in range(NT):
                        g.wait_ge(e["a_norm"], j + 1)
                        nc.gpsimd.tensor_tensor(x[:, j, :], x[:, j, :], att[:, j, :], ALU.add)\
                            .then_inc(e["x3_ready"], 1)
                    rstd_step("x3_stat", 2, "x3_rstd")
                    rstd_step("hh_stat", 3, "hh_rstd")
                    for j in range(NT):
                        g.wait_ge(e["hn_ready"], j + 1)
                        nc.gpsimd.tensor_tensor(hh[:, j, :], hh[:, j, :], w["fc2_b"][:, :], ALU.add)\
                            .then_inc(e["hb_ready"], 1)
                    rstd_step("r_stat", 4, "r_rstd")
                    for j in range(NT):
                        g.wait_ge(e["r_norm"], j + 1)
                        nc.gpsimd.tensor_tensor(x[:, j, :], x[:, j, :], att[:, j, :], ALU.add)\
                            .then_inc(e["out_ready"], 1)

                @block.vector
                def _(v):
                    v.wait_ge(e["idx_in"], 32)
                    for j in range(NT):
                        nc.vector.tensor_scalar(oh[:, j, :], idxb[:, :], w["iota_col"][:, j:j + 1], None,
                                                ALU.is_equal).then_inc(e["oh_ready"], 1)
                    for k in range(KC):
                        v.wait_ge(e["qb_full"], k + 1)
                        nc.vector.tensor_tensor(qbd[:, k, k * HALF:(k + 1) * HALF].rearrange("p (h u) -> p h u", u=S),
                                                ps[:, 4 + k, 0:HALF].rearrange("p (h u) -> p h u", u=S),
                                                w["bdmask"][:, :, 0:S], ALU.mult).then_inc(e["qbd_ready"], 1)
                    for j in range(NT):
                        v.wait_ge(e["v_full"], j + 1)
                        nc.vector.tensor_tensor(vv[:, j, :], ps[:, 4 + j % 2, 0:C], w["ps_bv"][:, :],
                                                ALU.add).then_inc(e["v_ready"], 1)
                    for mt in range(MT):
                        v.wait_ge(e["s_full"], mt + 1)
                        b0 = 2 * (mt % 2)
                        nc.vector.tensor_reduce(nmx[:, mt:mt + 1], ps[0:MR, b0:b0 + 2, :], AX.XY, ALU.max, negate=True)
                        nc.vector.drain()
                        nc.vector.tensor_scalar(nb[:, mt:mt + 1], nmx[:, mt:mt + 1], SCALE, None,
                                                ALU.mult).then_inc(e["nb_ready"], 1)
                        if mt == 1:
                            v.wait_ge(e["vm_full"], 1)
                            nc.vector.tensor_copy(vm[:, :], ps[:, 6, 0:KC])
                            nc.vector.drain()
                            for k in range(KC):
                                last = nc.vector.tensor_copy(vmr[:, k, :], vm[:, k:k + 1].to_broadcast([P, P]))
                            last.then_inc(e["vmr_ready"], 1)
                        if mt >= 1:
                            diagonal(nc, v, e, dg, sums, w, mt - 1)
                        if mt >= 2:
                            take_pt(nc, v, e, pt, ps, mt - 2, 1)
                    diagonal(nc, v, e, dg, sums, w, MT - 1)
                    take_pt(nc, v, e, pt, ps, MT - 2, 1)
                    take_pt(nc, v, e, pt, ps, MT - 1, 1)
                    v.wait_ge(e["base_full"], 1)
                    nc.vector.tensor_tensor(base[:, :], ps[:, 2, 0:C], w["ps_bo"][:, :], ALU.add)\
                        .then_inc(e["base_ready"], 1)
                    for k in range(KC):
                        v.wait_ge(e["ot_full"], k + 1)
                        nc.vector.scalar_tensor_tensor(
                            obd[:, k, k * HALF:(k + 1) * HALF].rearrange("p (h u) -> p h u", u=S),
                            ps[:, k, 0:HALF].rearrange("p (h u) -> p h u", u=S), vm[:, k:k + 1],
                            w["bdmask"][:, :, 0:S], ALU.subtract, ALU.mult).then_inc(e["obd_ready"], 1)
                    for mt in range(MT):
                        nc.vector.tensor_scalar(oht[:, mt, :], w["iota_row"][0:MR, :], idxc[:, mt:mt + 1], None,
                                                ALU.is_equal).then_inc(e["oht_ready"], 1)
                    for j in range(NT):
                        v.wait_ge(e["ctx_full"], j + 1)
                        nc.vector.tensor_tensor(att[:, j, :], ps[:, 6 + j % 2, 0:C], base[:, :],
                                                ALU.add).then_inc(e["ctx_ready"], 1)
                        nc.vector.drain()
                        last = layer_stats(nc, stats, mv, att[:, j, :], j)
                    last.then_inc(e["a_stat"], 1)

                    def normalise(dst, src, rstd_sem, ready):
                        v.wait_ge(e[rstd_sem], 1)
                        for j in range(NT):
                            nc.vector.tensor_scalar(dst[:, j, :], src[:, j, :], mv[:, j, 0:1], rstd[:, j:j + 1],
                                                    ALU.subtract, ALU.mult).then_inc(e[ready], 1)
                        nc.vector.drain()

                    def stats_of(src, done, ready=None):
                        for j in range(NT):
                            if ready:
                                v.wait_ge(e[ready], j + 1)
                            last = layer_stats(nc, stats, mv, src[:, j, :], j)
                        last.then_inc(e[done], 1)

                    normalise(att, att, "a_rstd", "a_norm")
                    stats_of(x, "x3_stat", "x3_ready")
                    normalise(hh, x, "x3_rstd", "hh_ready")
                    stats_of(hh, "hh_stat")
                    normalise(hn, hh, "hh_rstd", "hn_ready")
                    for j in range(NT):
                        v.wait_ge(e["f2_full"], j + 1)
                        v.wait_ge(e["hb_ready"], j + 1)
                        nc.vector.tensor_tensor(att[:, j, :], ps[:, 4 + j % 2, 0:C], hh[:, j, :],
                                                ALU.add).then_inc(e["r_ready"], 1)
                        nc.vector.drain()
                        last = layer_stats(nc, stats, mv, att[:, j, :], j)
                    last.then_inc(e["r_stat"], 1)
                    normalise(att, att, "r_rstd", "r_norm")

                @block.tensor
                def _(pe):
                    def turn(src, ready, full):
                        for n in range(NHALF):
                            pe.wait_ge(e[ready], 4 * (n + 1) if ready != "xn_in" else 16)
                            for k in range(KC):
                                for t in range(4):
                                    last = nc.tensor.transpose(ps[:, 2 * n + k, t * P:(t + 1) * P],
                                                               src[:, 4 * n + t, k * P:(k + 1) * P], w["ident"][:, :])
                                last.then_inc(e[full], 1)

                    turn(xn, "xn_in", "xnt_full")
                    pe.wait_ge(e["q_in"], 16)
                    for k in range(KC):
                        for j in range(NT):
                            if k == 0:
                                pe.wait_ge(e["oh_ready"], j + 1)
                            last = nc.tensor.matmul(ps[:, 4 + k, 0:HALF], q[:, j, k * P:(k + 1) * P],
                                                    oh[:, j, k * HALF:(k + 1) * HALF], start=(j == 0), stop=(j == NT - 1))
                        last.then_inc(e["qb_full"], 1)
                    pe.wait_ge(e["xnt_ready"], NHALF * KC)
                    u = 0
                    for cc in range(KC):
                        for n in range(NHALF):
                            if u >= 2:
                                pe.wait_ge(e["kt_ready"], u - 1)
                            for k in range(KC):
                                last = nc.tensor.matmul(ps[:, 6 + u % 2, :], w["ps_wk"][:, k, cc * P:(cc + 1) * P],
                                                        xnt[:, k, n * BANK:(n + 1) * BANK],
                                                        start=(k == 0), stop=(k == KC - 1))
                            last.then_inc(e["kt_full"], 1)
                            u += 1
                    pe.wait_ge(e["qbd_ready"], KC)
                    for j in range(NT):
                        if j >= 2:
                            pe.wait_ge(e["v_ready"], j - 1)
                        for k in range(KC):
                            last = nc.tensor.matmul(ps[:, 4 + j % 2, 0:C], xnt[:, k, j * P:(j + 1) * P],
                                                    w["ps_wv"][:, k, :], start=(k == 0), stop=(k == KC - 1))
                        last.then_inc(e["v_full"], 1)
                    pe.wait_ge(e["kt_ready"], KC * NHALF)

                    def scores(mt):
                        if mt >= 2:
                            pe.wait_ge(e["exp_ready"], mt - 1)
                        for n in range(NHALF):
                            cs = chunks_of(mt)
                            for k in cs:
                                last = nc.tensor.matmul(ps[0:MR, 2 * (mt % 2) + n, :], qbd[:, k, mt * MR:(mt + 1) * MR],
                                                        kt[:, k, n * BANK:(n + 1) * BANK],
                                                        start=(k == cs[0]), stop=(k == cs[-1]))
                        last.then_inc(e["s_full"], 1)

                    def probs_t(mt):
                        pe.wait_ge(e["dg_ready"], mt + 1)
                        if mt >= 1:
                            pe.wait_ge(e["pt_ready_a"], mt)
                            pe.wait_ge(e["pt_ready_v"], mt)
                        for j in range(NT):
                            last = nc.tensor.matmul(ps[:, 4 + j // 4, (j % 4) * MR:(j % 4 + 1) * MR],
                                                    pr[:, mt, j * P:(j + 1) * P], dg[:, mt, :], start=True, stop=True)
                            if j % 4 == 3:
                                last.then_inc(e["pt_full"], 1)

                    scores(0)
                    scores(1)
                    pe.wait_ge(e["v_ready"], NT)
                    for k in range(KC):
                        for j in range(NT):
                            last = nc.tensor.matmul(ps[:, 6, k:k + 1], vv[:, j, k * P:(k + 1) * P], mean1[:, :],
                                                    start=(j == 0), stop=(j == NT - 1))
                    last.then_inc(e["vm_full"], 1)
                    for mt in range(MT):
                        if mt + 2 < MT:
                            scores(mt + 2)
                        probs_t(mt)
                    pe.wait_ge(e["exp_ready"], MT)
                    pe.wait_ge(e["vmr_ready"], 1)
                    for k in range(KC):
                        last = nc.tensor.matmul(ps[:, 2, 0:C], vmr[:, k, :], w["ps_wo"][:, k, :],
                                                start=(k == 0), stop=(k == KC - 1))
                    last.then_inc(e["base_full"], 1)
                    pe.wait_ge(e["pt_ready_a"], MT)
                    pe.wait_ge(e["pt_ready_v"], MT)
                    for k in range(KC):
                        for j in range(NT):
                            last = nc.tensor.matmul(ps[:, k, 0:HALF], vv[:, j, k * P:(k + 1) * P],
                                                    pt[:, j, k * HALF:(k + 1) * HALF], start=(j == 0), stop=(j == NT - 1))
                        last.then_inc(e["ot_full"], 1)
                    pe.wait_ge(e["obd_ready"], KC)
                    for mt in range(MT):
                        if mt >= 2:
                            pe.wait_ge(e["g_ready"], mt - 1)
                        cs = chunks_of(mt)
                        for k in cs:
                            last = nc.tensor.matmul(ps[0:MR, 4 + mt % 2, 0:C], obd[:, k, mt * MR:(mt + 1) * MR],
                                                    w["ps_wo"][:, k, :], start=(k == cs[0]), stop=(k == cs[-1]))
                        last.then_inc(e["g_full"], 1)
                    pe.wait_ge(e["g_ready"], MT)
                    pe.wait_ge(e["oht_ready"], MT)
                    pe.wait_ge(e["base_ready"], 1)
                    for j in range(NT):
                        if j >= 2:
                            pe.wait_ge(e["ctx_ready"], j - 1)
                        for mt in range(MT):
                            last = nc.tensor.matmul(ps[:, 6 + j % 2, 0:C], oht[:, mt, j * P:(j + 1) * P], gg[:, mt, :],
                                                    start=(mt == 0), stop=(mt == MT - 1))
                        last.then_inc(e["ctx_full"], 1)
                    turn(hn, "hn_ready", "ht_full")
                    pe.wait_ge(e["ht_ready"], NHALF * KC)
                    for n in range(NHALF):
                        for f in range(F2T):
                            u = n * F2T + f
                            if u >= 4:
                                pe.wait_ge(e["y_ready"], u - 3)
                            for k in range(KC):
                                last = nc.tensor.matmul(ps[:, u % 4, :], w["fc1"][:, k, f * P:(f + 1) * P],
                                                        ht[:, k, n * BANK:(n + 1) * BANK],
                                                        start=(k == 0), stop=(k == KC - 1))
                            last.then_inc(e["f1_full"], 1)
                        for t in range(4):
                            j = 4 * n + t
                            pe.wait_ge(e["y_ready"], F2T * (n + 1))
                            if j >= 2:
                                pe.wait_ge(e["r_ready"], j - 1)
                            for f in range(F2T):
                                last = nc.tensor.matmul(ps[:, 4 + j % 2, 0:C], yb[:, f, t * P:(t + 1) * P],
                                                        w["fc2"][:, f, :], start=(f == 0), stop=(f == F2T - 1))
                            last.then_inc(e["f2_full"], 1)

                @block.scalar
                def _(a):
                    for n in range(NHALF):
                        for k in range(KC):
                            a.wait_ge(e["xnt_full"], KC * n + k + 1)
                            nc.scalar.copy(xnt[:, k, n * BANK:(n + 1) * BANK],
                                           ps[:, 2 * n + k, :]).then_inc(e["xnt_ready"], 1)
                    u = 0
                    for cc in range(KC):
                        for n in range(NHALF):
                            a.wait_ge(e["kt_full"], u + 1)
                            nc.scalar.activation(kt[:, cc, n * BANK:(n + 1) * BANK], ps[:, 6 + u % 2, :], ACT.Identity,
                                                 bias=w["ps_bk"][:, cc:cc + 1]).then_inc(e["kt_ready"], 1)
                            u += 1
                    for mt in range(MT):
                        a.wait_ge(e["nb_ready"], mt + 1)
                        b0 = 2 * (mt % 2)
                        nc.scalar.activation(pr[:, mt, :].rearrange("p (n t) -> p n t", n=NHALF), ps[0:MR, b0:b0 + 2, :],
                                             ACT.Exp, bias=nb[:, mt:mt + 1], scale=SCALE,
                                             accum_out=sums[:, mt:mt + 1]).then_inc(e["exp_ready"], 1)
                        if mt >= 1:
                            take_pt(nc, a, e, pt, ps, mt - 1, 0)
                    take_pt(nc, a, e, pt, ps, MT - 1, 0)
                    for mt in range(MT):
                        a.wait_ge(e["g_full"], mt + 1)
                        nc.scalar.copy(gg[:, mt, :], ps[0:MR, 4 + mt % 2, 0:C]).then_inc(e["g_ready"], 1)
                    for n in range(NHALF):
                        for k in range(KC):
                            a.wait_ge(e["ht_full"], KC * n + k + 1)
                            nc.scalar.activation(ht[:, k, n * BANK:(n + 1) * BANK], ps[:, 2 * n + k, :], ACT.Identity,
                                                 scale=w["gamma"][:, k:k + 1],
                                                 bias=w["beta"][:, k:k + 1]).then_inc(e["ht_ready"], 1)
                    for n in range(NHALF):
                        for f in range(F2T):
                            u = n * F2T + f
                            a.wait_ge(e["f1_full"], u + 1)
                            if n:
                                a.wait_ge(e["f2_full"], 4 * n)
                            nc.scalar.activation(yb[:, f, :], ps[:, u % 4, :], ACT.Silu,
                                                 bias=w["fc1_b"][:, f:f + 1]).then_inc(e["y_ready"], 1)
            m.clear()


def diagonal(nc, v, e, dg, sums, w, mt):
    v.wait_ge(e["exp_ready"], mt + 1)
    nc.vector.reciprocal(sums[:, mt:mt + 1], sums[:, mt:mt + 1])
    nc.vector.drain()
    nc.vector.tensor_scalar(dg[:, mt, :], w["ident"][0:MR, 0:MR], sums[:, mt:mt + 1], None,
                            ALU.mult).then_inc(e["dg_ready"], 1)


def take_pt(nc, eng, e, pt, ps, mt, half):
    eng.wait_ge(e["pt_full"], 2 * mt + half + 1)
    src = ps[:, 4 + half, 0:4 * MR].rearrange("p (j r) -> p j r", r=MR)
    dst = pt[:, 4 * half:4 * half + 4, mt * MR:(mt + 1) * MR]
    if half:
        nc.vector.tensor_copy(dst, src).then_inc(e["pt_ready_v"], 1)
    else:
        nc.scalar.copy(dst, src).then_inc(e["pt_ready_a"], 1)


def build_program(nc, io):
    with Memory(nc) as m:
        ps = m.stack.enter_context(nc.psum_tensor("ps", [P, 8, BANK], F32))
        w = {name: m.sb("w_" + name, shape, dt) for name, (shape, dt) in TABLES.items()}
        with Memory(nc) as first:
            w |= {name: first.sb("w_" + name, shape, dt) for name, (shape, dt) in ATTENTION_WEIGHTS.items()}
            setup_attention(nc, io, w, ps)
            attention_loop(nc, io, w, ps)
        w |= {name: m.sb("w_" + name, shape, dt) for name, (shape, dt) in OTHER_WEIGHTS.items()}
        with Memory(nc) as second:
            w |= {name: second.sb("w_" + name, shape, dt) for name, (shape, dt) in MOD_WEIGHTS.items()}
            setup_rest_and_top_tokens(nc, io, w, ps)
            mod_loop(nc, io, w, ps)
            top_queries(nc, io, w, ps)
        prob_loop(nc, io, w, ps)


_INS = ['L0_attn_x', 'L0_attn_W_attn', 'L0_attn_b_attn', 'L0_attn_W_proj', 'L0_attn_b_proj', 'L0_ffn_w_router',
        'L0_ffn_W_qkv', 'L0_ffn_W_out', 'L0_ffn_g1', 'L0_ffn_g2', 'L0_ffn_W1', 'L0_ffn_W2', 'L0_ffn_W3',
        'L1_attn_Wq', 'L1_attn_bq', 'L1_attn_Wk', 'L1_attn_bk', 'L1_attn_Wv', 'L1_attn_bv', 'L1_attn_Wo', 'L1_attn_bo',
        'L1_attn_sample_idx', 'L1_ffn_ln_gamma', 'L1_ffn_ln_beta', 'L1_ffn_fc1_q', 'L1_ffn_fc1_scales',
        'L1_ffn_fc1_bias', 'L1_ffn_fc2_q', 'L1_ffn_fc2_scales', 'L1_ffn_fc2_bias']
_SCRATCH = {"parts": ((2 * KC, PARTS, P, T), BF16), "nm_parts": ((PARTS, SETS, HS * NT, P), BF16),
            "x1": ((B, T, C), F32), "xn1": ((B, T, C), F32),
            "scores": ((B * NT, P), F32), "top_tokens": ((B, CAP), F32),
            "x2": ((B, T, C), F32), "xn2": ((B, T, C), F32), "q": ((B, T, C), F32), "top_queries": ((B, HU), F32)}


def kernel(**inputs):
    import concourse.bacc as _bacc
    from concourse.bass_utils import run_bass_kernel_spmd as _run

    nc = _bacc.Bacc("TRN2", target_bir_lowering=False, num_devices=1)
    arrays = {name: np.ascontiguousarray(inputs[name]) for name in _INS}
    theta = (1.0 / 10000.0 ** (np.arange(0, D, 2, dtype=np.float32) / D)).astype(np.float32)
    angle = (np.arange(H, dtype=np.float32)[:, None] * theta[None, :]).astype(np.float32)
    arrays["rope_cos"] = np.cos(angle).astype(np.float32).reshape(-1)
    arrays["rope_sin"] = np.sin(angle).astype(np.float32).reshape(-1)
    io = {name: nc.dram_tensor("in_" + name, a.shape, mybir.dt.from_np(a.dtype), kind="ExternalInput").ap()
          for name, a in arrays.items()}
    io["x"] = io["L0_attn_x"]
    for name, (shape, dt) in _SCRATCH.items():
        io[name] = nc.dram_tensor("scratch_" + name, shape, dt, kind="Internal").ap()
    io["out"] = nc.dram_tensor("out_0_dram", (B, T, C), F32, kind="ExternalOutput").ap()
    build_program(nc, io)
    r = _run(nc, [{"in_" + k: v for k, v in arrays.items()}], core_ids=[0])
    return r.results[0]["out_0_dram"]
```

```python
import math
from contextlib import ExitStack

import numpy as np

import concourse.bass as bass
from concourse import mybir

F32 = mybir.dt.float32
BF16 = mybir.dt.bfloat16
I32 = mybir.dt.int32
U32 = mybir.dt.uint32
ALU = mybir.AluOpType
ACT = mybir.ActivationFunctionType
AX = mybir.AxisListType

P = 128
B, T, C = 8, 1024, 256
NT = T // P
KC = C // P
H = 16
D = C // H
HC = H // KC
BANK = 512
NHALF = T // BANK
SCALE = 1.0 / math.sqrt(D)
CAP = 128
DFF = 682
FT = -(-DFF // P)
S = 35
S1 = S + 1
HU = H * S
MT = 5
MR = HU // MT
F2 = 1024
F2T = F2 // P
EPS_LN = 1e-5
EPS_RMS = 1e-6
NEG = -1e30
ROUNDS_C = CAP // 8
ROUNDS_E = -(-S // 8)


class Memory:

    def __init__(self, nc):
        self.nc = nc
        self.stack = ExitStack()
        self.sems = []

    def __enter__(self):
        self.stack.__enter__()
        return self

    def __exit__(self, *e):
        return self.stack.__exit__(*e)

    def sb(self, name, shape, dt=F32):
        return self.stack.enter_context(self.nc.sbuf_tensor(name, shape, dt))

    def sem(self, name):
        s = self.stack.enter_context(self.nc.semaphore(name))
        self.sems.append(s)
        return s

    def clear(self):
        numbers = sorted(s.num for s in self.sems)
        first = numbers[0]
        for n, number in enumerate(numbers):
            if n + 1 == len(numbers) or numbers[n + 1] != number + 1:
                self.nc.sync.sem_clear(range(first, number + 1))
                first = numbers[n + 1] if n + 1 < len(numbers) else None
        self.nc.all_engine_barrier()


def spread(ap, axis, n):
    ap = ap.unsqueeze(axis)
    shape = list(ap.shape)
    shape[axis] = n
    return ap.to_broadcast(shape)


def over_partitions(row, n=P):
    return row.partition_broadcast(n)



def setup_attention(nc, io, w, ps):
    with Memory(nc) as m:
        loaded = m.sem("loaded")
        made = m.sem("made")
        zeroed = m.sem("zeroed")
        turned = m.sem("turned")
        cols = m.sem("cols")
        rows = m.sem("rows")

        wqkv_raw = m.sb("wqkv_raw", [P, KC, 3 * C])
        ropec = m.sb("ropec", [P, H * D // 2])
        ropes = m.sb("ropes", [P, H * D // 2])
        brow = m.sb("brow", [1, 2 * C])
        brot = m.sb("brot", [1, 2 * C])
        one = m.sb("one", [1, 1])
        t0 = m.sb("t0", [P, H * D // 2])
        t1 = m.sb("t1", [P, H * D // 2])
        bv = m.sb("bv0", [P, KC])
        bvrep = m.sb("bvrep", [P, KC, P])
        bproj = m.sb("bproj", [P, C])
        iota_i = m.sb("iota_i", [P, T], I32)
        iota_c = m.sb("iota_c", [P, NT], I32)
        ones = m.sb("ones", [P, P])

        loads = [(wqkv_raw[:, :, :], io["L0_attn_W_attn"].rearrange("(k p) n -> p k n", p=P)),
                 (ropec[:, :], over_partitions(io["rope_cos"])),
                 (ropes[:, :], over_partitions(io["rope_sin"])),
                 (brow[:, :], io["L0_attn_b_attn"][0:2 * C].rearrange("(a n) -> a n", a=1)),
                 (bv[:, :], io["L0_attn_b_attn"][2 * C:3 * C].rearrange("(k p) -> p k", p=P)),
                 (bproj[:, :], over_partitions(io["L0_attn_b_proj"])),
                 (w["wproj"][:, :, :], io["L0_attn_W_proj"].rearrange("(k p) n -> p k n", p=P)),
                 (w["router"][:, :], over_partitions(io["L0_ffn_w_router"]))]

        with nc.Block() as block:
            @block.sync
            def _(sp):
                with nc.allow_non_contiguous_dma(reason="a few columns of a bias"):
                    for dst, src in loads:
                        sp.dma_start(dst, src).then_inc(loaded, 16)

            @block.gpsimd
            def _(g):
                nc.gpsimd.memset(ones[:, :], 1.0).then_inc(made, 1)
                nc.gpsimd.memset(w["ident"][:, :], 0.0).then_inc(made, 1)
                nc.gpsimd.memset(w["bdmask"][:, :, :], 1.0).then_inc(made, 1)
                nc.gpsimd.memset(w["mhalf"][:, :], -0.5)
                nc.gpsimd.iota(iota_i[:, :], pattern=[[1, T]], base=0, channel_multiplier=0)
                nc.gpsimd.iota(iota_c[:, :], pattern=[[P, NT]], base=0, channel_multiplier=1)
                g.wait_ge(made, 3)
                nc.gpsimd.affine_select(out=w["ident"][:, :], in_=w["ident"][:, :], compare_op=ALU.not_equal,
                                        fill=1.0, base=0, pattern=[[-1, P]], channel_multiplier=1)
                nc.gpsimd.affine_select(out=w["bdmask"][:, :, :], in_=w["bdmask"][:, :, :], compare_op=ALU.is_ge,
                                        fill=0.0, base=0, pattern=[[-D, HC], [0, S1]],
                                        channel_multiplier=1).then_inc(made, 1)
                g.wait_ge(made, 4)
                nc.gpsimd.affine_select(out=w["bdmask"][:, :, :], in_=w["bdmask"][:, :, :], compare_op=ALU.is_ge,
                                        fill=0.0, base=D - 1, pattern=[[D, HC], [0, S1]],
                                        channel_multiplier=-1).then_inc(made, 1)
                g.wait_ge(zeroed, 1)
                nc.gpsimd.affine_select(out=w["mask_qk"][:, :], in_=w["zeros16"][:, :], compare_op=ALU.is_ge,
                                        fill=NEG, base=0, pattern=[[-1, P]], channel_multiplier=1)
                nc.gpsimd.affine_select(out=w["mask_kq"][:, :], in_=w["zeros16"][:, :], compare_op=ALU.is_ge,
                                        fill=NEG, base=0, pattern=[[1, P]], channel_multiplier=-1)
                nc.gpsimd.affine_select(out=w["mask_f32"][:, :], in_=w["zeros32"][:, :], compare_op=ALU.is_ge,
                                        fill=NEG, base=0, pattern=[[-1, P]], channel_multiplier=1)

            @block.vector
            def _(v):
                nc.vector.memset(w["zeros32"][:, :], 0.0)
                nc.vector.memset(w["zeros16"][:, :], 0.0).then_inc(zeroed, 1)
                v.wait_ge(loaded, 16 * len(loads))
                for src, dst, n in [(wqkv_raw[:, k, :], w["wqkv"][:, k, :], P) for k in range(KC)] \
                        + [(brow[:, :], brot[:, :], 1)]:
                    for qk in range(2):
                        a = src[:, qk * C:(qk + 1) * C].rearrange("p (n two) -> p n two", two=2)
                        o = dst[:, qk * C:(qk + 1) * C].rearrange("p (n two) -> p n two", two=2)
                        for into, x, y, op in ((0, 0, 1, ALU.subtract), (1, 1, 0, ALU.add)):
                            nc.vector.tensor_tensor(t0[0:n, :], a[:, :, x], ropec[0:n, :], ALU.mult)
                            nc.vector.tensor_tensor(t1[0:n, :], a[:, :, y], ropes[0:n, :], ALU.mult)
                            nc.vector.drain()
                            nc.vector.tensor_tensor(o[:, :, into], t0[0:n, :], t1[0:n, :], op)
                            nc.vector.drain()
                nc.vector.memset(one[:, :], 1.0)
                v.wait_ge(made, 5)
                for k in range(KC):
                    nc.vector.tensor_copy(w["wqkv"][:, k, 2 * C:3 * C], wqkv_raw[:, k, 2 * C:3 * C])
                    nc.vector.tensor_scalar(bvrep[:, k, :], ones[:, :], bv[:, k:k + 1], None, ALU.mult)
                nc.vector.tensor_copy(w["ident16"][:, :], w["ident"][:, :]).then_inc(turned, 1)
                nc.vector.tensor_copy(w["iota_row"][:, :], iota_i[:, :])
                nc.vector.tensor_copy(w["iota_col"][:, :], iota_c[:, :])
                v.wait_ge(cols, 1)
                nc.vector.tensor_copy(w["bqk"][:, :], ps[:, 6, 0:2 * KC])
                v.wait_ge(rows, 1)
                nc.vector.tensor_tensor(w["bias_proj"][:, :], ps[:, 7, 0:C], bproj[:, :], ALU.add)

            @block.tensor
            def _(pe):
                pe.wait_ge(turned, 1)
                for n in range(2 * KC):
                    last = nc.tensor.matmul(ps[:, 6, n:n + 1], brot[0:1, n * P:(n + 1) * P], one[:, :],
                                            start=True, stop=True)
                last.then_inc(cols, 1)
                for k in range(KC):
                    last = nc.tensor.matmul(ps[:, 7, 0:C], bvrep[:, k, :], w["wproj"][:, k, :],
                                            start=(k == 0), stop=(k == KC - 1))
                last.then_inc(rows, 1)
        m.clear()


def setup_rest_and_top_tokens(nc, io, w, ps):
    with Memory(nc) as m:
        loaded = m.sem("loaded2")
        q_loaded = m.sem("q_loaded")
        padded = m.sem("padded")
        flipped = m.sem("flipped")
        flipped_out = m.sem("flipped_out")
        unpacked = m.sem("unpacked")
        scaled = m.sem("scaled")
        sc_full = m.sem("sc_full")
        sc_ready = m.sem("sc_ready")
        sc_out = m.sem("sc_out")
        sc_in = m.sem("sc_in")
        idx_ready = m.sem("idx_ready")
        idx_out = m.sem("idx_out")

        sidx = m.sb("sidx", [P, S], I32)
        sidxf = m.sb("sidxf", [P, S])
        bigq = m.sb("bigq", [P, 2, F2], I32)
        scl = m.sb("scl", [P, 2, F2])
        b2row = m.sb("b2row", [P, C])
        sct = m.sb("sct", [B * NT, P])
        s8 = m.sb("s8", [B, T])
        top = m.sb("top8", [B, CAP])
        idx = m.sb("idx", [B, CAP], U32)
        idxf = m.sb("idxf", [B, CAP])

        turn = [(io["L0_ffn_W_qkv"], 3 * C, w["mod_wqkv"]), (io["L0_ffn_W_out"], C, w["mod_wout"]),
                (io["L0_ffn_W1"], DFF, w["mod_w1"]), (io["L0_ffn_W2"], DFF, w["mod_w2"]),
                (io["L1_attn_Wq"], C, w["ps_wq"]), (io["L1_attn_Wk"], C, w["ps_wk"]),
                (io["L1_attn_Wv"], C, w["ps_wv"]), (io["L1_attn_Wo"], C, w["ps_wo"])]
        stage = [m.sb(f"stage{n}", [P, -(-nrows // P), C]) for n, (_, nrows, _) in enumerate(turn)]
        w3 = m.sb("w3stage", [P, KC, DFF])
        loads = [(w["g1"][:, :], over_partitions(io["L0_ffn_g1"])),
                 (w["g2"][:, :], over_partitions(io["L0_ffn_g2"])),
                 (sidx[:, :], over_partitions(io["L1_attn_sample_idx"])),
                 (w["ps_bq"][:, :], over_partitions(io["L1_attn_bq"])),
                 (w["ps_bv"][:, :], over_partitions(io["L1_attn_bv"])),
                 (w["ps_bo"][:, :], over_partitions(io["L1_attn_bo"])),
                 (b2row[:, :], over_partitions(io["L1_ffn_fc2_bias"])),
                 (w["ps_bk"][:, :], io["L1_attn_bk"].rearrange("(k p) -> p k", p=P)),
                 (w["gamma"][:, :], io["L1_ffn_ln_gamma"].rearrange("(k p) -> p k", p=P)),
                 (w["beta"][:, :], io["L1_ffn_ln_beta"].rearrange("(k p) -> p k", p=P)),
                 (w["fc1_b"][:, :], io["L1_ffn_fc1_bias"].rearrange("(k p) -> p k", p=P)),
                 (w3[:, :, :], io["L0_ffn_W3"].rearrange("(a p) n -> p a n", p=P))]
        pieces = []
        for n, (src, nrows, dst) in enumerate(turn):
            full = nrows // P
            loads.append((stage[n][:, 0:full, :], src[0:full * P, :].rearrange("(a p) c -> p a c", p=P)))
            if nrows % P:
                loads.append((stage[n][0:nrows % P, full, :], src[full * P:nrows, :]))
            for a in range(-(-nrows // P)):
                r = min(P, nrows - a * P)
                for c in range(KC):
                    pieces.append((stage[n][0:r, a, c * P:(c + 1) * P], dst[:, c, a * P:a * P + r], P, r))
        for a in range(FT):
            k = min(P, DFF - a * P)
            for c in range(KC):
                pieces.append((w3[:, c, a * P:a * P + k], w["mod_w3"][0:k, a, c * P:(c + 1) * P], k, P))
        quant = [(io["L1_ffn_fc1_q"][k * P:(k + 1) * P, :], io["L1_ffn_fc1_scales"][k, :], w["fc1"][:, k, :], 1)
                 for k in range(KC)]
        quant += [(io["L1_ffn_fc2_q"][n * 4 * P:(n + 1) * 4 * P, :],
                   io["L1_ffn_fc2_scales"][n * 4:(n + 1) * 4, :].rearrange("k n -> (k n)"),
                   w["fc2"][:, n * 4:(n + 1) * 4, :].rearrange("p k n -> p (k n)"), 4) for n in range(2)]

        with nc.Block() as block:
            @block.sync
            def _(sp):
                with nc.allow_non_contiguous_dma(reason="a few columns of a bias"):
                    for dst, src in loads:
                        sp.dma_start(dst, src).then_inc(loaded, 16)
                sp.wait_ge(sc_ready, 1)
                sp.dma_start(io["scores"], sct[:, :]).then_inc(sc_out, 16)
                sp.wait_ge(sc_out, 16)
                sp.dma_start(s8[:, :], io["scores"].rearrange("(b j) p -> b (j p)", b=B)).then_inc(sc_in, 16)
                for n, (codes, scales, _, k) in enumerate(quant):
                    if n >= 2:
                        sp.wait_ge(scaled, n - 1)
                    sp.dma_start(bigq[:, n % 2, :].rearrange("p (k n) -> p k n", k=k),
                                 codes.rearrange("(k p) n -> p k n", p=P)).then_inc(q_loaded, 16)
                    sp.dma_start(scl[:, n % 2, :], over_partitions(scales)).then_inc(q_loaded, 16)
                    sp.wait_ge(q_loaded, 32 * (n + 1))
                sp.wait_ge(idx_ready, 1)
                sp.dma_start(io["top_tokens"], idxf[:, :]).then_inc(idx_out, 16)
                sp.wait_ge(idx_out, 16)

            @block.gpsimd
            def _(g):
                for n, (_, _, dst, _) in enumerate(quant):
                    g.wait_ge(q_loaded, 32 * (n + 1))
                    nc.gpsimd.tensor_copy(dst, bigq[:, n % 2, :]).then_inc(unpacked, 1)

            @block.vector
            def _(v):
                nc.vector.memset(w["mod_w1"][:, :, DFF:FT * P], 0.0)
                nc.vector.memset(w["mod_w2"][:, :, DFF:FT * P], 0.0)
                nc.vector.memset(w["mod_w3"][:, FT - 1, :], 0.0).then_inc(padded, 1)
                v.wait_ge(sc_full, 1)
                nc.vector.tensor_copy(sct[:, :], ps[0:B * NT, 7, 0:P]).then_inc(sc_ready, 1)
                v.wait_ge(sc_in, 16)
                for n in range(ROUNDS_C):
                    t8 = slice(8 * n, 8 * n + 8)
                    nc.vector.max(top[:, t8], s8[:, :])
                    nc.vector.drain()
                    nc.vector.max_index(idx[:, t8], top[:, t8], s8[:, :])
                    nc.vector.drain()
                    if n < ROUNDS_C - 1:
                        nc.vector.match_replace(s8[:, :], top[:, t8], s8[:, :], -3e38)
                        nc.vector.drain()
                nc.vector.tensor_copy(idxf[:, :], idx[:, :]).then_inc(idx_ready, 1)
                for n, (_, _, dst, _) in enumerate(quant):
                    v.wait_ge(unpacked, n + 1)
                    nc.vector.scalar_tensor_tensor(dst, dst, -128.0, scl[:, n % 2, :],
                                                   ALU.add, ALU.mult).then_inc(scaled, 1)
                nc.vector.drain()
                nc.vector.tensor_scalar(w["fc2"][:, :, :], w["fc2"][:, :, :], 0.5, None, ALU.mult)
                v.wait_ge(loaded, 16 * len(loads))
                nc.vector.tensor_scalar(w["fc2_b"][:, :], b2row[:, :], 0.5, None, ALU.mult)
                nc.vector.tensor_copy(sidxf[:, :], sidx[:, :])
                nc.vector.drain()
                for j in range(NT):
                    nc.vector.tensor_scalar(w["onehot_s"][:, j, :], sidxf[:, :], w["iota_col"][:, j:j + 1], None,
                                            ALU.is_equal)

            @block.tensor
            def _(pe):
                nc.tensor.transpose(ps[0:B * NT, 7, 0:P], w["scores"][:, :, :].rearrange("p b j -> p (b j)"),
                                    w["ident"][:, :]).then_inc(sc_full, 1)
                pe.wait_ge(loaded, 16 * len(loads))
                for n, (src, _, k, r) in enumerate(pieces):
                    if n >= 4:
                        pe.wait_ge(flipped_out, n - 3)
                    nc.tensor.transpose(ps[0:k, n % 4, 0:r], src,
                                        w["ident"][0:src.shape[0], 0:src.shape[0]]).then_inc(flipped, 1)

            @block.scalar
            def _(a):
                a.wait_ge(padded, 1)
                for n, (_, dst, k, r) in enumerate(pieces):
                    a.wait_ge(flipped, n + 1)
                    nc.scalar.copy(dst, ps[0:k, n % 4, 0:r]).then_inc(flipped_out, 1)
        m.clear()


TABLES = {
    "ident": ([P, P], F32), "ident16": ([P, P], BF16), "mask_qk": ([P, P], BF16), "mask_kq": ([P, P], BF16),
    "zeros16": ([P, P], BF16), "zeros32": ([P, P], F32), "mask_f32": ([P, P], F32),
    "bdmask": ([P, HC, S1], F32), "mhalf": ([P, NT], F32),
    "iota_row": ([P, T], F32), "iota_col": ([P, NT], F32),
    "scores": ([P, B, NT], F32),
}
ATTENTION_WEIGHTS = {
    "wqkv": ([P, KC, 3 * C], F32), "bqk": ([P, 2 * KC], F32), "wproj": ([P, KC, C], F32),
    "bias_proj": ([P, C], F32), "router": ([P, C], F32),
}
MOD_WEIGHTS = {
    "g1": ([P, C], F32), "g2": ([P, C], F32), "onehot_s": ([P, NT, S], F32),
    "mod_wqkv": ([P, KC, 3 * C], F32), "mod_wout": ([P, KC, C], F32),
    "mod_w1": ([P, KC, FT * P], F32), "mod_w2": ([P, KC, FT * P], F32), "mod_w3": ([P, FT, C], F32),
    "measure": ([P, NT, B * H], F32),
}
OTHER_WEIGHTS = {
    "ps_wq": ([P, KC, C], F32), "ps_wk": ([P, KC, C], F32), "ps_wv": ([P, KC, C], F32), "ps_wo": ([P, KC, C], F32),
    "ps_bq": ([P, C], F32), "ps_bv": ([P, C], F32), "ps_bo": ([P, C], F32), "ps_bk": ([P, KC], F32),
    "gamma": ([P, KC], F32), "beta": ([P, KC], F32),
    "fc1": ([P, KC, F2], F32), "fc1_b": ([P, F2T], F32), "fc2": ([P, F2T, C], F32), "fc2_b": ([P, C], F32),
}



SETS = 4
HS = H // SETS
PARTS = 3
Q_PARTS = (0, 0, 0, 1, 1, 2)
K_PARTS = (0, 1, 2, 0, 1, 0)
ROWS = len(Q_PARTS) * D
ROWS_M = ROWS + PARTS
SET_CHUNK = SETS // KC

MU = [(hh, i, n, min(BANK, (i + 1) * P - n * BANK))
      for hh in range(HS) for i in range(NT) for n in range(NHALF) if (i + 1) * P > n * BANK]
EU = [(n, j, max(n * BANK, j * P), (n + 1) * BANK - max(n * BANK, j * P))
      for n in range(NHALF) for j in range((n + 1) * BANK // P)]

RING = (0, 1, 7)
RING_STEPS = ("max", "rows", "t1", "t2", "proj", "xt", "qk", "v")


def steps_of_turn(tail, attention, head):
    if not attention:
        order = [("load_x",)] if head else []
        if tail:
            order += [("load_xr",)] + [("t1", i) for i in range(NT)]
            for i in range(NT + 1):
                order += [("t2", i)] if i < NT else []
                order += [("proj", i - 1)] if i else []
            order += [(kind, j) for kind in ("a_norm", "x1_stat", "xn1", "score") for j in range(NT)] + [("store",)]
        if head:
            order += [(kind, j) for kind in ("x_stat", "x_norm") for j in range(NT)] + [("xt", n, k) for n in range(NHALF) for k in range(KC)]
            for r in range(2):
                order += [("qk", r, 0, n) for n in range(NHALF)] + [("parts", r, 0, n) for n in range(NHALF)]
            order += [("stack", 0)] + [("v", 0, n) for n in range(NHALF)]
            order += [("max", SETS, n) for n in range(len(MU))] + [("rows", SETS), ("nm", SETS)]
        return order
    n_eu = len(EU)
    beside = {g: [] for g in range(SETS * n_eu)}

    def put(at, *steps):
        beside[at].extend(steps)

    tiles = range(NT)
    if head:
        put(0, ("load_x",))
    if tail:
        put(0, ("load_xr",), *[("t1", i) for i in tiles])
        for i in tiles:
            put(1 + i, ("t2", i))
            put(2 + i, ("proj", i))
    put(1, ("qk", 0, 1, 0), ("qk", 0, 1, 1))
    put(2, ("parts", 0, 1, 0), ("qk", 1, 1, 0))
    put(3, ("parts", 0, 1, 1), ("qk", 1, 1, 1))
    put(4, ("parts", 1, 1, 0), ("v", 1, 0))
    put(5, ("parts", 1, 1, 1), ("stack", 1), ("v", 1, 1))
    if head:
        put(9, *[("x_stat", j) for j in tiles[0:4]])
        put(10, *[("x_stat", j) for j in tiles[4:6]])
        put(11, *[("x_stat", j) for j in tiles[6:8]])
        for t in range(4):
            put(13 + t, *[("x_norm", j) for j in tiles[2 * t:2 * t + 2]])
        put(17, ("xt", 0, 0), ("xt", 0, 1))
        put(18, ("xt", 1, 0), ("xt", 1, 1))
        put(22, ("qk", 0, 0, 0), ("qk", 0, 0, 1))
        put(23, ("qk", 1, 0, 0), ("qk", 1, 0, 1))
        put(24, ("parts", 0, 0, 0))
        put(25, ("parts", 0, 0, 1), ("v", 0, 0))
        put(26, ("parts", 1, 0, 0), ("v", 0, 1))
        put(27, ("parts", 1, 0, 1))
        put(28, ("stack", 0))
    if tail:
        put(10, *[("a_norm", j) for j in tiles[0:2]])
        put(11, *[("a_norm", j) for j in tiles[2:8]])
        put(21, *[("x1_stat", j) for j in tiles[0:4]])
        put(22, *[("x1_stat", j) for j in tiles[4:6]])
        put(23, *[("x1_stat", j) for j in tiles[6:8]])
        put(33, *[("xn1", j) for j in tiles])
        put(34, *[("score", j) for j in tiles[0:4]])
        put(35, *[("score", j) for j in tiles[4:8]], ("store",))
    for s in range(SETS):
        if s + 1 < SETS or head:
            done = 0
            for g in range(9):
                upto = len(MU) * (g + 1) // 9
                put(s * n_eu + g, *[("max", s + 1, n) for n in range(done, upto)])
                done = upto
            put(s * n_eu + 9, ("rows", s + 1), ("nm", s + 1))
    order = []
    for t in range(SETS * n_eu + 1):
        rest = beside.get(t, [])
        cut = [rest[len(rest) * n // 3:len(rest) * (n + 1) // 3] for n in range(3)]
        if t < SETS * n_eu:
            for pair in range(2):
                order += [("exp", *divmod(t, n_eu), pair)] + cut[pair]
        if t:
            s, g = divmod(t - 1, n_eu)
            order.append(("av", s, g))
            if g == n_eu - 1 or EU[g + 1][0] != EU[g][0]:
                order.append(("y_out", s, EU[g][0]))
        order += cut[2]
    return order


def layer_stats(nc, stats, mv, tile, j):
    nc.vector.bn_stats(stats[:, j, :], tile)
    nc.vector.drain()
    return nc.vector.bn_aggr(mv[:, j, :], stats[:, j, :])


def rstd_of(nc, var, out, w, n, eps, ready, tmp, count):
    nc.gpsimd.tensor_scalar(tmp, var, eps, None, ALU.add).then_inc(ready, 1)
    nc.gpsimd.wait_ge(ready, count)
    return nc.gpsimd.tensor_tensor(out, tmp, w["mhalf"][:, 0:n], ALU.pow)


def attention_loop(nc, io, w, ps):
    with Memory(nc) as m:
        mem = {
            "x": m.sb("x", [P, NT, C]),
            "hstats": m.sb("hstats", [P, NT, 6]), "hmv": m.sb("hmv", [P, NT, 2]),
            "hrstd": m.sb("hrstd", [P, NT]), "htmp": m.sb("htmp", [P, NT]),
            "xnt": m.sb("xnt", [P, KC, T]),
            "qk": m.sb("qk", [P, 2, T]),
            "part": m.sb("part", [P, 2, PARTS, T], BF16),
            "sq": m.sb("sq", [P, H, T], BF16),
            "sk": m.sb("sk", [P, H, T], BF16),
            "val": m.sb("val", [P, NT, H, 32]),
            "mx": m.sb("mx", [P, HS, NT, NHALF]),
            "nm": m.sb("nm", [P, HS, NT]),
            "nmr": m.sb("nmr", [HS * NT, P]),
            "nmp": m.sb("nmp", [HS * NT, PARTS, P], BF16),
            "pt": m.sb("pt", [P, 3, HS, BANK]),
            "yt": m.sb("yt", [P, SETS, T]),
            "rs": m.sb("rs", [P, 2, H]),
            "att": m.sb("att", [P, NT, C]),
            "ynt": m.sb("ynt", [P, 2, KC, P]),
            "xr": m.sb("xr", [P, NT, C]),
            "tstats": m.sb("tstats", [P, NT, 6]), "tmv": m.sb("tmv", [P, NT, 2]),
            "trstd": m.sb("trstd", [P, NT]), "ttmp": m.sb("ttmp", [P, NT]),
            "sc": m.sb("sc", [P, NT]), "junk": m.sb("junk", [P, 2, C], BF16),
        }
        names = """x_in x_stat head_step x_rstd x_ready
            parts_ready nm_ready nmp_ready nm_out s_full exp_done av_done yt_ready xr_in a_stat tail_step a_rstd a_norm x1_ready x1_stat x1_rstd xn1_ready stored""".split()
        e = {n: m.sem("a_" + n) for n in names}
        e["bank_filled"] = [m.sem(f"a_bank_filled{n}") for n in range(len(RING))]
        e["bank_taken"] = [m.sem(f"a_bank_taken{n}") for n in range(len(RING))]
        e["parts_out"] = [m.sem(f"a_parts_out{n}") for n in range(2 * KC)]
        e["stack_in"] = [m.sem(f"a_stack_in{n}") for n in range(KC)]
        e["nm_in"] = [m.sem(f"a_nm_in{s}") for s in range(SETS + 1)]

        with nc.Block() as block:
            @block.vector
            def _(v):
                nc.vector.memset(mem["val"][:, :, :, D:32], 0.0)
                nc.vector.memset(mem["sk"][ROWS:P, :, :], 1.0)
                nc.vector.memset(mem["mx"][:, :, :, :], -3e38)
                nc.vector.drain()
                nc.vector.memset(mem["val"][:, :, :, D:D + 1], 1.0)
        m.clear()

        attention_turn(nc, io, w, ps, mem, e, -1, tail=False, attention=False, head=True)
        m.clear()
        attention_turn(nc, io, w, ps, mem, e, 0, tail=False, attention=True, head=True)
        m.clear()
        with nc.Fori(1, B - 1) as b:
            attention_turn(nc, io, w, ps, mem, e, b, tail=True, attention=True, head=True)
            m.clear()
        attention_turn(nc, io, w, ps, mem, e, B - 1, tail=True, attention=True, head=False)
        m.clear()
        attention_turn(nc, io, w, ps, mem, e, B, tail=True, attention=False, head=False)
        m.clear()


def attention_turn(nc, io, w, ps, mem, e, b, tail, attention, head):
    order = steps_of_turn(tail, attention, head)
    numbers = {step: k for k, step in enumerate(s for s in order if s[0] in RING_STEPS)}
    filled, taken = e["bank_filled"], e["bank_taken"]
    n_eu = len(EU)
    x, xnt, qk, part, sq, sk, val = (mem[n] for n in ("x", "xnt", "qk", "part", "sq", "sk", "val"))
    mx, nm, nmr, nmp, pt, yt = (mem[n] for n in ("mx", "nm", "nmr", "nmp", "pt", "yt"))
    att, ynt, xr, sc = (mem[n] for n in ("att", "ynt", "xr", "sc"))
    R = HS * NT

    nth = {step: [s for s in order if s[0] == step[0]].index(step) for step in order}

    def bank_use(step):
        return numbers[step] % len(RING), numbers[step] // len(RING)

    def chunk_of(s):
        return s % SETS // SET_CHUNK

    with nc.Block() as block:
        @block.sync
        def _(sp):
            for step in order:
                kind, a = step[0], step[1:]
                if kind == "load_x":
                    sp.dma_start(x[:, :, :], io["x"][b + 1].rearrange("(j p) c -> p j c", p=P))\
                        .then_inc(e["x_in"], 16)
                elif kind == "load_xr":
                    sp.dma_start(xr[:, :, :], io["x"][b - 1].rearrange("(j p) c -> p j c", p=P))\
                        .then_inc(e["xr_in"], 16)
                elif kind == "parts":
                    r, chunk, n = a
                    if n == NHALF - 1:
                        sp.wait_ge(e["parts_ready"], nth[step] + 1)
                        sp.dma_start(io["parts"][2 * chunk + r].rearrange("a r t -> r a t"),
                                     part[:, r, :, :]).then_inc(e["parts_out"][2 * chunk + r], 16)
                elif kind == "stack":
                    chunk, = a
                    if attention and chunk == 0:
                        sp.wait_ge(e["exp_done"], 2 * n_eu * SET_CHUNK)
                    for r, dst, use in ((0, sq, Q_PARTS), (1, sk, K_PARTS)):
                        sp.wait_ge(e["parts_out"][2 * chunk + r], 16)
                        for c, p_ in enumerate(use):
                            sp.dma_start(dst[c * D:(c + 1) * D, chunk * HC:(chunk + 1) * HC, :],
                                         io["parts"][2 * chunk + r, p_].rearrange("(h d) t -> d h t", d=D))\
                                .then_inc(e["stack_in"][chunk], 16)
                elif kind == "nm":
                    s, = a
                    h0 = s % SETS * HS
                    sp.wait_ge(e["nmp_ready"], nth[step] + 1)
                    sp.dma_start(io["nm_parts"].rearrange("a r q -> r a q"), nmp[:, :, :]).then_inc(e["nm_out"], 16)
                    sp.wait_ge(e["nm_out"], 16 * (nth[step] + 1))
                    sp.dma_start(sq[ROWS:ROWS_M, h0:h0 + HS, :],
                                 io["nm_parts"].rearrange("a (h i) q -> a h (i q)", h=HS)).then_inc(e["nm_in"][s], 16)
                    sp.wait_ge(e["nm_in"][s], 16)
                elif kind == "store":
                    sp.wait_ge(e["x1_ready"], NT)
                    sp.dma_start(io["x1"][b - 1].rearrange("(j p) c -> p j c", p=P), xr[:, :, :])\
                        .then_inc(e["stored"], 16)
                    sp.wait_ge(e["xn1_ready"], NT)
                    sp.dma_start(io["xn1"][b - 1].rearrange("(j p) c -> p j c", p=P), att[:, :, :])\
                        .then_inc(e["stored"], 16)
            if tail:
                sp.wait_ge(e["stored"], 32)

        @block.gpsimd
        def _(g):
            for step in order:
                kind = step[0]
                if kind == "x_norm" and step[1] == 0:
                    g.wait_ge(e["x_stat"], 1)
                    rstd_of(nc, mem["hmv"][:, :, 1], mem["hrstd"][:, :], w, NT, EPS_LN, e["head_step"],
                            mem["htmp"][:, :], 1).then_inc(e["x_rstd"], 1)
                elif kind == "a_norm" and step[1] == 0:
                    g.wait_ge(e["a_stat"], 1)
                    rstd_of(nc, mem["tmv"][:, :, 1], mem["trstd"][:, :], w, NT, EPS_LN, e["tail_step"],
                            mem["ttmp"][:, :], 1).then_inc(e["a_rstd"], 1)
                    g.wait_ge(e["xr_in"], 16)
                    for j in range(NT):
                        g.wait_ge(e["a_norm"], j + 1)
                        nc.gpsimd.tensor_tensor(xr[:, j, :], xr[:, j, :], att[:, j, :], ALU.add)\
                            .then_inc(e["x1_ready"], 1)
                elif kind == "xn1" and step[1] == 0:
                    g.wait_ge(e["x1_stat"], 1)
                    rstd_of(nc, mem["tmv"][:, :, 1], mem["trstd"][:, :], w, NT, EPS_LN, e["tail_step"],
                            mem["ttmp"][:, :], 2).then_inc(e["x1_rstd"], 1)

        @block.vector
        def _(v):
            for step in order:
                kind, a = step[0], step[1:]
                if kind in RING_STEPS:
                    slot, uses = bank_use(step)
                if kind == "max":
                    s, n_unit = a
                    hh, i, half, n = MU[n_unit]
                    v.wait_ge(filled[slot], uses + 1)
                    nc.vector.reduce_max(mx[:, hh, i, half:half + 1], ps[:, RING[slot], 0:n], AX.X)\
                        .then_inc(taken[slot], 1)
                elif kind == "rows":
                    nc.vector.drain()
                    nc.vector.tensor_reduce(nm[:, :, :], mx[:, :, :, :], AX.X, ALU.max, negate=True)\
                        .then_inc(e["nm_ready"], 1)
                    v.wait_ge(filled[slot], uses + 1)
                    if nth[step]:
                        v.wait_ge(e["nm_out"], 16 * nth[step])
                    nc.vector.tensor_copy(nmr[:, :], ps[0:R, RING[slot], 0:P]).then_inc(taken[slot], 1)
                    nc.vector.drain()
                    nc.vector.tensor_copy(nmp[:, 0, :], nmr[:, :])
                    nc.vector.drain()
                    nc.vector.tensor_tensor(nmr[:, :], nmr[:, :], nmp[:, 0, :], ALU.subtract)
                    nc.vector.drain()
                    nc.vector.tensor_copy(nmp[:, 1, :], nmr[:, :])
                    nc.vector.drain()
                    nc.vector.tensor_tensor(nmp[:, 2, :], nmr[:, :], nmp[:, 1, :], ALU.subtract)\
                        .then_inc(e["nmp_ready"], 1)
                elif kind == "parts":
                    r, chunk, n = a
                    half = slice(n * BANK, (n + 1) * BANK)
                    slot, uses = bank_use(("qk", r, chunk, n))
                    v.wait_ge(taken[slot], uses + 1)
                    if nth[step] >= 2 * NHALF:
                        v.wait_ge(e["parts_out"][2 * (1 - chunk) + r], 16)
                    nc.vector.tensor_copy(part[:, r, 0, half], qk[:, r, half])
                    nc.vector.drain()
                    nc.vector.tensor_tensor(qk[:, r, half], qk[:, r, half], part[:, r, 0, half], ALU.subtract)
                    nc.vector.drain()
                    nc.vector.tensor_copy(part[:, r, 1, half], qk[:, r, half])
                    nc.vector.drain()
                    nc.vector.tensor_tensor(part[:, r, 2, half], qk[:, r, half], part[:, r, 1, half], ALU.subtract)\
                        .then_inc(e["parts_ready"], 1)
                elif kind == "x_stat":
                    j, = a
                    v.wait_ge(e["x_in"], 16)
                    last = layer_stats(nc, mem["hstats"], mem["hmv"], x[:, j, :], j)
                    if j == NT - 1:
                        last.then_inc(e["x_stat"], 1)
                elif kind == "x_norm":
                    j, = a
                    v.wait_ge(e["x_rstd"], 1)
                    nc.vector.tensor_scalar(x[:, j, :], x[:, j, :], mem["hmv"][:, j, 0:1],
                                            mem["hrstd"][:, j:j + 1], ALU.subtract, ALU.mult)\
                        .then_inc(e["x_ready"], 1)
                elif kind == "t1":
                    i, = a
                    v.wait_ge(filled[slot], uses + 1)
                    yq = ps[:, RING[slot], :].rearrange("p (h d) -> p h d", d=32)
                    nc.vector.reciprocal(mem["rs"][:, i % 2, :], yq[:, :, D])
                    nc.vector.drain()
                    nc.vector.tensor_tensor(att[:, i, :].rearrange("p (h d) -> p h d", d=D), yq[:, :, 0:D],
                                            spread(mem["rs"][:, i % 2, :], 2, D), ALU.mult)\
                        .then_inc(taken[slot], 1)
                elif kind == "proj":
                    i, = a
                    v.wait_ge(filled[slot], uses + 1)
                    nc.vector.tensor_tensor(att[:, i, :], ps[:, RING[slot], 0:C], w["bias_proj"][:, :], ALU.add)\
                        .then_inc(taken[slot], 1)
                    nc.vector.drain()
                    last = layer_stats(nc, mem["tstats"], mem["tmv"], att[:, i, :], i)
                    if i == NT - 1:
                        last.then_inc(e["a_stat"], 1)
                elif kind == "a_norm":
                    j, = a
                    v.wait_ge(e["a_rstd"], 1)
                    nc.vector.tensor_scalar(att[:, j, :], att[:, j, :], mem["tmv"][:, j, 0:1],
                                            mem["trstd"][:, j:j + 1], ALU.subtract, ALU.mult)\
                        .then_inc(e["a_norm"], 1)
                elif kind == "x1_stat":
                    j, = a
                    v.wait_ge(e["x1_ready"], j + 1)
                    last = layer_stats(nc, mem["tstats"], mem["tmv"], xr[:, j, :], j)
                    if j == NT - 1:
                        last.then_inc(e["x1_stat"], 1)
                elif kind == "xn1":
                    j, = a
                    v.wait_ge(e["x1_rstd"], 1)
                    nc.vector.tensor_scalar(att[:, j, :], xr[:, j, :], mem["tmv"][:, j, 0:1],
                                            mem["trstd"][:, j:j + 1], ALU.subtract, ALU.mult)\
                        .then_inc(e["xn1_ready"], 1)
                elif kind == "score":
                    j, = a
                    nc.vector.drain()
                    nc.vector.scalar_tensor_tensor(mem["junk"][:, j % 2, :], att[:, j, :], 1.0, w["router"][:, :],
                                                   ALU.mult, ALU.mult, accum_out=sc[:, j:j + 1])
                    if j == NT - 1:
                        nc.vector.drain()
                        nc.vector.tensor_copy(w["scores"][:, bass.ds(b - 1, 1), :], spread(sc[:, :], 1, 1))

        @block.tensor
        def _(pe):
            for step in order:
                kind, a = step[0], step[1:]
                if kind in RING_STEPS:
                    slot, uses = bank_use(step)
                    bank = RING[slot]
                    if uses:
                        pe.wait_ge(taken[slot], uses)
                if kind == "max":
                    s, n_unit = a
                    hh, i, half, n = MU[n_unit]
                    h = s % SETS * HS + hh
                    if n_unit == 0 and (s == SETS or s == SET_CHUNK):
                        pe.wait_ge(e["stack_in"][chunk_of(s)], 16 * 2 * len(Q_PARTS))
                    diag = (i * P) // BANK == half
                    last = nc.tensor.matmul(ps[:, bank, 0:n], sq[0:ROWS, h, i * P:(i + 1) * P],
                                            sk[0:ROWS, h, half * BANK:half * BANK + n], start=True, stop=not diag)
                    if diag:
                        last = nc.tensor.matmul(ps[:, bank, n - P:n], w["ident16"][:, :], w["mask_qk"][:, :],
                                                start=False, stop=True)
                    last.then_inc(filled[slot], 1)
                elif kind == "rows":
                    pe.wait_ge(e["nm_ready"], nth[step] + 1)
                    nc.tensor.transpose(ps[0:R, bank, 0:P], nm[:, :, :].rearrange("p h i -> p (h i)"),
                                        w["ident"][:, :]).then_inc(filled[slot], 1)
                elif kind == "exp":
                    s, g, pair = a
                    half, j, q0, n = EU[g]
                    if g == 0 and s:
                        pe.wait_ge(e["nm_in"][s], 16)
                    t = 2 * (s * n_eu + g) + pair
                    if t >= 2:
                        pe.wait_ge(e["exp_done"], t - 1)
                    for f in range(2):
                        h = s * HS + 2 * pair + f
                        bank = 2 + 2 * (t % 2) + f
                        diag = q0 == j * P
                        last = nc.tensor.matmul(ps[:, bank, 0:n], sk[0:ROWS_M, h, j * P:(j + 1) * P],
                                                sq[0:ROWS_M, h, q0:q0 + n], start=True, stop=not diag)
                        if diag:
                            last = nc.tensor.matmul(ps[:, bank, 0:P], w["ident16"][:, :], w["mask_kq"][:, :],
                                                    start=False, stop=True)
                    last.then_inc(e["s_full"], 1)
                elif kind == "av":
                    s, g = a
                    half, j, q0, n = EU[g]
                    t = s * n_eu + g
                    if j == 0 and NHALF * s + half:
                        pe.wait_ge(e["yt_ready"], NHALF * s + half)
                    if t == SET_CHUNK * n_eu:
                        for done in [("v", 1, n_) for n_ in range(NHALF)]:
                            pe.wait_ge(taken[bank_use(done)[0]], bank_use(done)[1] + 1)
                    pe.wait_ge(e["exp_done"], 2 * t + 2)
                    c0 = q0 - half * BANK
                    for hh in range(HS):
                        last = nc.tensor.matmul(ps[32 * hh:32 * hh + 32, 6, c0:c0 + n], val[:, j, s * HS + hh, :],
                                                pt[:, t % 3, hh, 0:n], start=(j == 0),
                                                stop=(q0 + n == (j + 1) * P), skip_group_check=True)
                    last.then_inc(e["av_done"], 1)
                elif kind == "xt":
                    n, k = a
                    pe.wait_ge(e["x_ready"], 4 * (n + 1))
                    for t in range(4):
                        last = nc.tensor.transpose(ps[:, bank, t * P:(t + 1) * P],
                                                   x[:, 4 * n + t, k * P:(k + 1) * P], w["ident"][:, :])
                    last.then_inc(filled[slot], 1)
                elif kind == "qk":
                    r, chunk, n = a
                    if chunk == 0:
                        for done in [("xt", n_, k_) for n_ in range(NHALF) for k_ in range(KC)]:
                            pe.wait_ge(taken[bank_use(done)[0]], bank_use(done)[1] + 1)
                    col = r * C + chunk * P
                    for k in range(KC):
                        last = nc.tensor.matmul(ps[:, bank, :], w["wqkv"][:, k, col:col + P],
                                                xnt[:, k, n * BANK:(n + 1) * BANK], start=(k == 0), stop=(k == KC - 1))
                    last.then_inc(filled[slot], 1)
                elif kind == "v":
                    chunk, n = a
                    if chunk == 0:
                        for done in [("xt", n_, k_) for n_ in range(NHALF) for k_ in range(KC)]:
                            pe.wait_ge(taken[bank_use(done)[0]], bank_use(done)[1] + 1)
                    col = 2 * C + chunk * P
                    for t in range(4):
                        for k in range(KC):
                            j = 4 * n + t
                            last = nc.tensor.matmul(ps[:, bank, t * P:(t + 1) * P],
                                                    xnt[:, k, j * P:(j + 1) * P], w["wqkv"][:, k, col:col + P],
                                                    start=(k == 0), stop=(k == KC - 1))
                    last.then_inc(filled[slot], 1)
                elif kind == "t1":
                    i, = a
                    for s in range(SETS):
                        last = nc.tensor.transpose(ps[:, bank, s * P:(s + 1) * P],
                                                   yt[:, s, i * P:(i + 1) * P], w["ident"][:, :])
                    last.then_inc(filled[slot], 1)
                elif kind == "t2":
                    i, = a
                    slot1, uses1 = bank_use(("t1", i))
                    pe.wait_ge(taken[slot1], uses1 + 1)
                    for k in range(KC):
                        last = nc.tensor.transpose(ps[:, bank, k * P:(k + 1) * P],
                                                   att[:, i, k * P:(k + 1) * P], w["ident"][:, :])
                    last.then_inc(filled[slot], 1)
                elif kind == "proj":
                    i, = a
                    slot2, uses2 = bank_use(("t2", i))
                    pe.wait_ge(taken[slot2], uses2 + 1)
                    for k in range(KC):
                        last = nc.tensor.matmul(ps[:, bank, 0:C], ynt[:, i % 2, k, :], w["wproj"][:, k, :],
                                                start=(k == 0), stop=(k == KC - 1))
                    last.then_inc(filled[slot], 1)

        @block.scalar
        def _(act):
            for step in order:
                kind, a = step[0], step[1:]
                if kind in RING_STEPS:
                    slot, uses = bank_use(step)
                if kind == "exp":
                    s, g, pair = a
                    half, j, q0, n = EU[g]
                    u = s * n_eu + g
                    t = 2 * u + pair
                    act.wait_ge(e["s_full"], t + 1)
                    if u >= 3:
                        act.wait_ge(e["av_done"], u - 2)
                    bank = 2 + 2 * (t % 2)
                    nc.scalar.activation(pt[:, u % 3, 2 * pair:2 * pair + 2, 0:n], ps[:, bank:bank + 2, 0:n],
                                         ACT.Exp, scale=SCALE).then_inc(e["exp_done"], 1)
                elif kind == "y_out":
                    s, half = a
                    act.wait_ge(e["av_done"], s * n_eu + sum(1 for u in EU if u[0] <= half))
                    if tail and s == 0:
                        for done in [("t1", i) for i in range(NT)]:
                            act.wait_ge(taken[bank_use(done)[0]], bank_use(done)[1] + 1)
                    nc.scalar.copy(yt[:, s, half * BANK:(half + 1) * BANK], ps[:, 6, :]).then_inc(e["yt_ready"], 1)
                elif kind == "xt":
                    n, k = a
                    act.wait_ge(filled[slot], uses + 1)
                    nc.scalar.copy(xnt[:, k, n * BANK:(n + 1) * BANK], ps[:, RING[slot], :])\
                        .then_inc(taken[slot], 1)
                elif kind == "qk":
                    r, chunk, n = a
                    act.wait_ge(filled[slot], uses + 1)
                    if nth[step] >= 2 * NHALF:
                        act.wait_ge(e["parts_ready"], nth[step] - 2 * NHALF + 1)
                    nc.scalar.activation(qk[:, r, n * BANK:(n + 1) * BANK], ps[:, RING[slot], :], ACT.Identity,
                                         bias=w["bqk"][:, r * KC + chunk:r * KC + chunk + 1])\
                        .then_inc(taken[slot], 1)
                elif kind == "v":
                    chunk, n = a
                    act.wait_ge(filled[slot], uses + 1)
                    if attention and chunk == 0:
                        act.wait_ge(e["av_done"], SET_CHUNK * n_eu)
                    nc.scalar.copy(val[:, 4 * n:4 * n + 4, chunk * HC:(chunk + 1) * HC, 0:D],
                                   ps[:, RING[slot], :].rearrange("p (j h d) -> p j h d", j=4, d=D))\
                        .then_inc(taken[slot], 1)
                elif kind == "t2":
                    i, = a
                    act.wait_ge(filled[slot], uses + 1)
                    if i >= 2:
                        slot2, uses2 = bank_use(("proj", i - 2))
                        act.wait_ge(filled[slot2], uses2 + 1)
                    nc.scalar.copy(ynt[:, i % 2, :, :],
                                   ps[:, RING[slot], 0:C].rearrange("p (k t) -> p k t", k=KC))\
                        .then_inc(taken[slot], 1)



def mod_loop(nc, io, w, ps):
    with Memory(nc) as m:
        x = m.sb("cx", [P, NT, C])
        xn = m.sb("cxn", [P, NT, C])
        idxc = m.sb("idxc", [P, 1])
        idxb = m.sb("idxb", [P, CAP])
        oh = m.sb("oh", [P, NT, CAP])
        oht = m.sb("oht", [CAP, T])
        xs = m.sb("xs", [P, C])
        ss = m.sb("ss", [P, 2])
        stmp = m.sb("stmp", [P, 2])
        srs = m.sb("srs", [P, 2])
        junk = m.sb("cjunk", [P, C])
        hn = m.sb("hn", [P, C])
        hnt = m.sb("hnt", [P, KC, P])
        qt = m.sb("cqt", [P, KC, P])
        kbd = m.sb("kbd", [P, KC, HC, P])
        vv = m.sb("vv", [P, C])
        sm = m.sb("sm", [P, H, P])
        smx = m.sb("smx", [P, H])
        ssum = m.sb("ssum", [P, H])
        pt = m.sb("cpt", [P, H, P])
        o = m.sb("co", [P, H, D])
        ot = m.sb("cot", [P, KC, P])
        xa = m.sb("xa", [P, C])
        gate = m.sb("gate", [P, FT, P])
        delta = m.sb("delta", [P, C])
        stats = m.sb("cstats", [P, NT, 6])
        mv = m.sb("cmv", [P, NT, 2])
        vtmp = m.sb("cvtmp", [P, NT])
        rstd = m.sb("crstd", [P, NT])
        xnt = m.sb("cxnt", [P, KC, T])
        xst = m.sb("xst", [P, KC, S])
        ks = m.sb("ks", [P, KC, S1])
        ksbd = m.sb("ksbd", [P, KC, HC, S1])
        q = m.sb("cq", [P, NT, C])
        qtt = m.sb("qtt", [P, KC, T])
        mm = m.sb("mm", [P, NT, KC, HC])

        names = """x_in xn_in idx_in oh_ready oht_ready xs_full xs_ss rms_step rms_ready hn_ready hnt_full hnt_ready
            qk_full v_full qt_ready kbd_ready vv_ready s_full s_masked s_less exp_ready pt_full pt_ready pt_ready_v
            o_full o_ready ot_full ot_ready xa_full gate_full up_full silu_ready gate_ready ff_full delta_ready
            put_full put_ready a_stat a_rstd a_norm x2_ready x2_stat x2_rstd xn2_ready xnt_full xnt_ready xst_full
            xst_ready ks_full ksbd_ready q_full q_ready qtt_full qtt_ready ms_full ms_ready stored
            pool_step""".split()
        e = {n: m.sem("c_" + n) for n in names}

        with nc.Fori(0, B) as b:
            with nc.Block() as block:
                @block.sync
                def _(sp):
                    sp.dma_start(idxb[:, :], over_partitions(io["top_tokens"][b, :])).then_inc(e["idx_in"], 16)
                    sp.dma_start(idxc[:, :], io["top_tokens"][b, :].rearrange("(p a) -> p a", a=1))\
                        .then_inc(e["idx_in"], 16)
                    sp.dma_start(xn[:, :, :], io["xn1"][b].rearrange("(j p) c -> p j c", p=P)).then_inc(e["xn_in"], 16)
                    sp.dma_start(x[:, :, :], io["x1"][b].rearrange("(j p) c -> p j c", p=P)).then_inc(e["x_in"], 16)
                    sp.wait_ge(e["x2_ready"], NT)
                    sp.dma_start(io["x2"][b].rearrange("(j p) c -> p j c", p=P), x[:, :, :]).then_inc(e["stored"], 16)
                    sp.wait_ge(e["xn2_ready"], NT)
                    sp.dma_start(io["xn2"][b].rearrange("(j p) c -> p j c", p=P), xn[:, :, :]).then_inc(e["stored"], 16)
                    sp.wait_ge(e["q_ready"], NT)
                    sp.dma_start(io["q"][b].rearrange("(j p) c -> p j c", p=P), q[:, :, :]).then_inc(e["stored"], 16)
                    sp.wait_ge(e["stored"], 48)

                @block.gpsimd
                def _(g):
                    for n in range(2):
                        g.wait_ge(e["xs_ss"], n + 1)
                        nc.gpsimd.tensor_scalar(stmp[:, n:n + 1], ss[:, n:n + 1], 1.0 / C, EPS_RMS,
                                                ALU.mult, ALU.add).then_inc(e["rms_step"], 1)
                        g.wait_ge(e["rms_step"], n + 1)
                        nc.gpsimd.tensor_tensor(srs[:, n:n + 1], stmp[:, n:n + 1], w["mhalf"][:, 0:1],
                                                ALU.pow).then_inc(e["rms_ready"], 1)
                    g.wait_ge(e["a_stat"], 1)
                    rstd_of(nc, mv[:, :, 1], rstd[:, :], w, NT, EPS_LN, e["pool_step"], vtmp[:, :], 1)\
                        .then_inc(e["a_rstd"], 1)
                    g.wait_ge(e["x_in"], 16)
                    for j in range(NT):
                        g.wait_ge(e["a_norm"], j + 1)
                        nc.gpsimd.tensor_tensor(x[:, j, :], x[:, j, :], xn[:, j, :], ALU.add)\
                            .then_inc(e["x2_ready"], 1)
                    g.wait_ge(e["x2_stat"], 1)
                    rstd_of(nc, mv[:, :, 1], rstd[:, :], w, NT, EPS_LN, e["pool_step"], vtmp[:, :], 2)\
                        .then_inc(e["x2_rstd"], 1)

                @block.vector
                def _(v):
                    v.wait_ge(e["idx_in"], 32)
                    for j in range(NT):
                        nc.vector.tensor_scalar(oh[:, j, :], idxb[:, :], w["iota_col"][:, j:j + 1], None,
                                                ALU.is_equal).then_inc(e["oh_ready"], 1)
                    nc.vector.tensor_scalar(oht[:, :], w["iota_row"][:, :], idxc[:, :], None,
                                            ALU.is_equal).then_inc(e["oht_ready"], 1)
                    v.wait_ge(e["xs_full"], 1)
                    nc.vector.tensor_copy(xs[:, :], ps[:, 0, 0:C])
                    nc.vector.drain()
                    nc.vector.scalar_tensor_tensor(junk[:, :], xs[:, :], 1.0, xs[:, :], ALU.mult, ALU.mult,
                                                   accum_out=ss[:, 0:1]).then_inc(e["xs_ss"], 1)
                    v.wait_ge(e["rms_ready"], 1)
                    nc.vector.scalar_tensor_tensor(hn[:, :], xs[:, :], srs[:, 0:1], w["g1"][:, :],
                                                   ALU.mult, ALU.mult).then_inc(e["hn_ready"], 1)
                    v.wait_ge(e["qk_full"], 1)
                    for k in range(KC):
                        nc.vector.tensor_tensor(kbd[:, k, :, :], spread(ps[:, 0, k * P:(k + 1) * P], 1, HC),
                                                w["bdmask"][:, :, 0:1].to_broadcast([P, HC, P]),
                                                ALU.mult).then_inc(e["kbd_ready"], 1)
                    for n in range(4):
                        v.wait_ge(e["s_full"], n + 1)
                        nc.vector.scalar_tensor_tensor(sm[:, 4 * n:4 * n + 4, :],
                                                       ps[:, 4 + n, :].rearrange("p (h k) -> p h k", k=P), SCALE,
                                                       spread(w["mask_f32"][:, :], 1, 4), ALU.mult, ALU.add)
                    nc.vector.drain()
                    nc.vector.reduce_max(smx[:, :], sm[:, :, :], AX.X)
                    nc.vector.drain()
                    nc.vector.tensor_tensor(sm[:, :, :], sm[:, :, :], spread(smx[:, :], 2, P),
                                            ALU.subtract).then_inc(e["s_less"], 1)
                    v.wait_ge(e["exp_ready"], 1)
                    nc.vector.reduce_sum(ssum[:, :], sm[:, :, :], AX.X)
                    nc.vector.drain()
                    nc.vector.reciprocal(ssum[:, :], ssum[:, :])
                    for n in (1, 3):
                        v.wait_ge(e["pt_full"], n + 1)
                        nc.vector.tensor_copy(pt[:, 4 * n:4 * n + 4, :],
                                              ps[:, n, :].rearrange("p (h k) -> p h k", k=P)).then_inc(e["pt_ready_v"], 1)
                    v.wait_ge(e["o_full"], 1)
                    nc.vector.tensor_tensor(o[:, :, :], ps[:, 4, 0:C].rearrange("p (h d) -> p h d", d=D),
                                            spread(ssum[:, :], 2, D), ALU.mult).then_inc(e["o_ready"], 1)
                    v.wait_ge(e["xa_full"], 1)
                    nc.vector.tensor_tensor(xa[:, :], ps[:, 6, 0:C], xs[:, :], ALU.add)
                    nc.vector.drain()
                    nc.vector.scalar_tensor_tensor(junk[:, :], xa[:, :], 1.0, xa[:, :], ALU.mult, ALU.mult,
                                                   accum_out=ss[:, 1:2]).then_inc(e["xs_ss"], 1)
                    v.wait_ge(e["rms_ready"], 2)
                    nc.vector.scalar_tensor_tensor(hn[:, :], xa[:, :], srs[:, 1:2], w["g2"][:, :],
                                                   ALU.mult, ALU.mult).then_inc(e["hn_ready"], 1)
                    v.wait_ge(e["silu_ready"], 2)
                    v.wait_ge(e["up_full"], 1)
                    nc.vector.tensor_tensor(gate[:, 0:4, :], gate[:, 0:4, :],
                                            ps[:, 2, :].rearrange("p (f t) -> p f t", t=P), ALU.mult)
                    nc.vector.tensor_tensor(gate[:, 4:FT, :], gate[:, 4:FT, :],
                                            ps[:, 3, 0:(FT - 4) * P].rearrange("p (f t) -> p f t", t=P),
                                            ALU.mult).then_inc(e["gate_ready"], 1)
                    v.wait_ge(e["ff_full"], 1)
                    nc.vector.tensor_tensor(delta[:, :], ps[:, 4, 0:C], xa[:, :], ALU.add)
                    nc.vector.drain()
                    nc.vector.tensor_tensor(delta[:, :], delta[:, :], xs[:, :], ALU.subtract).then_inc(e["delta_ready"], 1)
                    for j in range(NT):
                        v.wait_ge(e["put_full"], j + 1)
                        nc.vector.tensor_tensor(xn[:, j, :], xn[:, j, :], ps[:, 5 + j % 2, 0:C],
                                                ALU.add).then_inc(e["put_ready"], 1)
                        nc.vector.drain()
                        last = layer_stats(nc, stats, mv, xn[:, j, :], j)
                    last.then_inc(e["a_stat"], 1)
                    v.wait_ge(e["a_rstd"], 1)
                    for j in range(NT):
                        nc.vector.tensor_scalar(xn[:, j, :], xn[:, j, :], mv[:, j, 0:1], rstd[:, j:j + 1],
                                                ALU.subtract, ALU.mult).then_inc(e["a_norm"], 1)
                    nc.vector.drain()
                    for j in range(NT):
                        v.wait_ge(e["x2_ready"], j + 1)
                        last = layer_stats(nc, stats, mv, x[:, j, :], j)
                    last.then_inc(e["x2_stat"], 1)
                    v.wait_ge(e["x2_rstd"], 1)
                    for j in range(NT):
                        nc.vector.tensor_scalar(xn[:, j, :], x[:, j, :], mv[:, j, 0:1], rstd[:, j:j + 1],
                                                ALU.subtract, ALU.mult).then_inc(e["xn2_ready"], 1)
                    v.wait_ge(e["xst_full"], 1)
                    nc.vector.tensor_copy(xst[:, :, :], ps[:, 4, 0:KC * S].rearrange("p (k s) -> p k s", s=S))\
                        .then_inc(e["xst_ready"], 1)
                    v.wait_ge(e["ks_full"], 1)
                    for k in range(KC):
                        nc.vector.tensor_scalar(ks[:, k, 0:S], ps[:, 5, k * S:(k + 1) * S], w["ps_bk"][:, k:k + 1], None,
                                                ALU.add)
                    nc.vector.drain()
                    nc.vector.reduce_sum(ks[:, :, S:S1], ks[:, :, 0:S], AX.X)
                    nc.vector.drain()
                    nc.vector.tensor_scalar(ks[:, :, S:S1], ks[:, :, S:S1], 1.0 / S, None, ALU.mult)
                    nc.vector.drain()
                    for k in range(KC):
                        nc.vector.tensor_tensor(ksbd[:, k, :, :], spread(ks[:, k, :], 1, HC), w["bdmask"][:, :, :],
                                                ALU.mult).then_inc(e["ksbd_ready"], 1)
                    for j in range(NT):
                        v.wait_ge(e["q_full"], j + 1)
                        nc.vector.tensor_tensor(q[:, j, :], ps[:, 6 + j % 2, 0:C], w["ps_bq"][:, :],
                                                ALU.add).then_inc(e["q_ready"], 1)
                    for j in range(NT):
                        v.wait_ge(e["ms_full"], j + 1)
                        two = ps[:, 2 * (j % 2):2 * (j % 2) + 2, 0:HC * S1].rearrange("p k (h s) -> p k h s", s=S1)
                        nc.vector.reduce_max(mm[:, j, :, :], two[:, :, :, 0:S], AX.X)
                        nc.vector.drain()
                        nc.vector.tensor_tensor(mm[:, j, :, :], mm[:, j, :, :], two[:, :, :, S],
                                                ALU.subtract).then_inc(e["ms_ready"], 1)
                    nc.vector.drain()
                    nc.vector.tensor_copy(w["measure"][:, :, bass.ds(b * H, H)],
                                          mm[:, :, :, :].rearrange("p j k h -> p j (k h)"))

                @block.tensor
                def _(pe):
                    pe.wait_ge(e["xn_in"], 16)
                    for j in range(NT):
                        pe.wait_ge(e["oh_ready"], j + 1)
                        last = nc.tensor.matmul(ps[:, 0, 0:C], oh[:, j, :], xn[:, j, :],
                                                start=(j == 0), stop=(j == NT - 1))
                    last.then_inc(e["xs_full"], 1)

                    def turn(src, bank, full):
                        for k in range(KC):
                            last = nc.tensor.transpose(ps[:, bank, k * P:(k + 1) * P], src[:, k * P:(k + 1) * P],
                                                       w["ident"][:, :])
                        last.then_inc(full, 1)

                    pe.wait_ge(e["hn_ready"], 1)
                    turn(hn, 1, e["hnt_full"])
                    pe.wait_ge(e["hnt_ready"], 1)
                    for cc in range(2 * KC):
                        for k in range(KC):
                            last = nc.tensor.matmul(ps[:, 2 - cc // KC * 2, cc % KC * P:(cc % KC + 1) * P],
                                                    w["mod_wqkv"][:, k, cc * P:(cc + 1) * P], hnt[:, k, :],
                                                    start=(k == 0), stop=(k == KC - 1))
                    last.then_inc(e["qk_full"], 1)
                    for k in range(KC):
                        last = nc.tensor.matmul(ps[:, 3, 0:C], hnt[:, k, :], w["mod_wqkv"][:, k, 2 * C:3 * C],
                                                start=(k == 0), stop=(k == KC - 1))
                    last.then_inc(e["v_full"], 1)
                    pe.wait_ge(e["qt_ready"], 1)
                    for n in range(4):
                        k, half = divmod(n, 2)
                        pe.wait_ge(e["kbd_ready"], k + 1)
                        nc.tensor.matmul(ps[:, 4 + n, :], qt[:, k, :],
                                         kbd[:, k, 4 * half:4 * half + 4, :].rearrange("p h t -> p (h t)"),
                                         start=True, stop=True).then_inc(e["s_full"], 1)
                    pe.wait_ge(e["exp_ready"], 1)
                    pe.wait_ge(e["vv_ready"], 1)
                    for n in range(4):
                        for t in range(4):
                            last = nc.tensor.transpose(ps[:, n, t * P:(t + 1) * P], sm[:, 4 * n + t, :], w["ident"][:, :])
                        last.then_inc(e["pt_full"], 1)
                    pe.wait_ge(e["pt_ready"], 2)
                    pe.wait_ge(e["pt_ready_v"], 2)
                    for h in range(H):
                        last = nc.tensor.matmul(ps[:, 4, h * D:(h + 1) * D], pt[:, h, :], vv[:, h * D:(h + 1) * D],
                                                start=True, stop=True)
                    last.then_inc(e["o_full"], 1)
                    pe.wait_ge(e["o_ready"], 1)
                    turn(o[:, :, :].rearrange("p h d -> p (h d)"), 5, e["ot_full"])
                    pe.wait_ge(e["ot_ready"], 1)
                    for k in range(KC):
                        last = nc.tensor.matmul(ps[:, 6, 0:C], ot[:, k, :], w["mod_wout"][:, k, :],
                                                start=(k == 0), stop=(k == KC - 1))
                    last.then_inc(e["xa_full"], 1)
                    pe.wait_ge(e["hn_ready"], 2)
                    turn(hn, 7, e["hnt_full"])
                    pe.wait_ge(e["hnt_ready"], 2)
                    for wt, bank0, full in ((w["mod_w1"], 0, e["gate_full"]), (w["mod_w2"], 2, e["up_full"])):
                        for f in range(FT):
                            for k in range(KC):
                                last = nc.tensor.matmul(ps[:, bank0 + f // 4, (f % 4) * P:(f % 4 + 1) * P],
                                                        wt[:, k, f * P:(f + 1) * P], hnt[:, k, :],
                                                        start=(k == 0), stop=(k == KC - 1))
                        last.then_inc(full, 1)
                    pe.wait_ge(e["gate_ready"], 1)
                    for f in range(FT):
                        last = nc.tensor.matmul(ps[:, 4, 0:C], gate[:, f, :], w["mod_w3"][:, f, :],
                                                start=(f == 0), stop=(f == FT - 1))
                    last.then_inc(e["ff_full"], 1)
                    pe.wait_ge(e["delta_ready"], 1)
                    pe.wait_ge(e["oht_ready"], 1)
                    for j in range(NT):
                        if j >= 2:
                            pe.wait_ge(e["put_ready"], j - 1)
                        nc.tensor.matmul(ps[:, 5 + j % 2, 0:C], oht[:, j * P:(j + 1) * P], delta[:, :],
                                         start=True, stop=True).then_inc(e["put_full"], 1)
                    for n in range(NHALF):
                        pe.wait_ge(e["xn2_ready"], 4 * (n + 1))
                        for k in range(KC):
                            for t in range(4):
                                last = nc.tensor.transpose(ps[:, 2 * n + k, t * P:(t + 1) * P],
                                                           xn[:, 4 * n + t, k * P:(k + 1) * P], w["ident"][:, :])
                            last.then_inc(e["xnt_full"], 1)
                    for k in range(KC):
                        for j in range(NT):
                            last = nc.tensor.matmul(ps[:, 4, k * S:(k + 1) * S], xn[:, j, k * P:(k + 1) * P],
                                                    w["onehot_s"][:, j, :], start=(j == 0), stop=(j == NT - 1))
                    last.then_inc(e["xst_full"], 1)
                    pe.wait_ge(e["xst_ready"], 1)
                    for cc in range(KC):
                        for k in range(KC):
                            last = nc.tensor.matmul(ps[:, 5, cc * S:(cc + 1) * S], w["ps_wk"][:, k, cc * P:(cc + 1) * P],
                                                    xst[:, k, :], start=(k == 0), stop=(k == KC - 1))
                    last.then_inc(e["ks_full"], 1)
                    pe.wait_ge(e["xnt_ready"], NHALF * KC)
                    for j in range(NT):
                        if j >= 2:
                            pe.wait_ge(e["q_ready"], j - 1)
                        for k in range(KC):
                            last = nc.tensor.matmul(ps[:, 6 + j % 2, 0:C], xnt[:, k, j * P:(j + 1) * P],
                                                    w["ps_wq"][:, k, :], start=(k == 0), stop=(k == KC - 1))
                        last.then_inc(e["q_full"], 1)
                    for n in range(NHALF):
                        pe.wait_ge(e["q_ready"], 4 * (n + 1))
                        for k in range(KC):
                            for t in range(4):
                                last = nc.tensor.transpose(ps[:, 4 + 2 * n + k, t * P:(t + 1) * P],
                                                           q[:, 4 * n + t, k * P:(k + 1) * P], w["ident"][:, :])
                            last.then_inc(e["qtt_full"], 1)
                    pe.wait_ge(e["ksbd_ready"], KC)
                    for j in range(NT):
                        if j % 4 == 0:
                            pe.wait_ge(e["qtt_ready"], KC * (j // 4 + 1))
                        if j >= 2:
                            pe.wait_ge(e["ms_ready"], j - 1)
                        for k in range(KC):
                            last = nc.tensor.matmul(ps[:, 2 * (j % 2) + k, 0:HC * S1], qtt[:, k, j * P:(j + 1) * P],
                                                    ksbd[:, k, :, :].rearrange("p h s -> p (h s)"), start=True, stop=True)
                        last.then_inc(e["ms_full"], 1)

                @block.scalar
                def _(a):
                    def out_of(bank, dst, full, count, ready):
                        a.wait_ge(full, count)
                        nc.scalar.copy(dst, ps[:, bank, 0:C].rearrange("p (k t) -> p k t", k=KC)).then_inc(ready, 1)

                    out_of(1, hnt[:, :, :], e["hnt_full"], 1, e["hnt_ready"])
                    out_of(2, qt[:, :, :], e["qk_full"], 1, e["qt_ready"])
                    a.wait_ge(e["v_full"], 1)
                    nc.scalar.copy(vv[:, :], ps[:, 3, 0:C]).then_inc(e["vv_ready"], 1)
                    a.wait_ge(e["s_less"], 1)
                    nc.scalar.activation(sm[:, :, :], sm[:, :, :], ACT.Exp).then_inc(e["exp_ready"], 1)
                    for n in (0, 2):
                        a.wait_ge(e["pt_full"], n + 1)
                        nc.scalar.copy(pt[:, 4 * n:4 * n + 4, :],
                                       ps[:, n, :].rearrange("p (h k) -> p h k", k=P)).then_inc(e["pt_ready"], 1)
                    out_of(5, ot[:, :, :], e["ot_full"], 1, e["ot_ready"])
                    out_of(7, hnt[:, :, :], e["hnt_full"], 2, e["hnt_ready"])
                    a.wait_ge(e["gate_full"], 1)
                    nc.scalar.activation(gate[:, 0:4, :], ps[:, 0, :].rearrange("p (f t) -> p f t", t=P),
                                         ACT.Silu).then_inc(e["silu_ready"], 1)
                    nc.scalar.activation(gate[:, 4:FT, :], ps[:, 1, 0:(FT - 4) * P].rearrange("p (f t) -> p f t", t=P),
                                         ACT.Silu).then_inc(e["silu_ready"], 1)
                    for n in range(NHALF):
                        for k in range(KC):
                            a.wait_ge(e["xnt_full"], KC * n + k + 1)
                            nc.scalar.copy(xnt[:, k, n * BANK:(n + 1) * BANK],
                                           ps[:, 2 * n + k, :]).then_inc(e["xnt_ready"], 1)
                    for n in range(NHALF):
                        for k in range(KC):
                            a.wait_ge(e["qtt_full"], KC * n + k + 1)
                            nc.scalar.copy(qtt[:, k, n * BANK:(n + 1) * BANK],
                                           ps[:, 4 + 2 * n + k, :]).then_inc(e["qtt_ready"], 1)
            m.clear()


def top_queries(nc, io, w, ps):
    with Memory(nc) as m:
        full = m.sem("d_full")
        ready = m.sem("d_ready")
        stored = m.sem("d_stored")
        ms = m.sb("ms", [P, T])
        top = m.sb("dtop", [P, 8 * ROUNDS_E])
        idx = m.sb("didx", [P, 8 * ROUNDS_E], U32)
        idxf = m.sb("didxf", [P, 8 * ROUNDS_E])
        with nc.Block() as block:
            @block.tensor
            def _(pe):
                for j in range(NT):
                    nc.tensor.transpose(ps[:, j // 4, (j % 4) * P:(j % 4 + 1) * P], w["measure"][:, j, :],
                                        w["ident"][:, :]).then_inc(full, 1)

            @block.vector
            def _(v):
                for n in range(NHALF):
                    v.wait_ge(full, 4 * (n + 1))
                    nc.vector.tensor_copy(ms[:, n * BANK:(n + 1) * BANK], ps[:, n, :])
                nc.vector.drain()
                for n in range(ROUNDS_E):
                    t8 = slice(8 * n, 8 * n + 8)
                    nc.vector.max(top[:, t8], ms[:, :])
                    nc.vector.drain()
                    nc.vector.max_index(idx[:, t8], top[:, t8], ms[:, :])
                    nc.vector.drain()
                    if n < ROUNDS_E - 1:
                        nc.vector.match_replace(ms[:, :], top[:, t8], ms[:, :], -3e38)
                        nc.vector.drain()
                nc.vector.tensor_copy(idxf[:, :], idx[:, :]).then_inc(ready, 1)

            @block.sync
            def _(sp):
                sp.wait_ge(ready, 1)
                sp.dma_start(io["top_queries"].rearrange("b (h u) -> (b h) u", u=S), idxf[:, 0:S]).then_inc(stored, 16)
                sp.wait_ge(stored, 16)
        m.clear()



def chunks_of(mt):
    half = HU // KC
    return [k for k in range(KC) if mt * MR < (k + 1) * half and (mt + 1) * MR > k * half]


def prob_loop(nc, io, w, ps):
    HALF = HU // KC
    with Memory(nc) as m:
        x = m.sb("ex", [P, NT, C])
        xn = m.sb("exn", [P, NT, C])
        q = m.sb("eq", [P, NT, C])
        idxb = m.sb("eidxb", [P, HU])
        idxc = m.sb("eidxc", [MR, MT])
        oh = m.sb("eoh", [P, NT, HU])
        oht = m.sb("eoht", [MR, MT, T])
        xnt = m.sb("exnt", [P, KC, T])
        kt = m.sb("ekt", [P, KC, T])
        vv = m.sb("evv", [P, NT, C])
        qbd = m.sb("qbd", [P, KC, HU])
        obd = m.sb("obd", [P, KC, HU])
        nmx = m.sb("nmx", [MR, MT])
        nb = m.sb("nb", [MR, MT])
        sums = m.sb("sums", [MR, MT])
        dg = m.sb("dg", [MR, MT, MR])
        pr = m.sb("pr", [MR, MT, T])
        pt = m.sb("ept", [P, NT, HU])
        vm = m.sb("vm", [P, KC])
        vmr = m.sb("vmr", [P, KC, P])
        mean1 = m.sb("mean1", [P, 1])
        gg = m.sb("gg", [MR, MT, C])
        base = m.sb("base", [P, C])
        stats = m.sb("estats", [P, NT, 6])
        mv = m.sb("emv", [P, NT, 2])
        vtmp = m.sb("evtmp", [P, NT])
        rstd = m.sb("erstd", [P, NT])
        att = q
        hh = kt[:, :, :].rearrange("p k (j c) -> p (k j) c", c=C)
        hn = vv
        ht = xnt
        yb = oh[:, 0:NT, 0:BANK]

        names = """x_in xn_in q_in idx_in oh_ready oht_ready xnt_full xnt_ready qb_full qbd_ready kt_full kt_ready
            v_full v_ready s_full nb_ready exp_ready dg_ready pt_full pt_ready_a pt_ready_v vm_full vmr_ready ot_full
            obd_ready g_full g_ready base_full base_ready ctx_full ctx_ready a_stat a_rstd a_norm x3_ready x3_stat
            x3_rstd hh_ready hh_stat hh_rstd hn_ready hb_ready ht_full ht_ready f1_full y_ready f2_full r_ready r_stat
            r_rstd r_norm out_ready stored pool_step""".split()
        e = {n: m.sem("e_" + n) for n in names}

        with nc.Block() as block:
            @block.vector
            def _(v):
                nc.vector.memset(qbd[:, :, :], 0.0)
                nc.vector.memset(obd[:, :, :], 0.0)
                nc.vector.memset(mean1[:, :], 1.0 / T)
        m.clear()

        with nc.Fori(0, B) as b:
            with nc.Block() as block:
                @block.sync
                def _(sp):
                    def rows(name):
                        return io[name][b].rearrange("(j p) c -> p j c", p=P)

                    sp.dma_start(xn[:, :, :], rows("xn2")).then_inc(e["xn_in"], 16)
                    sp.dma_start(idxb[:, :], over_partitions(io["top_queries"][b, :])).then_inc(e["idx_in"], 16)
                    with nc.allow_non_contiguous_dma(reason="560 indices as columns"):
                        sp.dma_start(idxc[:, :], io["top_queries"][b, :].rearrange("(m r) -> r m", r=MR))\
                            .then_inc(e["idx_in"], 16)
                    sp.dma_start(q[:, :, :], rows("q")).then_inc(e["q_in"], 16)
                    sp.dma_start(x[:, :, :], rows("x2")).then_inc(e["x_in"], 16)
                    for n in range(2):
                        sp.wait_ge(e["out_ready"], 4 * (n + 1))
                        sp.dma_start(io["out"][b, n * BANK:(n + 1) * BANK, :].rearrange("(j p) c -> p j c", p=P),
                                     x[:, 4 * n:4 * n + 4, :]).then_inc(e["stored"], 16)
                    sp.wait_ge(e["stored"], 32)

                @block.gpsimd
                def _(g):
                    def rstd_step(stat, n, done):
                        g.wait_ge(e[stat], 1)
                        rstd_of(nc, mv[:, :, 1], rstd[:, :], w, NT, EPS_LN, e["pool_step"], vtmp[:, :], n)\
                            .then_inc(e[done], 1)

                    rstd_step("a_stat", 1, "a_rstd")
                    g.wait_ge(e["x_in"], 16)
                    for j in range(NT):
                        g.wait_ge(e["a_norm"], j + 1)
                        nc.gpsimd.tensor_tensor(x[:, j, :], x[:, j, :], att[:, j, :], ALU.add)\
                            .then_inc(e["x3_ready"], 1)
                    rstd_step("x3_stat", 2, "x3_rstd")
                    rstd_step("hh_stat", 3, "hh_rstd")
                    for j in range(NT):
                        g.wait_ge(e["hn_ready"], j + 1)
                        nc.gpsimd.tensor_tensor(hh[:, j, :], hh[:, j, :], w["fc2_b"][:, :], ALU.add)\
                            .then_inc(e["hb_ready"], 1)
                    rstd_step("r_stat", 4, "r_rstd")
                    for j in range(NT):
                        g.wait_ge(e["r_norm"], j + 1)
                        nc.gpsimd.tensor_tensor(x[:, j, :], x[:, j, :], att[:, j, :], ALU.add)\
                            .then_inc(e["out_ready"], 1)

                @block.vector
                def _(v):
                    v.wait_ge(e["idx_in"], 32)
                    for j in range(NT):
                        nc.vector.tensor_scalar(oh[:, j, :], idxb[:, :], w["iota_col"][:, j:j + 1], None,
                                                ALU.is_equal).then_inc(e["oh_ready"], 1)
                    for k in range(KC):
                        v.wait_ge(e["qb_full"], k + 1)
                        nc.vector.tensor_tensor(qbd[:, k, k * HALF:(k + 1) * HALF].rearrange("p (h u) -> p h u", u=S),
                                                ps[:, 4 + k, 0:HALF].rearrange("p (h u) -> p h u", u=S),
                                                w["bdmask"][:, :, 0:S], ALU.mult).then_inc(e["qbd_ready"], 1)
                    for j in range(NT):
                        v.wait_ge(e["v_full"], j + 1)
                        nc.vector.tensor_tensor(vv[:, j, :], ps[:, 4 + j % 2, 0:C], w["ps_bv"][:, :],
                                                ALU.add).then_inc(e["v_ready"], 1)
                    for mt in range(MT):
                        v.wait_ge(e["s_full"], mt + 1)
                        b0 = 2 * (mt % 2)
                        nc.vector.tensor_reduce(nmx[:, mt:mt + 1], ps[0:MR, b0:b0 + 2, :], AX.XY, ALU.max, negate=True)
                        nc.vector.drain()
                        nc.vector.tensor_scalar(nb[:, mt:mt + 1], nmx[:, mt:mt + 1], SCALE, None,
                                                ALU.mult).then_inc(e["nb_ready"], 1)
                        if mt == 1:
                            v.wait_ge(e["vm_full"], 1)
                            nc.vector.tensor_copy(vm[:, :], ps[:, 6, 0:KC])
                            nc.vector.drain()
                            for k in range(KC):
                                last = nc.vector.tensor_copy(vmr[:, k, :], vm[:, k:k + 1].to_broadcast([P, P]))
                            last.then_inc(e["vmr_ready"], 1)
                        if mt >= 1:
                            diagonal(nc, v, e, dg, sums, w, mt - 1)
                        if mt >= 2:
                            take_pt(nc, v, e, pt, ps, mt - 2, 1)
                    diagonal(nc, v, e, dg, sums, w, MT - 1)
                    take_pt(nc, v, e, pt, ps, MT - 2, 1)
                    take_pt(nc, v, e, pt, ps, MT - 1, 1)
                    v.wait_ge(e["base_full"], 1)
                    nc.vector.tensor_tensor(base[:, :], ps[:, 2, 0:C], w["ps_bo"][:, :], ALU.add)\
                        .then_inc(e["base_ready"], 1)
                    for k in range(KC):
                        v.wait_ge(e["ot_full"], k + 1)
                        nc.vector.scalar_tensor_tensor(
                            obd[:, k, k * HALF:(k + 1) * HALF].rearrange("p (h u) -> p h u", u=S),
                            ps[:, k, 0:HALF].rearrange("p (h u) -> p h u", u=S), vm[:, k:k + 1],
                            w["bdmask"][:, :, 0:S], ALU.subtract, ALU.mult).then_inc(e["obd_ready"], 1)
                    for mt in range(MT):
                        nc.vector.tensor_scalar(oht[:, mt, :], w["iota_row"][0:MR, :], idxc[:, mt:mt + 1], None,
                                                ALU.is_equal).then_inc(e["oht_ready"], 1)
                    for j in range(NT):
                        v.wait_ge(e["ctx_full"], j + 1)
                        nc.vector.tensor_tensor(att[:, j, :], ps[:, 6 + j % 2, 0:C], base[:, :],
                                                ALU.add).then_inc(e["ctx_ready"], 1)
                        nc.vector.drain()
                        last = layer_stats(nc, stats, mv, att[:, j, :], j)
                    last.then_inc(e["a_stat"], 1)

                    def normalise(dst, src, rstd_sem, ready):
                        v.wait_ge(e[rstd_sem], 1)
                        for j in range(NT):
                            nc.vector.tensor_scalar(dst[:, j, :], src[:, j, :], mv[:, j, 0:1], rstd[:, j:j + 1],
                                                    ALU.subtract, ALU.mult).then_inc(e[ready], 1)
                        nc.vector.drain()

                    def stats_of(src, done, ready=None):
                        for j in range(NT):
                            if ready:
                                v.wait_ge(e[ready], j + 1)
                            last = layer_stats(nc, stats, mv, src[:, j, :], j)
                        last.then_inc(e[done], 1)

                    normalise(att, att, "a_rstd", "a_norm")
                    stats_of(x, "x3_stat", "x3_ready")
                    normalise(hh, x, "x3_rstd", "hh_ready")
                    stats_of(hh, "hh_stat")
                    normalise(hn, hh, "hh_rstd", "hn_ready")
                    for j in range(NT):
                        v.wait_ge(e["f2_full"], j + 1)
                        v.wait_ge(e["hb_ready"], j + 1)
                        nc.vector.tensor_tensor(att[:, j, :], ps[:, 4 + j % 2, 0:C], hh[:, j, :],
                                                ALU.add).then_inc(e["r_ready"], 1)
                        nc.vector.drain()
                        last = layer_stats(nc, stats, mv, att[:, j, :], j)
                    last.then_inc(e["r_stat"], 1)
                    normalise(att, att, "r_rstd", "r_norm")

                @block.tensor
                def _(pe):
                    def turn(src, ready, full):
                        for n in range(NHALF):
                            pe.wait_ge(e[ready], 4 * (n + 1) if ready != "xn_in" else 16)
                            for k in range(KC):
                                for t in range(4):
                                    last = nc.tensor.transpose(ps[:, 2 * n + k, t * P:(t + 1) * P],
                                                               src[:, 4 * n + t, k * P:(k + 1) * P], w["ident"][:, :])
                                last.then_inc(e[full], 1)

                    turn(xn, "xn_in", "xnt_full")
                    pe.wait_ge(e["q_in"], 16)
                    for k in range(KC):
                        for j in range(NT):
                            if k == 0:
                                pe.wait_ge(e["oh_ready"], j + 1)
                            last = nc.tensor.matmul(ps[:, 4 + k, 0:HALF], q[:, j, k * P:(k + 1) * P],
                                                    oh[:, j, k * HALF:(k + 1) * HALF], start=(j == 0), stop=(j == NT - 1))
                        last.then_inc(e["qb_full"], 1)
                    pe.wait_ge(e["xnt_ready"], NHALF * KC)
                    u = 0
                    for cc in range(KC):
                        for n in range(NHALF):
                            if u >= 2:
                                pe.wait_ge(e["kt_ready"], u - 1)
                            for k in range(KC):
                                last = nc.tensor.matmul(ps[:, 6 + u % 2, :], w["ps_wk"][:, k, cc * P:(cc + 1) * P],
                                                        xnt[:, k, n * BANK:(n + 1) * BANK],
                                                        start=(k == 0), stop=(k == KC - 1))
                            last.then_inc(e["kt_full"], 1)
                            u += 1
                    pe.wait_ge(e["qbd_ready"], KC)
                    for j in range(NT):
                        if j >= 2:
                            pe.wait_ge(e["v_ready"], j - 1)
                        for k in range(KC):
                            last = nc.tensor.matmul(ps[:, 4 + j % 2, 0:C], xnt[:, k, j * P:(j + 1) * P],
                                                    w["ps_wv"][:, k, :], start=(k == 0), stop=(k == KC - 1))
                        last.then_inc(e["v_full"], 1)
                    pe.wait_ge(e["kt_ready"], KC * NHALF)

                    def scores(mt):
                        if mt >= 2:
                            pe.wait_ge(e["exp_ready"], mt - 1)
                        for n in range(NHALF):
                            cs = chunks_of(mt)
                            for k in cs:
                                last = nc.tensor.matmul(ps[0:MR, 2 * (mt % 2) + n, :], qbd[:, k, mt * MR:(mt + 1) * MR],
                                                        kt[:, k, n * BANK:(n + 1) * BANK],
                                                        start=(k == cs[0]), stop=(k == cs[-1]))
                        last.then_inc(e["s_full"], 1)

                    def probs_t(mt):
                        pe.wait_ge(e["dg_ready"], mt + 1)
                        if mt >= 1:
                            pe.wait_ge(e["pt_ready_a"], mt)
                            pe.wait_ge(e["pt_ready_v"], mt)
                        for j in range(NT):
                            last = nc.tensor.matmul(ps[:, 4 + j // 4, (j % 4) * MR:(j % 4 + 1) * MR],
                                                    pr[:, mt, j * P:(j + 1) * P], dg[:, mt, :], start=True, stop=True)
                            if j % 4 == 3:
                                last.then_inc(e["pt_full"], 1)

                    scores(0)
                    scores(1)
                    pe.wait_ge(e["v_ready"], NT)
                    for k in range(KC):
                        for j in range(NT):
                            last = nc.tensor.matmul(ps[:, 6, k:k + 1], vv[:, j, k * P:(k + 1) * P], mean1[:, :],
                                                    start=(j == 0), stop=(j == NT - 1))
                    last.then_inc(e["vm_full"], 1)
                    for mt in range(MT):
                        if mt + 2 < MT:
                            scores(mt + 2)
                        probs_t(mt)
                    pe.wait_ge(e["exp_ready"], MT)
                    pe.wait_ge(e["vmr_ready"], 1)
                    for k in range(KC):
                        last = nc.tensor.matmul(ps[:, 2, 0:C], vmr[:, k, :], w["ps_wo"][:, k, :],
                                                start=(k == 0), stop=(k == KC - 1))
                    last.then_inc(e["base_full"], 1)
                    pe.wait_ge(e["pt_ready_a"], MT)
                    pe.wait_ge(e["pt_ready_v"], MT)
                    for k in range(KC):
                        for j in range(NT):
                            last = nc.tensor.matmul(ps[:, k, 0:HALF], vv[:, j, k * P:(k + 1) * P],
                                                    pt[:, j, k * HALF:(k + 1) * HALF], start=(j == 0), stop=(j == NT - 1))
                        last.then_inc(e["ot_full"], 1)
                    pe.wait_ge(e["obd_ready"], KC)
                    for mt in range(MT):
                        if mt >= 2:
                            pe.wait_ge(e["g_ready"], mt - 1)
                        cs = chunks_of(mt)
                        for k in cs:
                            last = nc.tensor.matmul(ps[0:MR, 4 + mt % 2, 0:C], obd[:, k, mt * MR:(mt + 1) * MR],
                                                    w["ps_wo"][:, k, :], start=(k == cs[0]), stop=(k == cs[-1]))
                        last.then_inc(e["g_full"], 1)
                    pe.wait_ge(e["g_ready"], MT)
                    pe.wait_ge(e["oht_ready"], MT)
                    pe.wait_ge(e["base_ready"], 1)
                    for j in range(NT):
                        if j >= 2:
                            pe.wait_ge(e["ctx_ready"], j - 1)
                        for mt in range(MT):
                            last = nc.tensor.matmul(ps[:, 6 + j % 2, 0:C], oht[:, mt, j * P:(j + 1) * P], gg[:, mt, :],
                                                    start=(mt == 0), stop=(mt == MT - 1))
                        last.then_inc(e["ctx_full"], 1)
                    turn(hn, "hn_ready", "ht_full")
                    pe.wait_ge(e["ht_ready"], NHALF * KC)
                    for n in range(NHALF):
                        for f in range(F2T):
                            u = n * F2T + f
                            if u >= 4:
                                pe.wait_ge(e["y_ready"], u - 3)
                            for k in range(KC):
                                last = nc.tensor.matmul(ps[:, u % 4, :], w["fc1"][:, k, f * P:(f + 1) * P],
                                                        ht[:, k, n * BANK:(n + 1) * BANK],
                                                        start=(k == 0), stop=(k == KC - 1))
                            last.then_inc(e["f1_full"], 1)
                        for t in range(4):
                            j = 4 * n + t
                            pe.wait_ge(e["y_ready"], F2T * (n + 1))
                            if j >= 2:
                                pe.wait_ge(e["r_ready"], j - 1)
                            for f in range(F2T):
                                last = nc.tensor.matmul(ps[:, 4 + j % 2, 0:C], yb[:, f, t * P:(t + 1) * P],
                                                        w["fc2"][:, f, :], start=(f == 0), stop=(f == F2T - 1))
                            last.then_inc(e["f2_full"], 1)

                @block.scalar
                def _(a):
                    for n in range(NHALF):
                        for k in range(KC):
                            a.wait_ge(e["xnt_full"], KC * n + k + 1)
                            nc.scalar.copy(xnt[:, k, n * BANK:(n + 1) * BANK],
                                           ps[:, 2 * n + k, :]).then_inc(e["xnt_ready"], 1)
                    u = 0
                    for cc in range(KC):
                        for n in range(NHALF):
                            a.wait_ge(e["kt_full"], u + 1)
                            nc.scalar.activation(kt[:, cc, n * BANK:(n + 1) * BANK], ps[:, 6 + u % 2, :], ACT.Identity,
                                                 bias=w["ps_bk"][:, cc:cc + 1]).then_inc(e["kt_ready"], 1)
                            u += 1
                    for mt in range(MT):
                        a.wait_ge(e["nb_ready"], mt + 1)
                        b0 = 2 * (mt % 2)
                        nc.scalar.activation(pr[:, mt, :].rearrange("p (n t) -> p n t", n=NHALF), ps[0:MR, b0:b0 + 2, :],
                                             ACT.Exp, bias=nb[:, mt:mt + 1], scale=SCALE,
                                             accum_out=sums[:, mt:mt + 1]).then_inc(e["exp_ready"], 1)
                        if mt >= 1:
                            take_pt(nc, a, e, pt, ps, mt - 1, 0)
                    take_pt(nc, a, e, pt, ps, MT - 1, 0)
                    for mt in range(MT):
                        a.wait_ge(e["g_full"], mt + 1)
                        nc.scalar.copy(gg[:, mt, :], ps[0:MR, 4 + mt % 2, 0:C]).then_inc(e["g_ready"], 1)
                    for n in range(NHALF):
                        for k in range(KC):
                            a.wait_ge(e["ht_full"], KC * n + k + 1)
                            nc.scalar.activation(ht[:, k, n * BANK:(n + 1) * BANK], ps[:, 2 * n + k, :], ACT.Identity,
                                                 scale=w["gamma"][:, k:k + 1],
                                                 bias=w["beta"][:, k:k + 1]).then_inc(e["ht_ready"], 1)
                    for n in range(NHALF):
                        for f in range(F2T):
                            u = n * F2T + f
                            a.wait_ge(e["f1_full"], u + 1)
                            if n:
                                a.wait_ge(e["f2_full"], 4 * n)
                            nc.scalar.activation(yb[:, f, :], ps[:, u % 4, :], ACT.Silu,
                                                 bias=w["fc1_b"][:, f:f + 1]).then_inc(e["y_ready"], 1)
            m.clear()


def diagonal(nc, v, e, dg, sums, w, mt):
    v.wait_ge(e["exp_ready"], mt + 1)
    nc.vector.reciprocal(sums[:, mt:mt + 1], sums[:, mt:mt + 1])
    nc.vector.drain()
    nc.vector.tensor_scalar(dg[:, mt, :], w["ident"][0:MR, 0:MR], sums[:, mt:mt + 1], None,
                            ALU.mult).then_inc(e["dg_ready"], 1)


def take_pt(nc, eng, e, pt, ps, mt, half):
    eng.wait_ge(e["pt_full"], 2 * mt + half + 1)
    src = ps[:, 4 + half, 0:4 * MR].rearrange("p (j r) -> p j r", r=MR)
    dst = pt[:, 4 * half:4 * half + 4, mt * MR:(mt + 1) * MR]
    if half:
        nc.vector.tensor_copy(dst, src).then_inc(e["pt_ready_v"], 1)
    else:
        nc.scalar.copy(dst, src).then_inc(e["pt_ready_a"], 1)


def build_program(nc, io):
    with Memory(nc) as m:
        ps = m.stack.enter_context(nc.psum_tensor("ps", [P, 8, BANK], F32))
        w = {name: m.sb("w_" + name, shape, dt) for name, (shape, dt) in TABLES.items()}
        with Memory(nc) as first:
            w |= {name: first.sb("w_" + name, shape, dt) for name, (shape, dt) in ATTENTION_WEIGHTS.items()}
            setup_attention(nc, io, w, ps)
            attention_loop(nc, io, w, ps)
        w |= {name: m.sb("w_" + name, shape, dt) for name, (shape, dt) in OTHER_WEIGHTS.items()}
        with Memory(nc) as second:
            w |= {name: second.sb("w_" + name, shape, dt) for name, (shape, dt) in MOD_WEIGHTS.items()}
            setup_rest_and_top_tokens(nc, io, w, ps)
            mod_loop(nc, io, w, ps)
            top_queries(nc, io, w, ps)
        prob_loop(nc, io, w, ps)


_INS = ['L0_attn_x', 'L0_attn_W_attn', 'L0_attn_b_attn', 'L0_attn_W_proj', 'L0_attn_b_proj', 'L0_ffn_w_router',
        'L0_ffn_W_qkv', 'L0_ffn_W_out', 'L0_ffn_g1', 'L0_ffn_g2', 'L0_ffn_W1', 'L0_ffn_W2', 'L0_ffn_W3',
        'L1_attn_Wq', 'L1_attn_bq', 'L1_attn_Wk', 'L1_attn_bk', 'L1_attn_Wv', 'L1_attn_bv', 'L1_attn_Wo', 'L1_attn_bo',
        'L1_attn_sample_idx', 'L1_ffn_ln_gamma', 'L1_ffn_ln_beta', 'L1_ffn_fc1_q', 'L1_ffn_fc1_scales',
        'L1_ffn_fc1_bias', 'L1_ffn_fc2_q', 'L1_ffn_fc2_scales', 'L1_ffn_fc2_bias']
_SCRATCH = {"parts": ((2 * KC, PARTS, P, T), BF16), "nm_parts": ((PARTS, HS * NT, P), BF16),
            "x1": ((B, T, C), F32), "xn1": ((B, T, C), F32),
            "scores": ((B * NT, P), F32), "top_tokens": ((B, CAP), F32),
            "x2": ((B, T, C), F32), "xn2": ((B, T, C), F32), "q": ((B, T, C), F32), "top_queries": ((B, HU), F32)}


def kernel(**inputs):
    import concourse.bacc as _bacc
    from concourse.bass_utils import run_bass_kernel_spmd as _run

    nc = _bacc.Bacc("TRN2", target_bir_lowering=False, num_devices=1)
    arrays = {name: np.ascontiguousarray(inputs[name]) for name in _INS}
    theta = (1.0 / 10000.0 ** (np.arange(0, D, 2, dtype=np.float32) / D)).astype(np.float32)
    angle = (np.arange(H, dtype=np.float32)[:, None] * theta[None, :]).astype(np.float32)
    arrays["rope_cos"] = np.cos(angle).astype(np.float32).reshape(-1)
    arrays["rope_sin"] = np.sin(angle).astype(np.float32).reshape(-1)
    io = {name: nc.dram_tensor("in_" + name, a.shape, mybir.dt.from_np(a.dtype), kind="ExternalInput").ap()
          for name, a in arrays.items()}
    io["x"] = io["L0_attn_x"]
    for name, (shape, dt) in _SCRATCH.items():
        io[name] = nc.dram_tensor("scratch_" + name, shape, dt, kind="Internal").ap()
    io["out"] = nc.dram_tensor("out_0_dram", (B, T, C), F32, kind="ExternalOutput").ap()
    build_program(nc, io)
    r = _run(nc, [{"in_" + k: v for k, v in arrays.items()}], core_ids=[0])
    return r.results[0]["out_0_dram"]
```

```python
import math
from contextlib import ExitStack

import numpy as np

import concourse.bass as bass
from concourse import mybir

F32 = mybir.dt.float32
BF16 = mybir.dt.bfloat16
I32 = mybir.dt.int32
U32 = mybir.dt.uint32
ALU = mybir.AluOpType
ACT = mybir.ActivationFunctionType
AX = mybir.AxisListType

P = 128
B, T, C = 8, 1024, 256
NT = T // P
KC = C // P
H = 16
D = C // H
HC = H // KC
BANK = 512
NHALF = T // BANK
SCALE = 1.0 / math.sqrt(D)
CAP = 128
DFF = 682
FT = -(-DFF // P)
S = 35
S1 = S + 1
HU = H * S
MT = 5
MR = HU // MT
F2 = 1024
F2T = F2 // P
EPS_LN = 1e-5
EPS_RMS = 1e-6
NEG = -1e30
ROUNDS_C = CAP // 8
ROUNDS_E = -(-S // 8)
DEQUANT_ROUNDS = (7, 9, 11, 13)


class Memory:

    def __init__(self, nc):
        self.nc = nc
        self.stack = ExitStack()
        self.sems = []

    def __enter__(self):
        self.stack.__enter__()
        return self

    def __exit__(self, *e):
        return self.stack.__exit__(*e)

    def sb(self, name, shape, dt=F32):
        return self.stack.enter_context(self.nc.sbuf_tensor(name, shape, dt))

    def sem(self, name):
        s = self.stack.enter_context(self.nc.semaphore(name))
        self.sems.append(s)
        return s

    def clear(self):
        numbers = sorted(s.num for s in self.sems)
        first = numbers[0]
        for n, number in enumerate(numbers):
            if n + 1 == len(numbers) or numbers[n + 1] != number + 1:
                self.nc.sync.sem_clear(range(first, number + 1))
                first = numbers[n + 1] if n + 1 < len(numbers) else None
        self.nc.all_engine_barrier()


def spread(ap, axis, n):
    ap = ap.unsqueeze(axis)
    shape = list(ap.shape)
    shape[axis] = n
    return ap.to_broadcast(shape)


def over_partitions(row, n=P):
    return row.partition_broadcast(n)



def setup_attention(nc, io, w, ps, mem):
    with Memory(nc) as m:
        loaded = m.sem("loaded")
        x_loaded = m.sem("x_loaded")
        made = m.sem("made")
        masked = m.sem("masked")
        zeroed = m.sem("zeroed")
        turned = m.sem("turned")
        cols = m.sem("cols")
        rows = m.sem("rows")

        wqkv_raw = mem["pt"][:, 0, :, :].rearrange("p h n -> p (h n)")[:, 0:KC * 3 * C]\
            .rearrange("p (k n) -> p k n", k=KC)
        brow = mem["yt"][0:1, 0, 0:2 * C]
        brot = mem["yt"][0:1, 1, 0:2 * C]
        ropec = m.sb("ropec", [P, H * D // 2])
        ropes = m.sb("ropes", [P, H * D // 2])
        one = m.sb("one", [1, 1])
        t0 = m.sb("t0", [P, H * D // 2])
        t1 = m.sb("t1", [P, H * D // 2])
        bv = m.sb("bv0", [P, KC])
        bvrep = m.sb("bvrep", [P, KC, P])
        bproj = m.sb("bproj", [P, C])
        iota_i = m.sb("iota_i", [P, T], I32)
        iota_c = m.sb("iota_c", [P, NT], I32)
        ones = m.sb("ones", [P, P])

        loads = [(wqkv_raw[:, :, :], io["L0_attn_W_attn"].rearrange("(k p) n -> p k n", p=P)),
                 (ropec[:, :], over_partitions(io["rope_cos"])),
                 (ropes[:, :], over_partitions(io["rope_sin"])),
                 (brow[:, :], io["L0_attn_b_attn"][0:2 * C].rearrange("(a n) -> a n", a=1)),
                 (bv[:, :], io["L0_attn_b_attn"][2 * C:3 * C].rearrange("(k p) -> p k", p=P)),
                 (bproj[:, :], over_partitions(io["L0_attn_b_proj"])),
                 (w["wproj"][:, :, :], io["L0_attn_W_proj"].rearrange("(k p) n -> p k n", p=P)),
                 (w["router"][:, :], over_partitions(io["L0_ffn_w_router"]))]

        with nc.Block() as block:
            @block.sync
            def _(sp):
                with nc.allow_non_contiguous_dma(reason="a few columns of a bias"):
                    for dst, src in loads:
                        sp.dma_start(dst, src).then_inc(loaded, 16)
                sp.dma_start(mem["x"][:, :, :], io["x"][0].rearrange("(j p) c -> p j c", p=P)).then_inc(x_loaded, 16)
                sp.wait_ge(x_loaded, 16)

            @block.gpsimd
            def _(g):
                nc.gpsimd.memset(ones[:, :], 1.0).then_inc(made, 1)
                nc.gpsimd.memset(w["ident"][:, :], 0.0).then_inc(made, 1)
                nc.gpsimd.memset(w["bdmask"][:, :, :], 1.0).then_inc(made, 1)
                nc.gpsimd.memset(w["mhalf"][:, :], -0.5)
                nc.gpsimd.iota(iota_i[:, :], pattern=[[1, T]], base=0, channel_multiplier=0)
                nc.gpsimd.iota(iota_c[:, :], pattern=[[P, NT]], base=0, channel_multiplier=1)
                g.wait_ge(made, 3)
                nc.gpsimd.affine_select(out=w["ident"][:, :], in_=w["ident"][:, :], compare_op=ALU.not_equal,
                                        fill=1.0, base=0, pattern=[[-1, P]], channel_multiplier=1)
                nc.gpsimd.affine_select(out=w["bdmask"][:, :, :], in_=w["bdmask"][:, :, :], compare_op=ALU.is_ge,
                                        fill=0.0, base=0, pattern=[[-D, HC], [0, S1]],
                                        channel_multiplier=1).then_inc(made, 1)
                g.wait_ge(made, 4)
                nc.gpsimd.affine_select(out=w["bdmask"][:, :, :], in_=w["bdmask"][:, :, :], compare_op=ALU.is_ge,
                                        fill=0.0, base=D - 1, pattern=[[D, HC], [0, S1]],
                                        channel_multiplier=-1).then_inc(made, 1)
                g.wait_ge(zeroed, 1)
                nc.gpsimd.affine_select(out=w["mask_qk"][:, :], in_=w["zeros16"][:, :], compare_op=ALU.is_ge,
                                        fill=NEG, base=0, pattern=[[-1, P]], channel_multiplier=1)
                nc.gpsimd.affine_select(out=w["mask_kq"][:, :], in_=w["zeros16"][:, :], compare_op=ALU.is_ge,
                                        fill=NEG, base=0, pattern=[[1, P]], channel_multiplier=-1)
                nc.gpsimd.affine_select(out=w["mask_f32"][:, :], in_=w["zeros32"][:, :], compare_op=ALU.is_ge,
                                        fill=NEG, base=0, pattern=[[-1, P]], channel_multiplier=1)\
                    .then_inc(masked, 1)
                g.wait_ge(masked, 1)
                nc.gpsimd.memset(mem["sk"][ROWS:P, :, :], 1.0)

            @block.vector
            def _(v):
                nc.vector.memset(w["zeros32"][:, :], 0.0)
                nc.vector.memset(w["zeros16"][:, :], 0.0).then_inc(zeroed, 1)
                nc.vector.memset(mem["val"][:, :, :, D:32], 0.0)
                nc.vector.memset(mem["mx"][:, :, :, :], -3e38)
                nc.vector.drain()
                nc.vector.memset(mem["val"][:, :, :, D:D + 1], 1.0)
                v.wait_ge(loaded, 16 * len(loads))
                for src, dst, n in [(wqkv_raw[:, k, :], w["wqkv"][:, k, :], P) for k in range(KC)] \
                        + [(brow[:, :], brot[:, :], 1)]:
                    for qk in range(2):
                        a = src[:, qk * C:(qk + 1) * C].rearrange("p (n two) -> p n two", two=2)
                        o = dst[:, qk * C:(qk + 1) * C].rearrange("p (n two) -> p n two", two=2)
                        for into, x, y, op in ((0, 0, 1, ALU.subtract), (1, 1, 0, ALU.add)):
                            nc.vector.tensor_tensor(t0[0:n, :], a[:, :, x], ropec[0:n, :], ALU.mult)
                            nc.vector.tensor_tensor(t1[0:n, :], a[:, :, y], ropes[0:n, :], ALU.mult)
                            nc.vector.drain()
                            nc.vector.tensor_tensor(o[:, :, into], t0[0:n, :], t1[0:n, :], op)
                            nc.vector.drain()
                nc.vector.memset(one[:, :], 1.0)
                v.wait_ge(made, 5)
                for k in range(KC):
                    nc.vector.tensor_copy(w["wqkv"][:, k, 2 * C:3 * C], wqkv_raw[:, k, 2 * C:3 * C])
                    nc.vector.tensor_scalar(bvrep[:, k, :], ones[:, :], bv[:, k:k + 1], None, ALU.mult)
                nc.vector.tensor_copy(w["ident16"][:, :], w["ident"][:, :]).then_inc(turned, 1)
                nc.vector.tensor_copy(w["iota_row"][:, :], iota_i[:, :])
                nc.vector.tensor_copy(w["iota_col"][:, :], iota_c[:, :])
                v.wait_ge(cols, 1)
                nc.vector.tensor_copy(w["bqk"][:, :], ps[:, 6, 0:2 * KC])
                v.wait_ge(rows, 1)
                nc.vector.tensor_tensor(w["bias_proj"][:, :], ps[:, 7, 0:C], bproj[:, :], ALU.add)

            @block.tensor
            def _(pe):
                pe.wait_ge(turned, 1)
                for n in range(2 * KC):
                    last = nc.tensor.matmul(ps[:, 6, n:n + 1], brot[0:1, n * P:(n + 1) * P], one[:, :],
                                            start=True, stop=True)
                last.then_inc(cols, 1)
                for k in range(KC):
                    last = nc.tensor.matmul(ps[:, 7, 0:C], bvrep[:, k, :], w["wproj"][:, k, :],
                                            start=(k == 0), stop=(k == KC - 1))
                last.then_inc(rows, 1)
        m.clear()


def setup_rest_and_top_tokens(nc, io, w, ps):
    with Memory(nc) as m:
        loaded = m.sem("loaded2")
        q_loaded = m.sem("q_loaded")
        padded = m.sem("padded")
        flipped = m.sem("flipped")
        flipped_out = m.sem("flipped_out")
        unpacked = m.sem("unpacked")
        scaled = m.sem("scaled")
        sc_full = m.sem("sc_full")
        sc_ready = m.sem("sc_ready")
        sc_out = m.sem("sc_out")
        sc_in = m.sem("sc_in")
        idx_ready = m.sem("idx_ready")
        idx_out = m.sem("idx_out")

        sidx = m.sb("sidx", [P, S], I32)
        sidxf = m.sb("sidxf", [P, S])
        bigq = m.sb("bigq", [P, 2, F2], I32)
        scl = m.sb("scl", [P, 2, F2])
        b2row = m.sb("b2row", [P, C])
        sct = m.sb("sct", [B * NT, P])
        s8 = m.sb("s8", [B, T])
        top = m.sb("top8", [B, CAP])
        idx = m.sb("idx", [B, CAP], U32)
        idxf = m.sb("idxf", [B, CAP])

        turn = [(io["L0_ffn_W_qkv"], 3 * C, w["mod_wqkv"]), (io["L0_ffn_W_out"], C, w["mod_wout"]),
                (io["L0_ffn_W1"], DFF, w["mod_w1"]), (io["L0_ffn_W2"], DFF, w["mod_w2"]),
                (io["L1_attn_Wq"], C, w["ps_wq"]), (io["L1_attn_Wk"], C, w["ps_wk"]),
                (io["L1_attn_Wv"], C, w["ps_wv"]), (io["L1_attn_Wo"], C, w["ps_wo"])]
        stage = [m.sb(f"stage{n}", [P, -(-nrows // P), C]) for n, (_, nrows, _) in enumerate(turn)]
        w3 = m.sb("w3stage", [P, KC, DFF])
        loads = [(w["g1"][:, :], over_partitions(io["L0_ffn_g1"])),
                 (w["g2"][:, :], over_partitions(io["L0_ffn_g2"])),
                 (sidx[:, :], over_partitions(io["L1_attn_sample_idx"])),
                 (w["ps_bq"][:, :], over_partitions(io["L1_attn_bq"])),
                 (w["ps_bv"][:, :], over_partitions(io["L1_attn_bv"])),
                 (w["ps_bo"][:, :], over_partitions(io["L1_attn_bo"])),
                 (b2row[:, :], over_partitions(io["L1_ffn_fc2_bias"])),
                 (w["ps_bk"][:, :], io["L1_attn_bk"].rearrange("(k p) -> p k", p=P)),
                 (w["gamma"][:, :], io["L1_ffn_ln_gamma"].rearrange("(k p) -> p k", p=P)),
                 (w["beta"][:, :], io["L1_ffn_ln_beta"].rearrange("(k p) -> p k", p=P)),
                 (w["fc1_b"][:, :], io["L1_ffn_fc1_bias"].rearrange("(k p) -> p k", p=P)),
                 (w3[:, :, :], io["L0_ffn_W3"].rearrange("(a p) n -> p a n", p=P))]
        pieces = []
        for n, (src, nrows, dst) in enumerate(turn):
            full = nrows // P
            loads.append((stage[n][:, 0:full, :], src[0:full * P, :].rearrange("(a p) c -> p a c", p=P)))
            if nrows % P:
                loads.append((stage[n][0:nrows % P, full, :], src[full * P:nrows, :]))
            for a in range(-(-nrows // P)):
                r = min(P, nrows - a * P)
                for c in range(KC):
                    pieces.append((stage[n][0:r, a, c * P:(c + 1) * P], dst[:, c, a * P:a * P + r], P, r))
        for a in range(FT):
            k = min(P, DFF - a * P)
            for c in range(KC):
                pieces.append((w3[:, c, a * P:a * P + k], w["mod_w3"][0:k, a, c * P:(c + 1) * P], k, P))
        quant = [(io["L1_ffn_fc1_q"][k * P:(k + 1) * P, :], io["L1_ffn_fc1_scales"][k, :], w["fc1"][:, k, :], 1)
                 for k in range(KC)]
        quant += [(io["L1_ffn_fc2_q"][n * 4 * P:(n + 1) * 4 * P, :],
                   io["L1_ffn_fc2_scales"][n * 4:(n + 1) * 4, :].rearrange("k n -> (k n)"),
                   w["fc2"][:, n * 4:(n + 1) * 4, :].rearrange("p k n -> p (k n)"), 4) for n in range(2)]

        with nc.Block() as block:
            @block.sync
            def _(sp):
                sp.wait_ge(sc_ready, 1)
                sp.dma_start(io["scores"], sct[:, :]).then_inc(sc_out, 16)
                sp.wait_ge(sc_out, 16)
                sp.dma_start(s8[:, :], io["scores"].rearrange("(b j) p -> b (j p)", b=B)).then_inc(sc_in, 16)
                with nc.allow_non_contiguous_dma(reason="a few columns of a bias"):
                    for dst, src in loads:
                        sp.dma_start(dst, src).then_inc(loaded, 16)
                for n, (codes, scales, _, k) in enumerate(quant):
                    if n >= 2:
                        sp.wait_ge(scaled, n - 1)
                    sp.dma_start(bigq[:, n % 2, :].rearrange("p (k n) -> p k n", k=k),
                                 codes.rearrange("(k p) n -> p k n", p=P)).then_inc(q_loaded, 16)
                    sp.dma_start(scl[:, n % 2, :], over_partitions(scales)).then_inc(q_loaded, 16)
                    sp.wait_ge(q_loaded, 32 * (n + 1))
                sp.wait_ge(idx_ready, 1)
                sp.dma_start(io["top_tokens"], idxf[:, :]).then_inc(idx_out, 16)
                sp.wait_ge(idx_out, 16)

            @block.gpsimd
            def _(g):
                for n, (_, _, dst, _) in enumerate(quant):
                    g.wait_ge(q_loaded, 32 * (n + 1))
                    nc.gpsimd.tensor_copy(dst, bigq[:, n % 2, :]).then_inc(unpacked, 1)

            @block.vector
            def _(v):
                nc.vector.memset(w["mod_w1"][:, :, DFF:FT * P], 0.0)
                nc.vector.memset(w["mod_w2"][:, :, DFF:FT * P], 0.0)
                nc.vector.memset(w["mod_w3"][:, FT - 1, :], 0.0).then_inc(padded, 1)
                v.wait_ge(sc_full, 1)
                nc.vector.tensor_copy(sct[:, :], ps[0:B * NT, 7, 0:P]).then_inc(sc_ready, 1)
                v.wait_ge(sc_in, 16)
                for n in range(ROUNDS_C):
                    t8 = slice(8 * n, 8 * n + 8)
                    nc.vector.max(top[:, t8], s8[:, :])
                    nc.vector.drain()
                    nc.vector.max_index(idx[:, t8], top[:, t8], s8[:, :])
                    nc.vector.drain()
                    if n < ROUNDS_C - 1:
                        nc.vector.match_replace(s8[:, :], top[:, t8], s8[:, :], -3e38)
                        nc.vector.drain()
                    if n in DEQUANT_ROUNDS:
                        tile = DEQUANT_ROUNDS.index(n)
                        dst = quant[tile][2]
                        v.wait_ge(unpacked, tile + 1)
                        nc.vector.scalar_tensor_tensor(dst, dst, -128.0, scl[:, tile % 2, :],
                                                       ALU.add, ALU.mult).then_inc(scaled, 1)
                nc.vector.tensor_copy(idxf[:, :], idx[:, :]).then_inc(idx_ready, 1)
                nc.vector.tensor_scalar(w["fc2"][:, :, :], w["fc2"][:, :, :], 0.5, None, ALU.mult)
                v.wait_ge(loaded, 16 * len(loads))
                nc.vector.tensor_scalar(w["fc2_b"][:, :], b2row[:, :], 0.5, None, ALU.mult)
                nc.vector.tensor_copy(sidxf[:, :], sidx[:, :])
                nc.vector.drain()
                for j in range(NT):
                    nc.vector.tensor_scalar(w["onehot_s"][:, j, :], sidxf[:, :], w["iota_col"][:, j:j + 1], None,
                                            ALU.is_equal)

            @block.tensor
            def _(pe):
                nc.tensor.transpose(ps[0:B * NT, 7, 0:P], w["scores"][:, :, :].rearrange("p b j -> p (b j)"),
                                    w["ident"][:, :]).then_inc(sc_full, 1)
                pe.wait_ge(loaded, 16 * len(loads))
                for n, (src, _, k, r) in enumerate(pieces):
                    if n >= 4:
                        pe.wait_ge(flipped_out, n - 3)
                    nc.tensor.transpose(ps[0:k, n % 4, 0:r], src,
                                        w["ident"][0:src.shape[0], 0:src.shape[0]]).then_inc(flipped, 1)

            @block.scalar
            def _(a):
                a.wait_ge(padded, 1)
                for n, (_, dst, k, r) in enumerate(pieces):
                    a.wait_ge(flipped, n + 1)
                    nc.scalar.copy(dst, ps[0:k, n % 4, 0:r]).then_inc(flipped_out, 1)
        m.clear()


TABLES = {
    "ident": ([P, P], F32), "ident16": ([P, P], BF16), "mask_qk": ([P, P], BF16), "mask_kq": ([P, P], BF16),
    "zeros16": ([P, P], BF16), "zeros32": ([P, P], F32), "mask_f32": ([P, P], F32),
    "bdmask": ([P, HC, S1], F32), "mhalf": ([P, NT], F32),
    "iota_row": ([P, T], F32), "iota_col": ([P, NT], F32),
    "scores": ([P, B, NT], F32),
}
ATTENTION_WEIGHTS = {
    "wqkv": ([P, KC, 3 * C], F32), "bqk": ([P, 2 * KC], F32), "wproj": ([P, KC, C], F32),
    "bias_proj": ([P, C], F32), "router": ([P, C], F32),
}
MOD_WEIGHTS = {
    "g1": ([P, C], F32), "g2": ([P, C], F32), "onehot_s": ([P, NT, S], F32),
    "mod_wqkv": ([P, KC, 3 * C], F32), "mod_wout": ([P, KC, C], F32),
    "mod_w1": ([P, KC, FT * P], F32), "mod_w2": ([P, KC, FT * P], F32), "mod_w3": ([P, FT, C], F32),
    "measure": ([P, NT, B * H], F32),
}
OTHER_WEIGHTS = {
    "ps_wq": ([P, KC, C], F32), "ps_wk": ([P, KC, C], F32), "ps_wv": ([P, KC, C], F32), "ps_wo": ([P, KC, C], F32),
    "ps_bq": ([P, C], F32), "ps_bv": ([P, C], F32), "ps_bo": ([P, C], F32), "ps_bk": ([P, KC], F32),
    "gamma": ([P, KC], F32), "beta": ([P, KC], F32),
    "fc1": ([P, KC, F2], F32), "fc1_b": ([P, F2T], F32), "fc2": ([P, F2T, C], F32), "fc2_b": ([P, C], F32),
}



SETS = 4
HS = H // SETS
PARTS = 3
Q_PARTS = (0, 0, 0, 1, 1, 2)
K_PARTS = (0, 1, 2, 0, 1, 0)
ROWS = len(Q_PARTS) * D
ROWS_M = ROWS + PARTS
SET_CHUNK = SETS // KC

MU = [(hh, i, n, min(BANK, (i + 1) * P - n * BANK))
      for hh in range(HS) for i in range(NT) for n in range(NHALF) if (i + 1) * P > n * BANK]
EU = [(n, j, max(n * BANK, j * P), (n + 1) * BANK - max(n * BANK, j * P))
      for n in range(NHALF) for j in range((n + 1) * BANK // P)]

EARLY = 12
RING = (0, 1, 7)
RING_STEPS = ("max", "rows", "t1", "t2", "proj", "xt", "qk", "v")


def steps_of_turn(tail, attention, head):
    if not attention:
        order = []
        if tail:
            order += [("load_xr",)] + [("t1", i) for i in range(NT)]
            for i in range(NT + 1):
                order += [("t2", i)] if i < NT else []
                order += [("proj", i - 1)] if i else []
            order += [(kind, j) for kind in ("a_norm", "x1_stat", "xn1", "score") for j in range(NT)] + [("store",)]
        if head:
            order += [(kind, j) for kind in ("x_stat", "x_norm") for j in range(NT)] + [("xt", n, k) for n in range(NHALF) for k in range(KC)]
            for r in range(2):
                order += [("qk", r, 0, n) for n in range(NHALF)] + [("parts", r, 0, n) for n in range(NHALF)]
            order += [("stack", 0)] + [("v", 0, n) for n in range(NHALF)]
            order += [("max", SETS, n) for n in range(len(MU))] + [("rows", SETS), ("nm", SETS)]
            order += [("max", SETS + 1, n) for n in range(EARLY)]
        return order
    n_eu = len(EU)
    beside = {g: [] for g in range(SETS * n_eu)}

    def put(at, *steps):
        beside[at].extend(steps)

    tiles = range(NT)
    if head:
        put(0, ("load_x",))
    if tail:
        put(0, ("load_xr",))
        for i in tiles:
            put(i // 2, ("t1", i))
            put(9 + i, ("t2", i))
            put(10 + i, ("proj", i))
    put(1, ("qk", 0, 1, 0), ("qk", 0, 1, 1))
    put(2, ("parts", 0, 1, 0), ("qk", 1, 1, 0))
    put(3, ("parts", 0, 1, 1), ("qk", 1, 1, 1))
    put(4, ("parts", 1, 1, 0), ("v", 1, 0))
    put(5, ("parts", 1, 1, 1), ("stack", 1), ("v", 1, 1))
    if head:
        for t in range(4):
            put(9 + t, *[("x_stat", j) for j in tiles[2 * t:2 * t + 2]])
            put(15 + t, *[("x_norm", j) for j in tiles[2 * t:2 * t + 2]])
        put(19, ("xt", 0, 0), ("xt", 0, 1))
        put(20, ("xt", 1, 0), ("xt", 1, 1))
        put(23, ("qk", 0, 0, 0), ("qk", 0, 0, 1))
        put(24, ("qk", 1, 0, 0), ("qk", 1, 0, 1))
        put(25, ("parts", 0, 0, 0))
        put(26, ("parts", 0, 0, 1), ("v", 0, 0))
        put(27, ("parts", 1, 0, 0), ("v", 0, 1))
        put(28, ("parts", 1, 0, 1))
        put(29, ("stack", 0))
    if tail:
        for t in range(4):
            put(19 + t, *[("a_norm", j) for j in tiles[2 * t:2 * t + 2]])
            put(22 + t, *[("x1_stat", j) for j in tiles[2 * t:2 * t + 2]])
            put(34 + t, *[("xn1", j) for j in tiles[2 * t:2 * t + 2]])
            put(36 + t, *[("score", j) for j in tiles[2 * t:2 * t + 2]])
        put(41, ("store",))
    for s in range(SETS):
        if s + 1 < SETS or head:
            done = EARLY
            for g in range(8):
                upto = EARLY + (len(MU) - EARLY) * (g + 1) // 8
                put(s * n_eu + g, *[("max", s + 1, n) for n in range(done, upto)])
                done = upto
            put(s * n_eu + 8, ("rows", s + 1), ("nm", s + 1))
        if s + 2 < SETS or head:
            for n in range(EARLY):
                put(s * n_eu + 9 + 3 * n // EARLY, ("max", s + 2, n))
    order = []
    for t in range(SETS * n_eu + 1):
        rest = beside.get(t, [])
        cut = [rest[len(rest) * n // 3:len(rest) * (n + 1) // 3] for n in range(3)]
        if t < SETS * n_eu:
            for pair in range(2):
                order += [("exp", *divmod(t, n_eu), pair)] + cut[pair]
        if t:
            s, g = divmod(t - 1, n_eu)
            order.append(("av", s, g))
            if g == n_eu - 1 or EU[g + 1][0] != EU[g][0]:
                order.append(("y_out", s, EU[g][0]))
        order += cut[2]
    return order


def layer_stats(nc, stats, mv, tile, j):
    nc.vector.bn_stats(stats[:, j, :], tile)
    nc.vector.drain()
    return nc.vector.bn_aggr(mv[:, j, :], stats[:, j, :])


def rstd_of(nc, var, out, w, n, eps, ready, tmp, count):
    nc.gpsimd.tensor_scalar(tmp, var, eps, None, ALU.add).then_inc(ready, 1)
    nc.gpsimd.wait_ge(ready, count)
    return nc.gpsimd.tensor_tensor(out, tmp, w["mhalf"][:, 0:n], ALU.pow)


def rstd_and_shift(nc, moments, rstd, shift, w, tmp, ready, count):
    nc.gpsimd.tensor_scalar(tmp, moments[:, :, 1], EPS_LN, None, ALU.add).then_inc(ready, 1)
    nc.gpsimd.tensor_scalar(shift, moments[:, :, 0], -1.0, None, ALU.mult).then_inc(ready, 1)
    nc.gpsimd.wait_ge(ready, count + 2)
    nc.gpsimd.tensor_tensor(rstd, tmp, w["mhalf"][:, 0:NT], ALU.pow).then_inc(ready, 1)
    nc.gpsimd.wait_ge(ready, count + 3)
    return nc.gpsimd.tensor_tensor(shift, shift, rstd, ALU.mult)


def attention_loop(nc, io, w, ps):
    with Memory(nc) as m:
        mem = {
            "x": m.sb("x", [P, NT, C]),
            "hstats": m.sb("hstats", [P, NT, 6]), "hmv": m.sb("hmv", [P, NT, 2]),
            "hrstd": m.sb("hrstd", [P, NT]), "htmp": m.sb("htmp", [P, NT]), "hshift": m.sb("hshift", [P, NT]),
            "xnt": m.sb("xnt", [P, KC, T]),
            "qk": m.sb("qk", [P, 2, T]),
            "part": m.sb("part", [P, 2, PARTS, T], BF16),
            "sq": m.sb("sq", [P, H, T], BF16),
            "sk": m.sb("sk", [P, H, T], BF16),
            "val": m.sb("val", [P, NT, H, 32]),
            "mx": m.sb("mx", [P, HS, NT, NHALF]),
            "nm": m.sb("nm", [P, HS, NT]),
            "nmr": m.sb("nmr", [HS * NT, P]),
            "nmp": m.sb("nmp", [HS * NT, PARTS, P], BF16),
            "pt": m.sb("pt", [P, 3, HS, BANK]),
            "yt": m.sb("yt", [P, SETS, T]),
            "rs": m.sb("rs", [P, 2, H]),
            "att": m.sb("att", [P, NT, C]),
            "ynt": m.sb("ynt", [P, 2, KC, P]),
            "xr": m.sb("xr", [P, NT, C]),
            "tstats": m.sb("tstats", [P, NT, 6]), "tmv": m.sb("tmv", [P, NT, 2]),
            "trstd": m.sb("trstd", [P, NT]), "ttmp": m.sb("ttmp", [P, NT]), "tshift": m.sb("tshift", [P, NT]),
            "sc": m.sb("sc", [P, NT]), "junk": m.sb("junk", [P, NT, C], BF16),
        }
        names = """x_in x_stat head_step x_rstd x_ready
            parts_step nm_ready nmp_ready nm_out s_full exp_done av_done yt_ready xr_in a_stat tail_step a_rstd a_norm x1_ready x1_stat x1_rstd xn1_ready stored""".split()
        e = {n: m.sem("a_" + n) for n in names}
        e["bank_filled"] = [m.sem(f"a_bank_filled{n}") for n in range(len(RING))]
        e["bank_taken"] = [m.sem(f"a_bank_taken{n}") for n in range(len(RING))]
        e["parts_ready"] = [m.sem("a_q_parts_ready"), m.sem("a_k_parts_ready")]
        e["parts_out"] = [m.sem(f"a_parts_out{n}") for n in range(2 * KC)]
        e["stack_in"] = [m.sem(f"a_stack_in{n}") for n in range(KC)]
        e["nm_in"] = [m.sem(f"a_nm_in{s}") for s in range(SETS + 1)]

        setup_attention(nc, io, w, ps, mem)
        attention_turn(nc, io, w, ps, mem, e, -1, tail=False, attention=False, head=True)
        m.clear()
        attention_turn(nc, io, w, ps, mem, e, 0, tail=False, attention=True, head=True)
        m.clear()
        with nc.Fori(1, B - 1) as b:
            attention_turn(nc, io, w, ps, mem, e, b, tail=True, attention=True, head=True)
            m.clear()
        attention_turn(nc, io, w, ps, mem, e, B - 1, tail=True, attention=True, head=False)
        m.clear()
        attention_turn(nc, io, w, ps, mem, e, B, tail=True, attention=False, head=False)
        m.clear()


def attention_turn(nc, io, w, ps, mem, e, b, tail, attention, head):
    order = steps_of_turn(tail, attention, head)
    numbers = {step: k for k, step in enumerate(s for s in order if s[0] in RING_STEPS)}
    filled, taken = e["bank_filled"], e["bank_taken"]
    n_eu = len(EU)
    x, xnt, qk, part, sq, sk, val = (mem[n] for n in ("x", "xnt", "qk", "part", "sq", "sk", "val"))
    mx, nm, nmr, nmp, pt, yt = (mem[n] for n in ("mx", "nm", "nmr", "nmp", "pt", "yt"))
    att, ynt, xr, sc = (mem[n] for n in ("att", "ynt", "xr", "sc"))
    R = HS * NT

    nth = {step: [s for s in order if s[0] == step[0]].index(step) for step in order}

    def bank_use(step):
        return numbers[step] % len(RING), numbers[step] // len(RING)

    def halves_before(r, chunk, n):
        same = [s[1:] for s in order if s[0] == "parts" and s[1] == r]
        return same.index((r, chunk, n))

    def chunk_of(s):
        return s % SETS // SET_CHUNK

    with nc.Block() as block:
        @block.sync
        def _(sp):
            for step in order:
                kind, a = step[0], step[1:]
                if kind == "load_x":
                    sp.dma_start(x[:, :, :], io["x"][b + 1].rearrange("(j p) c -> p j c", p=P))\
                        .then_inc(e["x_in"], 16)
                elif kind == "load_xr":
                    sp.dma_start(xr[:, :, :], io["x"][b - 1].rearrange("(j p) c -> p j c", p=P))\
                        .then_inc(e["xr_in"], 16)
                elif kind == "parts":
                    r, chunk, n = a
                    if n == NHALF - 1:
                        sp.wait_ge(e["parts_ready"][r], halves_before(*a) + 1)
                        sp.dma_start(io["parts"][2 * chunk + r].rearrange("a r t -> r a t"),
                                     part[:, r, :, :]).then_inc(e["parts_out"][2 * chunk + r], 16)
                elif kind == "stack":
                    chunk, = a
                    if attention and chunk == 0:
                        sp.wait_ge(e["exp_done"], 2 * n_eu * SET_CHUNK)
                    for r, dst, use in ((0, sq, Q_PARTS), (1, sk, K_PARTS)):
                        sp.wait_ge(e["parts_out"][2 * chunk + r], 16)
                        for c, p_ in enumerate(use):
                            sp.dma_start(dst[c * D:(c + 1) * D, chunk * HC:(chunk + 1) * HC, :],
                                         io["parts"][2 * chunk + r, p_].rearrange("(h d) t -> d h t", d=D))\
                                .then_inc(e["stack_in"][chunk], 16)
                elif kind == "nm":
                    s, = a
                    h0 = s % SETS * HS
                    sp.wait_ge(e["nmp_ready"], nth[step] + 1)
                    sp.dma_start(io["nm_parts"].rearrange("a r q -> r a q"), nmp[:, :, :]).then_inc(e["nm_out"], 16)
                    sp.wait_ge(e["nm_out"], 16 * (nth[step] + 1))
                    sp.dma_start(sq[ROWS:ROWS_M, h0:h0 + HS, :],
                                 io["nm_parts"].rearrange("a (h i) q -> a h (i q)", h=HS)).then_inc(e["nm_in"][s], 16)
                    sp.wait_ge(e["nm_in"][s], 16)
                elif kind == "store":
                    sp.wait_ge(e["x1_ready"], NT)
                    sp.dma_start(io["x1"][b - 1].rearrange("(j p) c -> p j c", p=P), xr[:, :, :])\
                        .then_inc(e["stored"], 16)
                    sp.wait_ge(e["xn1_ready"], NT)
                    sp.dma_start(io["xn1"][b - 1].rearrange("(j p) c -> p j c", p=P), att[:, :, :])\
                        .then_inc(e["stored"], 16)
            if tail:
                sp.wait_ge(e["stored"], 32)

        @block.gpsimd
        def _(g):
            for step in order:
                kind, a = step[0], step[1:]
                if kind == "parts" and a[0] == 0:
                    r, chunk, n = a
                    half = slice(n * BANK, (n + 1) * BANK)
                    slot, uses = bank_use(("qk", r, chunk, n))
                    g.wait_ge(taken[slot], uses + 1)
                    done = halves_before(*a)
                    if done >= NHALF:
                        g.wait_ge(e["parts_out"][2 * (1 - chunk) + r], 16)
                    nc.gpsimd.tensor_copy(part[:, r, 0, half], qk[:, r, half]).then_inc(e["parts_step"], 1)
                    g.wait_ge(e["parts_step"], 3 * done + 1)
                    nc.gpsimd.tensor_tensor(qk[:, r, half], qk[:, r, half], part[:, r, 0, half], ALU.subtract)\
                        .then_inc(e["parts_step"], 1)
                    g.wait_ge(e["parts_step"], 3 * done + 2)
                    nc.gpsimd.tensor_copy(part[:, r, 1, half], qk[:, r, half]).then_inc(e["parts_step"], 1)
                    g.wait_ge(e["parts_step"], 3 * done + 3)
                    nc.gpsimd.tensor_tensor(part[:, r, 2, half], qk[:, r, half], part[:, r, 1, half], ALU.subtract)\
                        .then_inc(e["parts_ready"][r], 1)
                elif kind == "x_norm" and step[1] == 0:
                    g.wait_ge(e["x_stat"], 1)
                    rstd_and_shift(nc, mem["hmv"], mem["hrstd"][:, :], mem["hshift"][:, :], w, mem["htmp"][:, :],
                                   e["head_step"], 0).then_inc(e["x_rstd"], 1)
                elif kind == "a_norm" and step[1] == 0:
                    g.wait_ge(e["a_stat"], 1)
                    rstd_and_shift(nc, mem["tmv"], mem["trstd"][:, :], mem["tshift"][:, :], w, mem["ttmp"][:, :],
                                   e["tail_step"], 0).then_inc(e["a_rstd"], 1)
                    g.wait_ge(e["xr_in"], 16)
                    for j in range(NT):
                        g.wait_ge(e["a_norm"], j + 1)
                        nc.gpsimd.tensor_tensor(xr[:, j, :], xr[:, j, :], att[:, j, :], ALU.add)\
                            .then_inc(e["x1_ready"], 1)
                elif kind == "xn1" and step[1] == 0:
                    g.wait_ge(e["x1_stat"], 1)
                    rstd_and_shift(nc, mem["tmv"], mem["trstd"][:, :], mem["tshift"][:, :], w, mem["ttmp"][:, :],
                                   e["tail_step"], 3).then_inc(e["x1_rstd"], 1)

        @block.vector
        def _(v):
            for step in order:
                kind, a = step[0], step[1:]
                if kind in RING_STEPS:
                    slot, uses = bank_use(step)
                if kind == "max":
                    s, n_unit = a
                    hh, i, half, n = MU[n_unit]
                    v.wait_ge(filled[slot], uses + 1)
                    nc.vector.reduce_max(mx[:, hh, i, half:half + 1], ps[:, RING[slot], 0:n], AX.X)\
                        .then_inc(taken[slot], 1)
                elif kind == "rows":
                    nc.vector.drain()
                    nc.vector.tensor_reduce(nm[:, :, :], mx[:, :, :, :], AX.X, ALU.max, negate=True)\
                        .then_inc(e["nm_ready"], 1)
                    v.wait_ge(filled[slot], uses + 1)
                    if nth[step]:
                        v.wait_ge(e["nm_out"], 16 * nth[step])
                    nc.vector.tensor_copy(nmr[:, :], ps[0:R, RING[slot], 0:P]).then_inc(taken[slot], 1)
                    nc.vector.drain()
                    nc.vector.tensor_copy(nmp[:, 0, :], nmr[:, :])
                    nc.vector.drain()
                    nc.vector.tensor_tensor(nmr[:, :], nmr[:, :], nmp[:, 0, :], ALU.subtract)
                    nc.vector.drain()
                    nc.vector.tensor_copy(nmp[:, 1, :], nmr[:, :])
                    nc.vector.drain()
                    nc.vector.tensor_tensor(nmp[:, 2, :], nmr[:, :], nmp[:, 1, :], ALU.subtract)\
                        .then_inc(e["nmp_ready"], 1)
                elif kind == "parts" and a[0] == 1:
                    r, chunk, n = a
                    half = slice(n * BANK, (n + 1) * BANK)
                    slot, uses = bank_use(("qk", r, chunk, n))
                    v.wait_ge(taken[slot], uses + 1)
                    if halves_before(*a) >= NHALF:
                        v.wait_ge(e["parts_out"][2 * (1 - chunk) + r], 16)
                    nc.vector.tensor_copy(part[:, r, 0, half], qk[:, r, half])
                    nc.vector.drain()
                    nc.vector.tensor_tensor(qk[:, r, half], qk[:, r, half], part[:, r, 0, half], ALU.subtract)
                    nc.vector.drain()
                    nc.vector.tensor_copy(part[:, r, 1, half], qk[:, r, half])
                    nc.vector.drain()
                    nc.vector.tensor_tensor(part[:, r, 2, half], qk[:, r, half], part[:, r, 1, half], ALU.subtract)\
                        .then_inc(e["parts_ready"][r], 1)
                elif kind == "x_stat":
                    j, = a
                    if attention:
                        v.wait_ge(e["x_in"], 16)
                    last = layer_stats(nc, mem["hstats"], mem["hmv"], x[:, j, :], j)
                    if j == NT - 1:
                        last.then_inc(e["x_stat"], 1)
                elif kind == "t1":
                    i, = a
                    v.wait_ge(filled[slot], uses + 1)
                    yq = ps[:, RING[slot], :].rearrange("p (h d) -> p h d", d=32)
                    nc.vector.reciprocal(mem["rs"][:, i % 2, :], yq[:, :, D])
                    nc.vector.drain()
                    nc.vector.tensor_tensor(att[:, i, :].rearrange("p (h d) -> p h d", d=D), yq[:, :, 0:D],
                                            spread(mem["rs"][:, i % 2, :], 2, D), ALU.mult)\
                        .then_inc(taken[slot], 1)
                elif kind == "proj":
                    i, = a
                    v.wait_ge(filled[slot], uses + 1)
                    nc.vector.tensor_tensor(att[:, i, :], ps[:, RING[slot], 0:C], w["bias_proj"][:, :], ALU.add)\
                        .then_inc(taken[slot], 1)
                    nc.vector.drain()
                    last = layer_stats(nc, mem["tstats"], mem["tmv"], att[:, i, :], i)
                    if i == NT - 1:
                        last.then_inc(e["a_stat"], 1)
                elif kind == "x1_stat":
                    j, = a
                    v.wait_ge(e["x1_ready"], j + 1)
                    last = layer_stats(nc, mem["tstats"], mem["tmv"], xr[:, j, :], j)
                    if j == NT - 1:
                        last.then_inc(e["x1_stat"], 1)
                elif kind == "score":
                    j, = a
                    v.wait_ge(e["xn1_ready"], j + 1)
                    nc.vector.scalar_tensor_tensor(mem["junk"][:, j, :], att[:, j, :], 1.0, w["router"][:, :],
                                                   ALU.mult, ALU.mult, accum_out=sc[:, j:j + 1])
                    if j == NT - 1:
                        nc.vector.drain()
                        nc.vector.tensor_copy(w["scores"][:, bass.ds(b - 1, 1), :], spread(sc[:, :], 1, 1))

        @block.tensor
        def _(pe):
            for step in order:
                kind, a = step[0], step[1:]
                if kind in RING_STEPS:
                    slot, uses = bank_use(step)
                    bank = RING[slot]
                    if uses:
                        pe.wait_ge(taken[slot], uses)
                if kind == "max":
                    s, n_unit = a
                    hh, i, half, n = MU[n_unit]
                    h = s % SETS * HS + hh
                    if n_unit == 0 and (s == SETS or s == SET_CHUNK):
                        pe.wait_ge(e["stack_in"][chunk_of(s)], 16 * 2 * len(Q_PARTS))
                    diag = (i * P) // BANK == half
                    last = nc.tensor.matmul(ps[:, bank, 0:n], sq[0:ROWS, h, i * P:(i + 1) * P],
                                            sk[0:ROWS, h, half * BANK:half * BANK + n], start=True, stop=not diag)
                    if diag:
                        last = nc.tensor.matmul(ps[:, bank, n - P:n], w["ident16"][:, :], w["mask_qk"][:, :],
                                                start=False, stop=True)
                    last.then_inc(filled[slot], 1)
                elif kind == "rows":
                    pe.wait_ge(e["nm_ready"], nth[step] + 1)
                    nc.tensor.transpose(ps[0:R, bank, 0:P], nm[:, :, :].rearrange("p h i -> p (h i)"),
                                        w["ident"][:, :]).then_inc(filled[slot], 1)
                elif kind == "exp":
                    s, g, pair = a
                    half, j, q0, n = EU[g]
                    if g == 0 and s:
                        pe.wait_ge(e["nm_in"][s], 16)
                    t = 2 * (s * n_eu + g) + pair
                    if t >= 2:
                        pe.wait_ge(e["exp_done"], t - 1)
                    for f in range(2):
                        h = s * HS + 2 * pair + f
                        bank = 2 + 2 * (t % 2) + f
                        diag = q0 == j * P
                        last = nc.tensor.matmul(ps[:, bank, 0:n], sk[0:ROWS_M, h, j * P:(j + 1) * P],
                                                sq[0:ROWS_M, h, q0:q0 + n], start=True, stop=not diag)
                        if diag:
                            last = nc.tensor.matmul(ps[:, bank, 0:P], w["ident16"][:, :], w["mask_kq"][:, :],
                                                    start=False, stop=True)
                    last.then_inc(e["s_full"], 1)
                elif kind == "av":
                    s, g = a
                    half, j, q0, n = EU[g]
                    t = s * n_eu + g
                    if j == 0 and NHALF * s + half:
                        pe.wait_ge(e["yt_ready"], NHALF * s + half)
                    if t == SET_CHUNK * n_eu:
                        for done in [("v", 1, n_) for n_ in range(NHALF)]:
                            pe.wait_ge(taken[bank_use(done)[0]], bank_use(done)[1] + 1)
                    pe.wait_ge(e["exp_done"], 2 * t + 2)
                    c0 = q0 - half * BANK
                    for hh in range(HS):
                        last = nc.tensor.matmul(ps[32 * hh:32 * hh + 32, 6, c0:c0 + n], val[:, j, s * HS + hh, :],
                                                pt[:, t % 3, hh, 0:n], start=(j == 0),
                                                stop=(q0 + n == (j + 1) * P), skip_group_check=True)
                    last.then_inc(e["av_done"], 1)
                elif kind == "xt":
                    n, k = a
                    pe.wait_ge(e["x_ready"], 4 * (n + 1))
                    for t in range(4):
                        last = nc.tensor.transpose(ps[:, bank, t * P:(t + 1) * P],
                                                   x[:, 4 * n + t, k * P:(k + 1) * P], w["ident"][:, :])
                    last.then_inc(filled[slot], 1)
                elif kind == "qk":
                    r, chunk, n = a
                    if chunk == 0:
                        for done in [("xt", n_, k_) for n_ in range(NHALF) for k_ in range(KC)]:
                            pe.wait_ge(taken[bank_use(done)[0]], bank_use(done)[1] + 1)
                    col = r * C + chunk * P
                    for k in range(KC):
                        last = nc.tensor.matmul(ps[:, bank, :], w["wqkv"][:, k, col:col + P],
                                                xnt[:, k, n * BANK:(n + 1) * BANK], start=(k == 0), stop=(k == KC - 1))
                    last.then_inc(filled[slot], 1)
                elif kind == "v":
                    chunk, n = a
                    if chunk == 0:
                        for done in [("xt", n_, k_) for n_ in range(NHALF) for k_ in range(KC)]:
                            pe.wait_ge(taken[bank_use(done)[0]], bank_use(done)[1] + 1)
                    col = 2 * C + chunk * P
                    for t in range(4):
                        for k in range(KC):
                            j = 4 * n + t
                            last = nc.tensor.matmul(ps[:, bank, t * P:(t + 1) * P],
                                                    xnt[:, k, j * P:(j + 1) * P], w["wqkv"][:, k, col:col + P],
                                                    start=(k == 0), stop=(k == KC - 1))
                    last.then_inc(filled[slot], 1)
                elif kind == "t1":
                    i, = a
                    for s in range(SETS):
                        last = nc.tensor.transpose(ps[:, bank, s * P:(s + 1) * P],
                                                   yt[:, s, i * P:(i + 1) * P], w["ident"][:, :])
                    last.then_inc(filled[slot], 1)
                elif kind == "t2":
                    i, = a
                    slot1, uses1 = bank_use(("t1", i))
                    pe.wait_ge(taken[slot1], uses1 + 1)
                    for k in range(KC):
                        last = nc.tensor.transpose(ps[:, bank, k * P:(k + 1) * P],
                                                   att[:, i, k * P:(k + 1) * P], w["ident"][:, :])
                    last.then_inc(filled[slot], 1)
                elif kind == "proj":
                    i, = a
                    slot2, uses2 = bank_use(("t2", i))
                    pe.wait_ge(taken[slot2], uses2 + 1)
                    for k in range(KC):
                        last = nc.tensor.matmul(ps[:, bank, 0:C], ynt[:, i % 2, k, :], w["wproj"][:, k, :],
                                                start=(k == 0), stop=(k == KC - 1))
                    last.then_inc(filled[slot], 1)

        @block.scalar
        def _(act):
            for step in order:
                kind, a = step[0], step[1:]
                if kind in RING_STEPS:
                    slot, uses = bank_use(step)
                if kind == "exp":
                    s, g, pair = a
                    half, j, q0, n = EU[g]
                    u = s * n_eu + g
                    t = 2 * u + pair
                    act.wait_ge(e["s_full"], t + 1)
                    if u >= 3:
                        act.wait_ge(e["av_done"], u - 2)
                    bank = 2 + 2 * (t % 2)
                    nc.scalar.activation(pt[:, u % 3, 2 * pair:2 * pair + 2, 0:n], ps[:, bank:bank + 2, 0:n],
                                         ACT.Exp, scale=SCALE).then_inc(e["exp_done"], 1)
                elif kind == "y_out":
                    s, half = a
                    act.wait_ge(e["av_done"], s * n_eu + sum(1 for u in EU if u[0] <= half))
                    if tail and s == 0:
                        for done in [("t1", i) for i in range(NT)]:
                            act.wait_ge(taken[bank_use(done)[0]], bank_use(done)[1] + 1)
                    nc.scalar.copy(yt[:, s, half * BANK:(half + 1) * BANK], ps[:, 6, :]).then_inc(e["yt_ready"], 1)
                elif kind == "x_norm":
                    j, = a
                    act.wait_ge(e["x_rstd"], 1)
                    nc.scalar.activation(x[:, j, :], x[:, j, :], ACT.Identity, scale=mem["hrstd"][:, j:j + 1],
                                         bias=mem["hshift"][:, j:j + 1]).then_inc(e["x_ready"], 1)
                elif kind == "a_norm":
                    j, = a
                    act.wait_ge(e["a_rstd"], 1)
                    nc.scalar.activation(att[:, j, :], att[:, j, :], ACT.Identity, scale=mem["trstd"][:, j:j + 1],
                                         bias=mem["tshift"][:, j:j + 1]).then_inc(e["a_norm"], 1)
                elif kind == "xn1":
                    j, = a
                    act.wait_ge(e["x1_rstd"], 1)
                    nc.scalar.activation(att[:, j, :], xr[:, j, :], ACT.Identity, scale=mem["trstd"][:, j:j + 1],
                                         bias=mem["tshift"][:, j:j + 1]).then_inc(e["xn1_ready"], 1)
                elif kind == "xt":
                    n, k = a
                    act.wait_ge(filled[slot], uses + 1)
                    nc.scalar.copy(xnt[:, k, n * BANK:(n + 1) * BANK], ps[:, RING[slot], :])\
                        .then_inc(taken[slot], 1)
                elif kind == "qk":
                    r, chunk, n = a
                    act.wait_ge(filled[slot], uses + 1)
                    if halves_before(*a) >= NHALF:
                        act.wait_ge(e["parts_ready"][r], halves_before(*a) - NHALF + 1)
                    nc.scalar.activation(qk[:, r, n * BANK:(n + 1) * BANK], ps[:, RING[slot], :], ACT.Identity,
                                         bias=w["bqk"][:, r * KC + chunk:r * KC + chunk + 1])\
                        .then_inc(taken[slot], 1)
                elif kind == "v":
                    chunk, n = a
                    act.wait_ge(filled[slot], uses + 1)
                    if attention and chunk == 0:
                        act.wait_ge(e["av_done"], SET_CHUNK * n_eu)
                    nc.scalar.copy(val[:, 4 * n:4 * n + 4, chunk * HC:(chunk + 1) * HC, 0:D],
                                   ps[:, RING[slot], :].rearrange("p (j h d) -> p j h d", j=4, d=D))\
                        .then_inc(taken[slot], 1)
                elif kind == "t2":
                    i, = a
                    act.wait_ge(filled[slot], uses + 1)
                    if i >= 2:
                        slot2, uses2 = bank_use(("proj", i - 2))
                        act.wait_ge(filled[slot2], uses2 + 1)
                    nc.scalar.copy(ynt[:, i % 2, :, :],
                                   ps[:, RING[slot], 0:C].rearrange("p (k t) -> p k t", k=KC))\
                        .then_inc(taken[slot], 1)



SLOTS = 4
PAIR_STEPS = ("xs", "hnt", "q_t", "k_t", "val", "s", "pt", "o", "ot", "xa", "hnt2", "gate", "up", "ff",
              "put", "xt", "xst", "ks", "q", "qt", "ms")


def mod_steps(pick, block_out, post):
    tiles = range(NT)
    of_pick = {"oh", "xs", "hn", "hnt", "k_t", "q_t", "val", "s", "less", "exp", "sum"}
    of_block = {"keep_xs", "pt", "o", "ot", "xa", "hn2", "hnt2", "gate", "up", "ff"}
    order = [("keep_xs",), ("pt", 0), ("oht",)] + [("oh", j) for j in tiles]
    order += [("pt", 1), ("put", 0), ("o",), ("put", 1), ("ot",), ("xs",)] + [("a_norm", j) for j in tiles]
    order += [("hn",), ("xa",), ("hnt",), ("hn2",), ("k_t",), ("q_t",), ("val",), ("hnt2",)]
    order += [("x2_stat", j) for j in tiles] + [("gate",), ("up",), ("s", 0)] + [("xn2", j) for j in tiles]
    order += [("xt", 0), ("s", 1), ("xt", 1), ("ff",), ("xst",), ("q", 0), ("less",), ("ks",), ("q", 1)]
    order += [("qt", 0), ("qt", 1), ("exp",)] + [("ms", j) for j in tiles] + [("sum",), ("measure",)]
    return [step for step in order if (pick if step[0] in of_pick else block_out if step[0] in of_block else post)]


def mod_loop(nc, io, w, ps):
    with Memory(nc) as m:
        mem = {
            "xm": m.sb("xm", [P, NT, C]), "idxb": m.sb("idxb", [P, CAP]),
            "oh": m.sb("oh", [P, NT, CAP]),
            "xs": m.sb("xs", [P, C]), "hn": m.sb("hn", [P, C]), "hnt": m.sb("hnt", [P, KC, P]),
            "qt": m.sb("cqt", [P, KC, P]),
            "kbd": m.sb("kbd", [P, KC, HC, P]),
            "val": m.sb("cval", [P, C]), "sm": m.sb("sm", [P, H, P]),
            "smx": m.sb("smx", [P, H]), "ssum": m.sb("ssum", [P, H]),
            "ss": m.sb("ss", [P, 2]), "stmp": m.sb("stmp", [P, 2]), "srs": m.sb("srs", [P, 2]),
            "junk": m.sb("cjunk", [P, C]),
            "xs1": m.sb("xs1", [P, C]), "pt": m.sb("cpt", [P, H, P]), "o": m.sb("co", [P, H, D]),
            "ot": m.sb("cot", [P, KC, P]), "xa": m.sb("xa", [P, C]), "hn2": m.sb("hn2", [P, C]),
            "hnt2": m.sb("hnt2", [P, KC, P]), "gate": m.sb("gate", [P, FT, P]), "delta": m.sb("delta", [P, C]),
            "x": m.sb("cx", [P, NT, C]), "xn": m.sb("cxn", [P, NT, C]), "idxc": m.sb("idxc", [P, 1]),
            "oht": m.sb("oht", [CAP, T]),
            "stats": m.sb("cstats", [P, NT, 6]), "mv": m.sb("cmv", [P, NT, 2]),
            "vtmp": m.sb("cvtmp", [P, NT]), "rstd": m.sb("crstd", [P, NT]),
            "xnt": m.sb("cxnt", [P, KC, T]), "xst": m.sb("xst", [P, KC, S]), "ks": m.sb("ks", [P, KC, S1]),
            "ksbd": m.sb("ksbd", [P, KC, HC, S1]),
            "q": m.sb("cq", [P, NT, C]), "qtt": m.sb("qtt", [P, KC, T]), "mm": m.sb("mm", [P, NT, KC, HC]),
        }
        names = """first_in next_in oh_ready oht_ready xs_ss rms_step rms_ready xs_kept hn_ready
            less_ready exp_done xa_ss rms2_step rms2_ready hn2_ready silu_ready delta_ready a_stat a_rstd a_norm x2_ready
            x2_stat x2_rstd xn2_ready ksbd_ready x2_stored xn2_stored
            q_stored pool_step""".split()
        e = {n: m.sem("c_" + n) for n in names}
        e["pair_filled"] = [m.sem(f"c_pair_filled{n}") for n in range(SLOTS)]
        e["pair_taken"] = [m.sem(f"c_pair_taken{n}") for n in range(SLOTS)]

        with nc.Block() as block:
            @block.sync
            def _(sp):
                sp.dma_start(mem["idxb"][:, :], over_partitions(io["top_tokens"][0, :])).then_inc(e["first_in"], 16)
                sp.dma_start(mem["xm"][:, :, :], io["xn1"][0].rearrange("(j p) c -> p j c", p=P))\
                    .then_inc(e["first_in"], 16)
                sp.wait_ge(e["first_in"], 32)
        m.clear()
        mod_turn(nc, io, w, ps, mem, e, 0, pick=True, block_out=False, post=False, next_pick=True, next_post=False)
        m.clear()
        mod_turn(nc, io, w, ps, mem, e, 1, pick=True, block_out=True, post=False, next_pick=True, next_post=True)
        m.clear()
        with nc.Fori(2, B - 1) as b:
            mod_turn(nc, io, w, ps, mem, e, b, pick=True, block_out=True, post=True, next_pick=True, next_post=True)
            m.clear()
        mod_turn(nc, io, w, ps, mem, e, B - 1, pick=True, block_out=True, post=True, next_pick=False, next_post=True)
        m.clear()
        mod_turn(nc, io, w, ps, mem, e, B, pick=False, block_out=True, post=True, next_pick=False, next_post=True)
        m.clear()
        mod_turn(nc, io, w, ps, mem, e, B + 1, pick=False, block_out=False, post=True, next_pick=False,
                 next_post=False)
        m.clear()


def mod_turn(nc, io, w, ps, mem, e, b, pick, block_out, post, next_pick, next_post):
    order = mod_steps(pick, block_out, post)
    numbers = {step: k for k, step in enumerate(s for s in order if s[0] in PAIR_STEPS)}
    filled, taken = e["pair_filled"], e["pair_taken"]
    (xm, idxb, oh, xs, hn, hnt, qt, kbd, val, sm, smx, ssum, ss, stmp, srs, junk, xs1, pt, o, ot, xa, hn2, hnt2, gate,
     delta, x, xn, idxc, oht, stats, mv, vtmp, rstd, xnt, xst, ks, ksbd, q, qtt, mm) = (mem[n] for n in """xm idxb oh xs
        hn hnt qt kbd val sm smx ssum ss stmp srs junk xs1 pt o ot xa hn2 hnt2 gate delta x xn idxc oht stats mv vtmp
        rstd xnt xst ks ksbd q qtt mm""".split())

    def pair_use(*step):
        return numbers[step] % SLOTS, numbers[step] // SLOTS

    def until_filled(engine, *step):
        slot, uses = pair_use(*step)
        engine.wait_ge(filled[slot], uses + 1)

    def until_taken(engine, *step):
        slot, uses = pair_use(*step)
        engine.wait_ge(taken[slot], uses + 1)

    def pair(*step):
        slot, _ = pair_use(*step)
        return ps[:, 2 * slot:2 * slot + 2, :]

    def rows(name, n):
        return io[name][n].rearrange("(j p) c -> p j c", p=P)

    with nc.Block() as block:
        @block.sync
        def _(sp):
            if next_pick:
                until_filled(sp, "xs")
                sp.dma_start(idxb[:, :], over_partitions(io["top_tokens"][b + 1, :])).then_inc(e["next_in"], 16)
                sp.dma_start(xm[:, :, :], rows("xn1", b + 1)).then_inc(e["next_in"], 16)
            if post:
                sp.wait_ge(e["x2_ready"], NT)
                sp.dma_start(rows("x2", b - 2), x[:, :, :]).then_inc(e["x2_stored"], 16)
                sp.wait_ge(e["xn2_ready"], NT)
                sp.dma_start(rows("xn2", b - 2), xn[:, :, :]).then_inc(e["xn2_stored"], 16)
                until_filled(sp, "xt", NHALF - 1)
                until_filled(sp, "xst")
            if next_post:
                if post:
                    sp.wait_ge(e["xn2_stored"], 16)
                    sp.wait_ge(e["oht_ready"], 1)
                    sp.wait_ge(e["x2_stored"], 16)
                sp.dma_start(idxc[:, :], io["top_tokens"][b - 1, :].rearrange("(p a) -> p a", a=1))\
                    .then_inc(e["next_in"], 16)
                sp.dma_start(xn[:, :, :], rows("xn1", b - 1)).then_inc(e["next_in"], 16)
                sp.dma_start(x[:, :, :], rows("x1", b - 1)).then_inc(e["next_in"], 16)
            if post:
                until_taken(sp, "q", NHALF - 1)
                sp.dma_start(rows("q", b - 2), q[:, :, :]).then_inc(e["q_stored"], 16)
                sp.wait_ge(e["x2_stored"], 16)
                sp.wait_ge(e["xn2_stored"], 16)
                sp.wait_ge(e["q_stored"], 16)
            if next_pick or next_post:
                sp.wait_ge(e["next_in"], 16 * (2 * next_pick + 3 * next_post))

        @block.gpsimd
        def _(g):
            for step in order:
                kind, a = step[0], step[1:]
                if kind == "keep_xs":
                    nc.gpsimd.tensor_copy(xs1[:, :], xs[:, :]).then_inc(e["xs_kept"], 1)
                elif kind == "hn":
                    g.wait_ge(e["xs_ss"], 1)
                    nc.gpsimd.tensor_scalar(stmp[:, 0:1], ss[:, 0:1], 1.0 / C, EPS_RMS, ALU.mult, ALU.add)\
                        .then_inc(e["rms_step"], 1)
                    g.wait_ge(e["rms_step"], 1)
                    nc.gpsimd.tensor_tensor(srs[:, 0:1], stmp[:, 0:1], w["mhalf"][:, 0:1], ALU.pow)\
                        .then_inc(e["rms_ready"], 1)
                elif kind == "hn2":
                    g.wait_ge(e["xa_ss"], 1)
                    nc.gpsimd.tensor_scalar(stmp[:, 1:2], ss[:, 1:2], 1.0 / C, EPS_RMS, ALU.mult, ALU.add)\
                        .then_inc(e["rms2_step"], 1)
                    g.wait_ge(e["rms2_step"], 1)
                    nc.gpsimd.tensor_tensor(srs[:, 1:2], stmp[:, 1:2], w["mhalf"][:, 0:1], ALU.pow)\
                        .then_inc(e["rms2_ready"], 1)
                elif kind == "a_norm" and a[0] == 0:
                    g.wait_ge(e["a_stat"], 1)
                    rstd_of(nc, mv[:, :, 1], rstd[:, :], w, NT, EPS_LN, e["pool_step"], vtmp[:, :], 1)\
                        .then_inc(e["a_rstd"], 1)
                elif kind == "x2_stat":
                    j, = a
                    g.wait_ge(e["a_norm"], j + 1)
                    nc.gpsimd.tensor_tensor(x[:, j, :], x[:, j, :], xn[:, j, :], ALU.add)\
                        .then_inc(e["x2_ready"], 1)
                elif kind == "xn2" and a[0] == 0:
                    g.wait_ge(e["x2_stat"], 1)
                    rstd_of(nc, mv[:, :, 1], rstd[:, :], w, NT, EPS_LN, e["pool_step"], vtmp[:, :], 2)\
                        .then_inc(e["x2_rstd"], 1)

        @block.vector
        def _(v):
            for step in order:
                kind, a = step[0], step[1:]
                if kind in PAIR_STEPS:
                    slot, uses = pair_use(*step)
                    both = pair(*step)
                    one = both[:, 0, :]
                if kind == "oh":
                    j, = a
                    nc.vector.tensor_scalar(oh[:, j, :], idxb[:, :], w["iota_col"][:, j:j + 1], None,
                                            ALU.is_equal).then_inc(e["oh_ready"], 1)
                elif kind == "xs":
                    v.wait_ge(filled[slot], uses + 1)
                    if block_out:
                        v.wait_ge(e["xs_kept"], 1)
                    nc.vector.tensor_copy(xs[:, :], one[:, 0:C]).then_inc(taken[slot], 1)
                    nc.vector.drain()
                    nc.vector.scalar_tensor_tensor(junk[:, :], xs[:, :], 1.0, xs[:, :], ALU.mult, ALU.mult,
                                                   accum_out=ss[:, 0:1]).then_inc(e["xs_ss"], 1)
                elif kind == "hn":
                    v.wait_ge(e["rms_ready"], 1)
                    nc.vector.scalar_tensor_tensor(hn[:, :], xs[:, :], srs[:, 0:1], w["g1"][:, :],
                                                   ALU.mult, ALU.mult).then_inc(e["hn_ready"], 1)
                elif kind == "k_t":
                    v.wait_ge(filled[slot], uses + 1)
                    for k in range(KC):
                        last = nc.vector.tensor_tensor(kbd[:, k, :, :], spread(one[:, k * P:(k + 1) * P], 1, HC),
                                                       w["bdmask"][:, :, 0:1].to_broadcast([P, HC, P]), ALU.mult)
                    last.then_inc(taken[slot], 1)
                elif kind == "s":
                    n, = a
                    v.wait_ge(filled[slot], uses + 1)
                    if block_out:
                        until_filled(v, "pt", n)
                    nc.vector.scalar_tensor_tensor(sm[:, HC * n:HC * (n + 1), :],
                                                   both.rearrange("p two (h k) -> p (two h) k", k=P), SCALE,
                                                   spread(w["mask_f32"][:, :], 1, HC), ALU.mult, ALU.add)\
                        .then_inc(taken[slot], 1)
                elif kind == "less":
                    nc.vector.drain()
                    nc.vector.tensor_reduce(smx[:, :], sm[:, :, :], AX.X, ALU.max, negate=True)\
                        .then_inc(e["less_ready"], 1)
                elif kind == "sum":
                    v.wait_ge(e["exp_done"], 1)
                    nc.vector.reciprocal(ssum[:, :], ssum[:, :])
                elif kind == "pt" and a[0] == 1:
                    v.wait_ge(filled[slot], uses + 1)
                    nc.vector.tensor_copy(pt[:, HC:H, :], both.rearrange("p two (h k) -> p (two h) k", k=P))\
                        .then_inc(taken[slot], 1)
                elif kind == "o":
                    v.wait_ge(filled[slot], uses + 1)
                    nc.vector.tensor_tensor(o[:, :, :], one[:, 0:C].rearrange("p (h d) -> p h d", d=D),
                                            spread(ssum[:, :], 2, D), ALU.mult).then_inc(taken[slot], 1)
                elif kind == "xa":
                    v.wait_ge(filled[slot], uses + 1)
                    v.wait_ge(e["xs_kept"], 1)
                    nc.vector.tensor_tensor(xa[:, :], one[:, 0:C], xs1[:, :], ALU.add).then_inc(taken[slot], 1)
                    nc.vector.drain()
                    nc.vector.scalar_tensor_tensor(junk[:, :], xa[:, :], 1.0, xa[:, :], ALU.mult, ALU.mult,
                                                   accum_out=ss[:, 1:2]).then_inc(e["xa_ss"], 1)
                elif kind == "hn2":
                    v.wait_ge(e["rms2_ready"], 1)
                    nc.vector.scalar_tensor_tensor(hn2[:, :], xa[:, :], srs[:, 1:2], w["g2"][:, :],
                                                   ALU.mult, ALU.mult).then_inc(e["hn2_ready"], 1)
                elif kind == "up":
                    v.wait_ge(filled[slot], uses + 1)
                    until_taken(v, "gate")
                    nc.vector.tensor_tensor(gate[:, :, :],
                                            both.rearrange("p two (f t) -> p (two f) t", t=P)[:, 0:FT, :],
                                            gate[:, :, :], ALU.mult).then_inc(taken[slot], 1)
                elif kind == "ff":
                    v.wait_ge(filled[slot], uses + 1)
                    if post:
                        until_filled(v, "put", NHALF - 1)
                    nc.vector.tensor_tensor(delta[:, :], one[:, 0:C], xa[:, :], ALU.add).then_inc(taken[slot], 1)
                    nc.vector.drain()
                    nc.vector.tensor_tensor(delta[:, :], delta[:, :], xs1[:, :], ALU.subtract)\
                        .then_inc(e["delta_ready"], 1)
                elif kind == "oht":
                    nc.vector.tensor_scalar(oht[:, :], w["iota_row"][:, :], idxc[:, :], None,
                                            ALU.is_equal).then_inc(e["oht_ready"], 1)
                elif kind == "put":
                    n, = a
                    v.wait_ge(filled[slot], uses + 1)
                    tiles = slice(4 * n, 4 * n + 4)
                    nc.vector.tensor_tensor(xn[:, tiles, :].rearrange("p j c -> p (j c)"),
                                            xn[:, tiles, :].rearrange("p j c -> p (j c)"),
                                            both.rearrange("p two n -> p (two n)"), ALU.add).then_inc(taken[slot], 1)
                    nc.vector.drain()
                    for j in range(4 * n, 4 * n + 4):
                        nc.vector.bn_stats(stats[:, j, :], xn[:, j, :])
                    nc.vector.drain()
                    for j in range(4 * n, 4 * n + 4):
                        last = nc.vector.bn_aggr(mv[:, j, :], stats[:, j, :])
                    if n == NHALF - 1:
                        last.then_inc(e["a_stat"], 1)
                elif kind == "a_norm":
                    j, = a
                    v.wait_ge(e["a_rstd"], 1)
                    nc.vector.tensor_scalar(xn[:, j, :], xn[:, j, :], mv[:, j, 0:1], rstd[:, j:j + 1],
                                            ALU.subtract, ALU.mult).then_inc(e["a_norm"], 1)
                elif kind == "x2_stat":
                    j, = a
                    v.wait_ge(e["x2_ready"], j + 1)
                    last = layer_stats(nc, stats, mv, x[:, j, :], j)
                    if j == NT - 1:
                        last.then_inc(e["x2_stat"], 1)
                elif kind == "xn2":
                    j, = a
                    v.wait_ge(e["x2_rstd"], 1)
                    nc.vector.tensor_scalar(xn[:, j, :], x[:, j, :], mv[:, j, 0:1], rstd[:, j:j + 1],
                                            ALU.subtract, ALU.mult).then_inc(e["xn2_ready"], 1)
                elif kind == "xst":
                    v.wait_ge(filled[slot], uses + 1)
                    nc.vector.tensor_copy(xst[:, :, :], one[:, 0:KC * S].rearrange("p (k s) -> p k s", s=S))\
                        .then_inc(taken[slot], 1)
                elif kind == "ks":
                    v.wait_ge(filled[slot], uses + 1)
                    for k in range(KC):
                        last = nc.vector.tensor_scalar(ks[:, k, 0:S], one[:, k * S:(k + 1) * S],
                                                       w["ps_bk"][:, k:k + 1], None, ALU.add)
                    last.then_inc(taken[slot], 1)
                    nc.vector.drain()
                    nc.vector.reduce_sum(ks[:, :, S:S1], ks[:, :, 0:S], AX.X)
                    nc.vector.drain()
                    nc.vector.tensor_scalar(ks[:, :, S:S1], ks[:, :, S:S1], 1.0 / S, None, ALU.mult)
                    nc.vector.drain()
                    for k in range(KC):
                        nc.vector.tensor_tensor(ksbd[:, k, :, :], spread(ks[:, k, :], 1, HC), w["bdmask"][:, :, :],
                                                ALU.mult).then_inc(e["ksbd_ready"], 1)
                elif kind == "q":
                    n, = a
                    v.wait_ge(filled[slot], uses + 1)
                    nc.vector.tensor_tensor(q[:, 4 * n:4 * n + 4, :],
                                            both.rearrange("p two (j c) -> p (two j) c", c=C),
                                            spread(w["ps_bq"][:, :], 1, 4), ALU.add).then_inc(taken[slot], 1)
                elif kind == "ms":
                    j, = a
                    v.wait_ge(filled[slot], uses + 1)
                    of_heads = both[:, :, 0:HC * S1].rearrange("p k (h s) -> p k h s", s=S1)
                    nc.vector.reduce_max(mm[:, j, :, :], of_heads[:, :, :, 0:S], AX.X)
                    nc.vector.drain()
                    nc.vector.tensor_tensor(mm[:, j, :, :], mm[:, j, :, :], of_heads[:, :, :, S],
                                            ALU.subtract).then_inc(taken[slot], 1)
                elif kind == "measure":
                    nc.vector.drain()
                    nc.vector.tensor_copy(w["measure"][:, :, bass.ds((b - 2) * H, H)],
                                          mm[:, :, :, :].rearrange("p j k h -> p j (k h)"))

        @block.tensor
        def _(pe):
            def turn(src, into):
                for k in range(KC):
                    last = nc.tensor.transpose(into[:, k * P:(k + 1) * P], src[:, k * P:(k + 1) * P], w["ident"][:, :])
                return last

            def turn_tiles(src, n, into):
                for k in range(KC):
                    for t in range(4):
                        last = nc.tensor.transpose(into[:, k, t * P:(t + 1) * P],
                                                   src[:, 4 * n + t, k * P:(k + 1) * P], w["ident"][:, :])
                return last

            for step in order:
                kind, a = step[0], step[1:]
                if kind not in PAIR_STEPS:
                    continue
                slot, uses = pair_use(*step)
                both = pair(*step)
                one = both[:, 0, :]
                if uses:
                    pe.wait_ge(taken[slot], uses)
                if kind == "xs":
                    for j in range(NT):
                        pe.wait_ge(e["oh_ready"], j + 1)
                        last = nc.tensor.matmul(one[:, 0:C], oh[:, j, :], xm[:, j, :],
                                                start=(j == 0), stop=(j == NT - 1))
                elif kind == "hnt":
                    pe.wait_ge(e["hn_ready"], 1)
                    last = turn(hn, one)
                elif kind in ("q_t", "k_t"):
                    until_taken(pe, "hnt")
                    at0 = C * (kind == "k_t")
                    for cc in range(KC):
                        for k in range(KC):
                            last = nc.tensor.matmul(one[:, cc * P:(cc + 1) * P],
                                                    w["mod_wqkv"][:, k, at0 + cc * P:at0 + (cc + 1) * P],
                                                    hnt[:, k, :], start=(k == 0), stop=(k == KC - 1))
                elif kind == "val":
                    for k in range(KC):
                        last = nc.tensor.matmul(one[:, 0:C], hnt[:, k, :], w["mod_wqkv"][:, k, 2 * C:3 * C],
                                                start=(k == 0), stop=(k == KC - 1))
                elif kind == "s":
                    n, = a
                    until_taken(pe, "q_t")
                    until_taken(pe, "k_t")
                    for half in range(2):
                        last = nc.tensor.matmul(both[:, half, :], qt[:, n, :],
                                                kbd[:, n, 4 * half:4 * half + 4, :].rearrange("p h t -> p (h t)"),
                                                start=True, stop=True)
                elif kind == "pt":
                    n, = a
                    for h in range(HC):
                        last = nc.tensor.transpose(both[:, h // 4, h % 4 * P:(h % 4 + 1) * P], sm[:, HC * n + h, :],
                                                   w["ident"][:, :])
                elif kind == "o":
                    until_taken(pe, "pt", 0)
                    until_taken(pe, "pt", 1)
                    for h in range(H):
                        last = nc.tensor.matmul(one[:, h * D:(h + 1) * D], pt[:, h, :], val[:, h * D:(h + 1) * D],
                                                start=True, stop=True)
                elif kind == "ot":
                    until_taken(pe, "o")
                    last = turn(o[:, :, :].rearrange("p h d -> p (h d)"), one)
                elif kind == "xa":
                    until_taken(pe, "ot")
                    for k in range(KC):
                        last = nc.tensor.matmul(one[:, 0:C], ot[:, k, :], w["mod_wout"][:, k, :],
                                                start=(k == 0), stop=(k == KC - 1))
                elif kind == "hnt2":
                    pe.wait_ge(e["hn2_ready"], 1)
                    last = turn(hn2, one)
                elif kind in ("gate", "up"):
                    until_taken(pe, "hnt2")
                    wt = w["mod_w1"] if kind == "gate" else w["mod_w2"]
                    for f in range(FT):
                        for k in range(KC):
                            last = nc.tensor.matmul(both[:, f // 4, (f % 4) * P:(f % 4 + 1) * P],
                                                    wt[:, k, f * P:(f + 1) * P], hnt2[:, k, :],
                                                    start=(k == 0), stop=(k == KC - 1))
                elif kind == "ff":
                    until_taken(pe, "up")
                    for f in range(FT):
                        last = nc.tensor.matmul(one[:, 0:C], gate[:, f, :], w["mod_w3"][:, f, :],
                                                start=(f == 0), stop=(f == FT - 1))
                elif kind == "put":
                    n, = a
                    pe.wait_ge(e["oht_ready"], 1)
                    for t in range(4):
                        j = 4 * n + t
                        last = nc.tensor.matmul(both[:, t // 2, t % 2 * C:(t % 2 + 1) * C],
                                                oht[:, j * P:(j + 1) * P], delta[:, :], start=True, stop=True)
                elif kind == "xt":
                    n, = a
                    pe.wait_ge(e["xn2_ready"], 4 * (n + 1))
                    last = turn_tiles(xn, n, both)
                elif kind == "xst":
                    for k in range(KC):
                        for j in range(NT):
                            last = nc.tensor.matmul(one[:, k * S:(k + 1) * S], xn[:, j, k * P:(k + 1) * P],
                                                    w["onehot_s"][:, j, :], start=(j == 0), stop=(j == NT - 1))
                elif kind == "ks":
                    until_taken(pe, "xst")
                    for cc in range(KC):
                        for k in range(KC):
                            last = nc.tensor.matmul(one[:, cc * S:(cc + 1) * S], w["ps_wk"][:, k, cc * P:(cc + 1) * P],
                                                    xst[:, k, :], start=(k == 0), stop=(k == KC - 1))
                elif kind == "q":
                    n, = a
                    until_taken(pe, "xt", n)
                    for t in range(4):
                        j = 4 * n + t
                        for k in range(KC):
                            last = nc.tensor.matmul(both[:, t // 2, t % 2 * C:(t % 2 + 1) * C],
                                                    xnt[:, k, j * P:(j + 1) * P], w["ps_wq"][:, k, :],
                                                    start=(k == 0), stop=(k == KC - 1))
                elif kind == "qt":
                    n, = a
                    until_taken(pe, "q", n)
                    last = turn_tiles(q, n, both)
                elif kind == "ms":
                    j, = a
                    pe.wait_ge(e["ksbd_ready"], KC)
                    until_taken(pe, "qt", j // 4)
                    for k in range(KC):
                        last = nc.tensor.matmul(both[:, k, 0:HC * S1], qtt[:, k, j * P:(j + 1) * P],
                                                ksbd[:, k, :, :].rearrange("p h s -> p (h s)"), start=True, stop=True)
                last.then_inc(filled[slot], 1)

        @block.scalar
        def _(act):
            chunks = {"hnt": hnt, "q_t": qt, "ot": ot, "hnt2": hnt2}
            for step in order:
                kind, a = step[0], step[1:]
                if kind in PAIR_STEPS:
                    slot, uses = pair_use(*step)
                    both = pair(*step)
                    one = both[:, 0, :]
                if kind in chunks:
                    act.wait_ge(filled[slot], uses + 1)
                    nc.scalar.copy(chunks[kind][:, :, :], one[:, 0:C].rearrange("p (k t) -> p k t", k=KC))\
                        .then_inc(taken[slot], 1)
                elif kind == "val":
                    act.wait_ge(filled[slot], uses + 1)
                    if block_out:
                        until_filled(act, "o")
                    nc.scalar.copy(val[:, :], one[:, 0:C]).then_inc(taken[slot], 1)
                elif kind == "exp":
                    act.wait_ge(e["less_ready"], 1)
                    for h in range(H):
                        last = nc.scalar.activation(sm[:, h, :], sm[:, h, :], ACT.Exp, bias=smx[:, h:h + 1],
                                                    accum_out=ssum[:, h:h + 1])
                    last.then_inc(e["exp_done"], 1)
                elif kind == "pt" and a[0] == 0:
                    act.wait_ge(filled[slot], uses + 1)
                    nc.scalar.copy(pt[:, 0:HC, :], both.rearrange("p two (h k) -> p (two h) k", k=P))\
                        .then_inc(taken[slot], 1)
                elif kind == "gate":
                    act.wait_ge(filled[slot], uses + 1)
                    nc.scalar.activation(gate[:, :, :], both.rearrange("p two (f t) -> p (two f) t", t=P)[:, 0:FT, :],
                                         ACT.Silu).then_inc(taken[slot], 1)
                elif kind in ("xt", "qt"):
                    n, = a
                    act.wait_ge(filled[slot], uses + 1)
                    nc.scalar.copy((xnt if kind == "xt" else qtt)[:, :, n * BANK:(n + 1) * BANK], both)\
                        .then_inc(taken[slot], 1)


def top_queries(nc, io, w, ps):
    with Memory(nc) as m:
        full = m.sem("d_full")
        ready = m.sem("d_ready")
        stored = m.sem("d_stored")
        ms = m.sb("ms", [P, T])
        top = m.sb("dtop", [P, 8 * ROUNDS_E])
        idx = m.sb("didx", [P, 8 * ROUNDS_E], U32)
        idxf = m.sb("didxf", [P, 8 * ROUNDS_E])
        with nc.Block() as block:
            @block.tensor
            def _(pe):
                for j in range(NT):
                    nc.tensor.transpose(ps[:, j // 4, (j % 4) * P:(j % 4 + 1) * P], w["measure"][:, j, :],
                                        w["ident"][:, :]).then_inc(full, 1)

            @block.vector
            def _(v):
                for n in range(NHALF):
                    v.wait_ge(full, 4 * (n + 1))
                    nc.vector.tensor_copy(ms[:, n * BANK:(n + 1) * BANK], ps[:, n, :])
                nc.vector.drain()
                for n in range(ROUNDS_E):
                    t8 = slice(8 * n, 8 * n + 8)
                    nc.vector.max(top[:, t8], ms[:, :])
                    nc.vector.drain()
                    nc.vector.max_index(idx[:, t8], top[:, t8], ms[:, :])
                    nc.vector.drain()
                    if n < ROUNDS_E - 1:
                        nc.vector.match_replace(ms[:, :], top[:, t8], ms[:, :], -3e38)
                        nc.vector.drain()
                nc.vector.tensor_copy(idxf[:, :], idx[:, :]).then_inc(ready, 1)

            @block.sync
            def _(sp):
                sp.wait_ge(ready, 1)
                sp.dma_start(io["top_queries"].rearrange("b (h u) -> (b h) u", u=S), idxf[:, 0:S]).then_inc(stored, 16)
                sp.wait_ge(stored, 16)
        m.clear()



HALF = HU // KC


def chunks_of(mt):
    return [k for k in range(KC) if mt * MR < (k + 1) * HALF and (mt + 1) * MR > k * HALF]


def prob_steps(attention, forward):
    tiles = range(NT)
    first = [("oh", j) for j in tiles] + [("xt", n, k) for n in range(NHALF) for k in range(KC)] \
        + [("qtop", k) for k in range(KC)] + [("kt", cc, n) for cc in range(KC) for n in range(NHALF)] \
        + [("v", j) for j in tiles]
    second = [("s", 0), ("s", 1), ("vm",)]
    for mt in range(MT):
        second += [("s", mt + 2)] if mt + 2 < MT else []
        second += [("pt", mt), ("oht", mt)]
    second += [("base",)] + [("ot", k) for k in range(KC)] + [("g", mt) for mt in range(MT)] \
        + [("ctx", j) for j in tiles]
    norms = [(kind, j) for kind in ("a_norm", "x3_stat", "hh", "hh_stat", "hn") for j in tiles]
    products = []
    for n in range(NHALF):
        products += [("ht", n, k) for k in range(KC)]
        products += [("f1", n, f) for f in range(F2T)] + [("f2", 4 * n + t) for t in range(4)]
    after = [("r_norm", j) for j in tiles]
    if not attention:
        return [("load_x",)] + norms + products + after
    if not forward:
        return first + second

    def mixed(a, b):
        out, done = [], 0
        for n, step in enumerate(a):
            out.append(step)
            upto = len(b) * (n + 1) // len(a)
            out += b[done:upto]
            done = upto
        return out

    early = len(second) - NT - MT
    return [("load_x",)] + mixed(first, norms) + mixed(second[:early], products) \
        + second[early:early + MT] + after + second[early + MT:]


def prob_loop(nc, io, w, ps):
    with Memory(nc) as m:
        oh = m.sb("eoh", [P, NT, HU])
        mem = {
            "xn": m.sb("exn", [P, NT, C]), "q": m.sb("eq", [P, NT, C]),
            "idxb": m.sb("eidxb", [P, HU]), "idxc": m.sb("eidxc", [MR, MT]),
            "oh": oh,
            "pt": oh,
            "oht": m.sb("eoht", [MR, MT, T]),
            "xnt": m.sb("exnt", [P, KC, T]), "kt": m.sb("ekt", [P, KC, T]), "vv": m.sb("evv", [P, NT, C]),
            "qbd": m.sb("qbd", [P, KC, HU]),
            "obd": m.sb("obd", [P, KC, HU]),
            "nmx": m.sb("nmx", [MR, MT]), "nb": m.sb("nb", [MR, MT]), "sums": m.sb("sums", [MR, MT]),
            "pr": m.sb("pr", [MR, 3, T]),
            "vm": m.sb("vm", [P, KC]), "vmr": m.sb("vmr", [P, KC, P]), "mean1": m.sb("mean1", [P, 1]),
            "gg": m.sb("gg", [MR, MT, C]), "base": m.sb("base", [P, C]),
            "stats": m.sb("estats", [P, NT, 6]), "rstd": m.sb("erstd", [P, NT]), "vtmp": m.sb("evtmp", [P, NT]),
            "mv": m.sb("emv", [P, NT, 2]), "fmv": m.sb("efmv", [P, NT, 2]), "fstats": m.sb("efstats", [P, NT, 6]),
            "att": m.sb("eatt", [P, NT, C]), "x": m.sb("ex", [P, NT, C]), "hh": m.sb("ehh", [P, NT, C]),
            "ht": m.sb("eht", [P, KC, T]), "yb": m.sb("eyb", [P, F2T, BANK]),
        }
        names = """x_in next_in first_in oh_ready oht_ready xnt_full xnt_ready qb_full qbd_ready kt_full kt_ready
            v_full v_ready s_full nb_ready exp_ready pn_ready pt_full pt_ready_a pt_ready_v vm_full vmr_ready ot_full
            obd_ready g_full g_ready base_full base_ready ctx_full ctx_ready a_rstd a_norm x3_ready x3_stat
            x3_rstd hh_ready hh_stat hh_rstd hn_ready hb_ready ht_full ht_ready f1_full y_ready f2_full r_ready r_stat
            r_rstd r_norm out_ready stored pool_step""".split()
        e = {n: m.sem("e_" + n) for n in names}

        with nc.Block() as block:
            @block.vector
            def _(v):
                nc.vector.memset(mem["qbd"][:, :, :], 0.0)
                nc.vector.memset(mem["obd"][:, :, :], 0.0)
                nc.vector.memset(mem["mean1"][:, :], 1.0 / T)

            @block.sync
            def _(sp):
                sp.dma_start(mem["idxb"][:, :], over_partitions(io["top_queries"][0, :])).then_inc(e["first_in"], 16)
                with nc.allow_non_contiguous_dma(reason="560 indices as columns"):
                    sp.dma_start(mem["idxc"][:, :], io["top_queries"][0, :].rearrange("(m r) -> r m", r=MR))\
                        .then_inc(e["first_in"], 16)
                for name, source in (("xn", "xn2"), ("q", "q")):
                    sp.dma_start(mem[name][:, :, :], io[source][0].rearrange("(j p) c -> p j c", p=P))\
                        .then_inc(e["first_in"], 16)
                sp.wait_ge(e["first_in"], 64)
        m.clear()
        prob_turn(nc, io, w, ps, mem, e, 0, attention=True, forward=False, following=True)
        m.clear()
        with nc.Fori(1, B - 1) as b:
            prob_turn(nc, io, w, ps, mem, e, b, attention=True, forward=True, following=True)
            m.clear()
        prob_turn(nc, io, w, ps, mem, e, B - 1, attention=True, forward=True, following=False)
        m.clear()
        prob_turn(nc, io, w, ps, mem, e, B, attention=False, forward=True, following=False)
        m.clear()


def prob_turn(nc, io, w, ps, mem, e, b, attention, forward, following):
    order = prob_steps(attention, forward)
    (xn, q, idxb, idxc, oh, pt, oht, xnt, kt, vv, qbd, obd, nmx, nb, sums, pr, vm, vmr, mean1, gg, base, stats,
     rstd, mv, fmv, fstats, att, x, hh, ht, yb) = (mem[n] for n in """xn q idxb idxc oh pt oht xnt kt vv qbd obd nmx nb
        sums pr vm vmr mean1 gg base stats rstd mv fmv fstats att x hh ht yb""".split())

    with nc.Block() as block:
        @block.sync
        def _(sp):
            def rows(name, n):
                return io[name][n].rearrange("(j p) c -> p j c", p=P)

            if forward:
                sp.dma_start(x[:, :, :], rows("x2", b - 1)).then_inc(e["x_in"], 16)
            if following:
                sp.wait_ge(e["oh_ready"], NT)
                sp.dma_start(idxb[:, :], over_partitions(io["top_queries"][b + 1, :])).then_inc(e["next_in"], 16)
                sp.wait_ge(e["xnt_ready"], NHALF * KC)
                sp.dma_start(xn[:, :, :], rows("xn2", b + 1)).then_inc(e["next_in"], 16)
                sp.wait_ge(e["qb_full"], KC)
                sp.dma_start(q[:, :, :], rows("q", b + 1)).then_inc(e["next_in"], 16)
                sp.wait_ge(e["oht_ready"], MT)
                with nc.allow_non_contiguous_dma(reason="560 indices as columns"):
                    sp.dma_start(idxc[:, :], io["top_queries"][b + 1, :].rearrange("(m r) -> r m", r=MR))\
                        .then_inc(e["next_in"], 16)
            if forward:
                for n in range(2):
                    sp.wait_ge(e["out_ready"], 4 * (n + 1))
                    sp.dma_start(io["out"][b - 1, n * BANK:(n + 1) * BANK, :].rearrange("(j p) c -> p j c", p=P),
                                 x[:, 4 * n:4 * n + 4, :]).then_inc(e["stored"], 16)
                sp.wait_ge(e["stored"], 32)
            if following:
                sp.wait_ge(e["next_in"], 64)

        @block.gpsimd
        def _(g):
            if not forward:
                return

            def rstd_step(var, n, done):
                rstd_of(nc, var, rstd[:, :], w, NT, EPS_LN, e["pool_step"], mem["vtmp"][:, :], n)\
                    .then_inc(e[done], 1)

            rstd_step(mv[:, :, 1], 1, "a_rstd")
            g.wait_ge(e["x_in"], 16)
            for j in range(NT):
                g.wait_ge(e["a_norm"], j + 1)
                nc.gpsimd.tensor_tensor(x[:, j, :], x[:, j, :], att[:, j, :], ALU.add).then_inc(e["x3_ready"], 1)
            g.wait_ge(e["x3_stat"], 1)
            rstd_step(fmv[:, :, 1], 2, "x3_rstd")
            g.wait_ge(e["hh_stat"], 1)
            rstd_step(fmv[:, :, 1], 3, "hh_rstd")
            for j in range(NT):
                g.wait_ge(e["hn_ready"], j + 1)
                nc.gpsimd.tensor_tensor(hh[:, j, :], hh[:, j, :], w["fc2_b"][:, :], ALU.add)\
                    .then_inc(e["hb_ready"], 1)
            g.wait_ge(e["r_stat"], 1)
            rstd_step(fmv[:, :, 1], 4, "r_rstd")
            for j in range(NT):
                g.wait_ge(e["r_norm"], j + 1)
                nc.gpsimd.tensor_tensor(x[:, j, :], x[:, j, :], hh[:, j, :], ALU.add).then_inc(e["out_ready"], 1)

        @block.vector
        def _(v):
            def normalise(dst, src, moments, j, ready):
                nc.vector.tensor_scalar(dst[:, j, :], src[:, j, :], moments[:, j, 0:1], rstd[:, j:j + 1],
                                        ALU.subtract, ALU.mult).then_inc(e[ready], 1)

            for step in order:
                kind, a = step[0], step[1:]
                if kind == "oh":
                    j, = a
                    nc.vector.tensor_scalar(oh[:, j, :], idxb[:, :], w["iota_col"][:, j:j + 1], None,
                                            ALU.is_equal).then_inc(e["oh_ready"], 1)
                elif kind == "oht":
                    mt, = a
                    nc.vector.tensor_scalar(oht[:, mt, :], w["iota_row"][0:MR, :], idxc[:, mt:mt + 1], None,
                                            ALU.is_equal).then_inc(e["oht_ready"], 1)
                elif kind == "qtop":
                    k, = a
                    v.wait_ge(e["qb_full"], k + 1)
                    nc.vector.tensor_tensor(qbd[:, k, k * HALF:(k + 1) * HALF].rearrange("p (h u) -> p h u", u=S),
                                            ps[:, 4 + k, 0:HALF].rearrange("p (h u) -> p h u", u=S),
                                            w["bdmask"][:, :, 0:S], ALU.mult).then_inc(e["qbd_ready"], 1)
                elif kind == "v":
                    j, = a
                    v.wait_ge(e["v_full"], j + 1)
                    nc.vector.tensor_tensor(vv[:, j, :], ps[:, 4 + j % 2, 0:C], w["ps_bv"][:, :],
                                            ALU.add).then_inc(e["v_ready"], 1)
                elif kind == "s":
                    mt, = a
                    v.wait_ge(e["s_full"], mt + 1)
                    b0 = 2 * (mt % 2)
                    nc.vector.tensor_reduce(nmx[:, mt:mt + 1], ps[0:MR, b0:b0 + 2, :], AX.XY, ALU.max, negate=True)
                    nc.vector.drain()
                    nc.vector.tensor_scalar(nb[:, mt:mt + 1], nmx[:, mt:mt + 1], SCALE, None,
                                            ALU.mult).then_inc(e["nb_ready"], 1)
                elif kind == "vm":
                    v.wait_ge(e["vm_full"], 1)
                    nc.vector.tensor_copy(vm[:, :], ps[:, 4, 0:KC])
                    nc.vector.drain()
                    for k in range(KC):
                        last = nc.vector.tensor_copy(vmr[:, k, :], vm[:, k:k + 1].to_broadcast([P, P]))
                    last.then_inc(e["vmr_ready"], 1)
                elif kind == "pt":
                    mt, = a
                    v.wait_ge(e["exp_ready"], mt + 1)
                    nc.vector.reciprocal(sums[:, mt:mt + 1], sums[:, mt:mt + 1])
                    nc.vector.drain()
                    nc.vector.tensor_scalar(pr[:, mt % 3, :], pr[:, mt % 3, :], sums[:, mt:mt + 1], None,
                                            ALU.mult).then_inc(e["pn_ready"], 1)
                    v.wait_ge(e["pt_full"], 2 * mt + 2)
                    nc.vector.tensor_copy(pt[:, 4:8, mt * MR:(mt + 1) * MR],
                                          ps[:, 5, 0:4 * MR].rearrange("p (j r) -> p j r", r=MR))\
                        .then_inc(e["pt_ready_v"], 1)
                elif kind == "base":
                    v.wait_ge(e["base_full"], 1)
                    nc.vector.tensor_tensor(base[:, :], ps[:, 2, 0:C], w["ps_bo"][:, :], ALU.add)\
                        .then_inc(e["base_ready"], 1)
                elif kind == "ot":
                    k, = a
                    v.wait_ge(e["ot_full"], k + 1)
                    nc.vector.scalar_tensor_tensor(
                        obd[:, k, k * HALF:(k + 1) * HALF].rearrange("p (h u) -> p h u", u=S),
                        ps[:, k, 0:HALF].rearrange("p (h u) -> p h u", u=S), vm[:, k:k + 1],
                        w["bdmask"][:, :, 0:S], ALU.subtract, ALU.mult).then_inc(e["obd_ready"], 1)
                elif kind == "ctx":
                    j, = a
                    v.wait_ge(e["ctx_full"], j + 1)
                    if forward:
                        v.wait_ge(e["r_ready"], NT)
                    nc.vector.tensor_tensor(att[:, j, :], ps[:, 2 + j % 2, 0:C], base[:, :],
                                            ALU.add).then_inc(e["ctx_ready"], 1)
                    nc.vector.drain()
                    layer_stats(nc, stats, mv, att[:, j, :], j)
                elif kind == "a_norm":
                    v.wait_ge(e["a_rstd"], 1)
                    normalise(att, att, mv, a[0], "a_norm")
                elif kind == "x3_stat":
                    j, = a
                    v.wait_ge(e["x3_ready"], j + 1)
                    last = layer_stats(nc, fstats, fmv, x[:, j, :], j)
                    if j == NT - 1:
                        last.then_inc(e["x3_stat"], 1)
                elif kind == "hh":
                    v.wait_ge(e["x3_rstd"], 1)
                    normalise(hh, x, fmv, a[0], "hh_ready")
                elif kind == "hh_stat":
                    j, = a
                    if j == 0:
                        nc.vector.drain()
                    last = layer_stats(nc, fstats, fmv, hh[:, j, :], j)
                    if j == NT - 1:
                        last.then_inc(e["hh_stat"], 1)
                elif kind == "hn":
                    v.wait_ge(e["hh_rstd"], 1)
                    normalise(att, hh, fmv, a[0], "hn_ready")
                elif kind == "f2":
                    j, = a
                    v.wait_ge(e["f2_full"], j + 1)
                    v.wait_ge(e["hb_ready"], j + 1)
                    nc.vector.tensor_tensor(hh[:, j, :], ps[:, 6 + j % 2, 0:C], hh[:, j, :],
                                            ALU.add).then_inc(e["r_ready"], 1)
                    nc.vector.drain()
                    last = layer_stats(nc, fstats, fmv, hh[:, j, :], j)
                    if j == NT - 1:
                        last.then_inc(e["r_stat"], 1)
                elif kind == "r_norm":
                    v.wait_ge(e["r_rstd"], 1)
                    normalise(hh, hh, fmv, a[0], "r_norm")

        @block.tensor
        def _(pe):
            def turned(src, bank, n, k, full):
                for t in range(4):
                    last = nc.tensor.transpose(ps[:, bank, t * P:(t + 1) * P],
                                               src[:, 4 * n + t, k * P:(k + 1) * P], w["ident"][:, :])
                last.then_inc(e[full], 1)

            for step in order:
                kind, a = step[0], step[1:]
                if kind == "xt":
                    n, k = a
                    turned(xn, 2 * n + k, n, k, "xnt_full")
                elif kind == "qtop":
                    k, = a
                    for j in range(NT):
                        if k == 0:
                            pe.wait_ge(e["oh_ready"], j + 1)
                        last = nc.tensor.matmul(ps[:, 4 + k, 0:HALF], q[:, j, k * P:(k + 1) * P],
                                                oh[:, j, k * HALF:(k + 1) * HALF], start=(j == 0), stop=(j == NT - 1))
                    last.then_inc(e["qb_full"], 1)
                elif kind == "kt":
                    cc, n = a
                    u = cc * NHALF + n
                    pe.wait_ge(e["xnt_ready"], NHALF * KC)
                    if u >= 2:
                        pe.wait_ge(e["kt_ready"], u - 1)
                    for k in range(KC):
                        last = nc.tensor.matmul(ps[:, u % 2, :], w["ps_wk"][:, k, cc * P:(cc + 1) * P],
                                                xnt[:, k, n * BANK:(n + 1) * BANK], start=(k == 0), stop=(k == KC - 1))
                    last.then_inc(e["kt_full"], 1)
                elif kind == "v":
                    j, = a
                    if j == 0:
                        pe.wait_ge(e["qbd_ready"], KC)
                    if j >= 2:
                        pe.wait_ge(e["v_ready"], j - 1)
                    for k in range(KC):
                        last = nc.tensor.matmul(ps[:, 4 + j % 2, 0:C], xnt[:, k, j * P:(j + 1) * P],
                                                w["ps_wv"][:, k, :], start=(k == 0), stop=(k == KC - 1))
                    last.then_inc(e["v_full"], 1)
                elif kind == "s":
                    mt, = a
                    pe.wait_ge(e["kt_ready"], KC * NHALF)
                    if mt >= 2:
                        pe.wait_ge(e["exp_ready"], mt - 1)
                    cs = chunks_of(mt)
                    for n in range(NHALF):
                        for k in cs:
                            last = nc.tensor.matmul(ps[0:MR, 2 * (mt % 2) + n, :], qbd[:, k, mt * MR:(mt + 1) * MR],
                                                    kt[:, k, n * BANK:(n + 1) * BANK],
                                                    start=(k == cs[0]), stop=(k == cs[-1]))
                    last.then_inc(e["s_full"], 1)
                elif kind == "vm":
                    pe.wait_ge(e["v_ready"], NT)
                    for k in range(KC):
                        for j in range(NT):
                            last = nc.tensor.matmul(ps[:, 4, k:k + 1], vv[:, j, k * P:(k + 1) * P], mean1[:, :],
                                                    start=(j == 0), stop=(j == NT - 1))
                    last.then_inc(e["vm_full"], 1)
                elif kind == "pt":
                    mt, = a
                    pe.wait_ge(e["vmr_ready"], 1)
                    pe.wait_ge(e["pn_ready"], mt + 1)
                    if mt >= 1:
                        pe.wait_ge(e["pt_ready_a"], mt)
                        pe.wait_ge(e["pt_ready_v"], mt)
                    for j in range(NT):
                        last = nc.tensor.transpose(ps[:, 4 + j // 4, (j % 4) * MR:(j % 4 + 1) * MR],
                                                   pr[:, mt % 3, j * P:(j + 1) * P], w["ident"][0:MR, 0:MR])
                        if j % 4 == 3:
                            last.then_inc(e["pt_full"], 1)
                elif kind == "base":
                    pe.wait_ge(e["exp_ready"], MT)
                    for k in range(KC):
                        last = nc.tensor.matmul(ps[:, 2, 0:C], vmr[:, k, :], w["ps_wo"][:, k, :],
                                                start=(k == 0), stop=(k == KC - 1))
                    last.then_inc(e["base_full"], 1)
                elif kind == "ot":
                    k, = a
                    pe.wait_ge(e["pt_ready_a"], MT)
                    pe.wait_ge(e["pt_ready_v"], MT)
                    for j in range(NT):
                        last = nc.tensor.matmul(ps[:, k, 0:HALF], vv[:, j, k * P:(k + 1) * P],
                                                pt[:, j, k * HALF:(k + 1) * HALF], start=(j == 0), stop=(j == NT - 1))
                    last.then_inc(e["ot_full"], 1)
                elif kind == "g":
                    mt, = a
                    cs = chunks_of(mt)
                    pe.wait_ge(e["obd_ready"], cs[-1] + 1)
                    if mt >= 2:
                        pe.wait_ge(e["g_ready"], mt - 1)
                    for k in cs:
                        last = nc.tensor.matmul(ps[0:MR, 4 + mt % 2, 0:C], obd[:, k, mt * MR:(mt + 1) * MR],
                                                w["ps_wo"][:, k, :], start=(k == cs[0]), stop=(k == cs[-1]))
                    last.then_inc(e["g_full"], 1)
                elif kind == "ctx":
                    j, = a
                    if j == 0:
                        pe.wait_ge(e["g_ready"], MT)
                        pe.wait_ge(e["oht_ready"], MT)
                        pe.wait_ge(e["base_ready"], 1)
                    if j >= 2:
                        pe.wait_ge(e["ctx_ready"], j - 1)
                    for mt in range(MT):
                        last = nc.tensor.matmul(ps[:, 2 + j % 2, 0:C], oht[:, mt, j * P:(j + 1) * P], gg[:, mt, :],
                                                start=(mt == 0), stop=(mt == MT - 1))
                    last.then_inc(e["ctx_full"], 1)
                elif kind == "ht":
                    n, k = a
                    if n:
                        pe.wait_ge(e["r_ready"], 4 * n - 1 + k)
                    pe.wait_ge(e["hn_ready"], 4 * (n + 1))
                    turned(att, 6 + k % 2, n, k, "ht_full")
                elif kind == "f1":
                    n, f = a
                    if f < 2:
                        pe.wait_ge(e["ht_ready"], KC * (n + 1))
                    else:
                        pe.wait_ge(e["y_ready"], n * F2T + f - 1)
                    for k in range(KC):
                        last = nc.tensor.matmul(ps[:, 6 + f % 2, :], w["fc1"][:, k, f * P:(f + 1) * P],
                                                ht[:, k, n * BANK:(n + 1) * BANK],
                                                start=(k == 0), stop=(k == KC - 1))
                    last.then_inc(e["f1_full"], 1)
                elif kind == "f2":
                    j, = a
                    n, t = divmod(j, 4)
                    if t < 2:
                        pe.wait_ge(e["y_ready"], F2T * (n + 1))
                    else:
                        pe.wait_ge(e["r_ready"], j - 1)
                    for f in range(F2T):
                        last = nc.tensor.matmul(ps[:, 6 + j % 2, 0:C], yb[:, f, t * P:(t + 1) * P],
                                                w["fc2"][:, f, :], start=(f == 0), stop=(f == F2T - 1))
                    last.then_inc(e["f2_full"], 1)

        @block.scalar
        def _(act):
            for step in order:
                kind, a = step[0], step[1:]
                if kind == "xt":
                    n, k = a
                    act.wait_ge(e["xnt_full"], KC * n + k + 1)
                    nc.scalar.copy(xnt[:, k, n * BANK:(n + 1) * BANK], ps[:, 2 * n + k, :]).then_inc(e["xnt_ready"], 1)
                elif kind == "kt":
                    cc, n = a
                    u = cc * NHALF + n
                    act.wait_ge(e["kt_full"], u + 1)
                    nc.scalar.activation(kt[:, cc, n * BANK:(n + 1) * BANK], ps[:, u % 2, :], ACT.Identity,
                                         bias=w["ps_bk"][:, cc:cc + 1]).then_inc(e["kt_ready"], 1)
                elif kind == "s":
                    mt, = a
                    act.wait_ge(e["nb_ready"], mt + 1)
                    if mt >= 3:
                        act.wait_ge(e["pt_full"], 2 * (mt - 2))
                    b0 = 2 * (mt % 2)
                    nc.scalar.activation(pr[:, mt % 3, :].rearrange("p (n t) -> p n t", n=NHALF),
                                         ps[0:MR, b0:b0 + 2, :], ACT.Exp, bias=nb[:, mt:mt + 1], scale=SCALE,
                                         accum_out=sums[:, mt:mt + 1]).then_inc(e["exp_ready"], 1)
                elif kind == "pt":
                    mt, = a
                    act.wait_ge(e["pt_full"], 2 * mt + 1)
                    nc.scalar.copy(pt[:, 0:4, mt * MR:(mt + 1) * MR],
                                   ps[:, 4, 0:4 * MR].rearrange("p (j r) -> p j r", r=MR)).then_inc(e["pt_ready_a"], 1)
                elif kind == "g":
                    mt, = a
                    act.wait_ge(e["g_full"], mt + 1)
                    nc.scalar.copy(gg[:, mt, :], ps[0:MR, 4 + mt % 2, 0:C]).then_inc(e["g_ready"], 1)
                elif kind == "ht":
                    n, k = a
                    act.wait_ge(e["ht_full"], KC * n + k + 1)
                    nc.scalar.activation(ht[:, k, n * BANK:(n + 1) * BANK], ps[:, 6 + k % 2, :], ACT.Identity,
                                         scale=w["gamma"][:, k:k + 1],
                                         bias=w["beta"][:, k:k + 1]).then_inc(e["ht_ready"], 1)
                elif kind == "f1":
                    n, f = a
                    act.wait_ge(e["f1_full"], n * F2T + f + 1)
                    if n:
                        act.wait_ge(e["f2_full"], 4 * n)
                    nc.scalar.activation(yb[:, f, :], ps[:, 6 + f % 2, :], ACT.Silu,
                                         bias=w["fc1_b"][:, f:f + 1]).then_inc(e["y_ready"], 1)


def build_program(nc, io):
    with Memory(nc) as m:
        ps = m.stack.enter_context(nc.psum_tensor("ps", [P, 8, BANK], F32))
        w = {name: m.sb("w_" + name, shape, dt) for name, (shape, dt) in TABLES.items()}
        with Memory(nc) as first:
            w |= {name: first.sb("w_" + name, shape, dt) for name, (shape, dt) in ATTENTION_WEIGHTS.items()}
            attention_loop(nc, io, w, ps)
        w |= {name: m.sb("w_" + name, shape, dt) for name, (shape, dt) in OTHER_WEIGHTS.items()}
        with Memory(nc) as second:
            w |= {name: second.sb("w_" + name, shape, dt) for name, (shape, dt) in MOD_WEIGHTS.items()}
            setup_rest_and_top_tokens(nc, io, w, ps)
            mod_loop(nc, io, w, ps)
            top_queries(nc, io, w, ps)
        prob_loop(nc, io, w, ps)


_INS = ['L0_attn_x', 'L0_attn_W_attn', 'L0_attn_b_attn', 'L0_attn_W_proj', 'L0_attn_b_proj', 'L0_ffn_w_router',
        'L0_ffn_W_qkv', 'L0_ffn_W_out', 'L0_ffn_g1', 'L0_ffn_g2', 'L0_ffn_W1', 'L0_ffn_W2', 'L0_ffn_W3',
        'L1_attn_Wq', 'L1_attn_bq', 'L1_attn_Wk', 'L1_attn_bk', 'L1_attn_Wv', 'L1_attn_bv', 'L1_attn_Wo', 'L1_attn_bo',
        'L1_attn_sample_idx', 'L1_ffn_ln_gamma', 'L1_ffn_ln_beta', 'L1_ffn_fc1_q', 'L1_ffn_fc1_scales',
        'L1_ffn_fc1_bias', 'L1_ffn_fc2_q', 'L1_ffn_fc2_scales', 'L1_ffn_fc2_bias']
_SCRATCH = {"parts": ((2 * KC, PARTS, P, T), BF16), "nm_parts": ((PARTS, HS * NT, P), BF16),
            "x1": ((B, T, C), F32), "xn1": ((B, T, C), F32),
            "scores": ((B * NT, P), F32), "top_tokens": ((B, CAP), F32),
            "x2": ((B, T, C), F32), "xn2": ((B, T, C), F32), "q": ((B, T, C), F32), "top_queries": ((B, HU), F32)}


def kernel(**inputs):
    import concourse.bacc as _bacc
    from concourse.bass_utils import run_bass_kernel_spmd as _run

    nc = _bacc.Bacc("TRN2", target_bir_lowering=False, num_devices=1)
    arrays = {name: np.ascontiguousarray(inputs[name]) for name in _INS}
    theta = (1.0 / 10000.0 ** (np.arange(0, D, 2, dtype=np.float32) / D)).astype(np.float32)
    angle = (np.arange(H, dtype=np.float32)[:, None] * theta[None, :]).astype(np.float32)
    arrays["rope_cos"] = np.cos(angle).astype(np.float32).reshape(-1)
    arrays["rope_sin"] = np.sin(angle).astype(np.float32).reshape(-1)
    io = {name: nc.dram_tensor("in_" + name, a.shape, mybir.dt.from_np(a.dtype), kind="ExternalInput").ap()
          for name, a in arrays.items()}
    io["x"] = io["L0_attn_x"]
    for name, (shape, dt) in _SCRATCH.items():
        io[name] = nc.dram_tensor("scratch_" + name, shape, dt, kind="Internal").ap()
    io["out"] = nc.dram_tensor("out_0_dram", (B, T, C), F32, kind="ExternalOutput").ap()
    build_program(nc, io)
    r = _run(nc, [{"in_" + k: v for k, v in arrays.items()}], core_ids=[0])
    return r.results[0]["out_0_dram"]
```
